# Optimizing a Trainium2 kernel written in Bass

```python
import numpy as np
import jax
import jax.numpy as jnp

def _softmax(x, axis=-1):
    return jax.nn.softmax(x, axis=axis)

def _gelu(x):
    return jax.nn.gelu(x, approximate=True)

def _silu(x):
    return jax.nn.silu(x)

def _sigmoid(x):
    return jax.nn.sigmoid(x)

def _layernorm(x, axis=-1, eps=1e-05):
    m = jnp.mean(x, axis=axis, keepdims=True)
    v = jnp.var(x, axis=axis, keepdims=True)
    return (x - m) / jnp.sqrt(v + eps)

def _scatter_add(tgt, idx, src, axis=0):
    return tgt.at[idx].add(src)

def _segment_sum(src, seg, n):
    return jax.ops.segment_sum(src, seg, n)
kernel_name = 'mk_adj_resnorm_d4_adj_r2_8acd29'

def setup_inputs(seed: int=0):
    np.random.seed(seed)
    _w = jnp.asarray

    def _rec_inputs():
        import jax
        import jax.numpy as jnp
        _gk = jax.random.key(seed)
        x = -0.0002928 + 1 * jax.random.normal(jax.random.fold_in(_gk, 1), (128, 128, 128), jnp.float32)
        _a = jax.random.bernoulli(jax.random.fold_in(_gk, 2), 0.0625, (128, 128))
        _a = jnp.logical_or(_a, jnp.swapaxes(_a, -1, -2))
        _a = jnp.logical_or(_a, jnp.eye(128, dtype=bool))
        _af = _a.astype(jnp.float32)
        _af = _af * jax.random.uniform(jax.random.fold_in(_gk, 3), (128, 128), jnp.float32, 0.05, 5.41998)
        adj = _af
        return (x, adj)
    x, adj = _rec_inputs()

    def _L0_gnn_setup():
        import jax, jax.numpy as jnp
        import numpy as np
        NEG = -1e+30
        key = jax.random.key(seed)
        ks = jax.random.split(key, 4)
        B, T, C = (4, 2048, 128)
        x = jax.random.normal(ks[0], (B, T, C), dtype=jnp.float32)
        adj_mask = jax.random.normal(ks[1], (T, T), dtype=jnp.float32)
        Wqkv = jax.random.normal(ks[2], (C, 3 * C), dtype=jnp.float32) * (1.0 / np.sqrt(C))
        Wo = jax.random.normal(ks[3], (C, C), dtype=jnp.float32) * (1.0 / np.sqrt(C))
        return {'x': x, 'adj_mask': adj_mask, 'Wqkv': Wqkv, 'Wo': Wo}
    _L0_gnn_all = _L0_gnn_setup()
    _L0_gnn_in = {k: v for k, v in _L0_gnn_all.items() if k in ('Wqkv', 'Wo')}
    del _L0_gnn_all

    def _L1_gnn_setup():
        import jax, jax.numpy as jnp
        import numpy as np
        ALPHA = 0.2
        key = jax.random.key(seed)
        k1, k2, k3, k4 = jax.random.split(key, 4)
        B, N, Fin, Fout = (8, 1024, 128, 128)
        h = jax.random.normal(k1, (B, N, Fin), dtype=jnp.float32)
        adj = jax.random.randint(k2, (N, N), 0, 2).astype(jnp.float32)
        adj = jnp.maximum(adj, jnp.eye(N, dtype=jnp.float32))

        def xavier(k, shape, gain=1.414):
            fan_in, fan_out = (shape[0], shape[1])
            a = gain * np.sqrt(6.0 / (fan_in + fan_out))
            return jax.random.uniform(k, shape, dtype=jnp.float32, minval=-a, maxval=a)
        W = xavier(k3, (Fin, Fout))
        a = xavier(k4, (2 * Fout, 1))
        return {'h': h, 'adj_matrix': adj, 'W': W, 'a': a}
    _L1_gnn_all = _L1_gnn_setup()
    _L1_gnn_in = {k: v for k, v in _L1_gnn_all.items() if k in ('W', 'a')}
    del _L1_gnn_all

    def _L2_gnn_setup():
        import jax, jax.numpy as jnp
        import numpy as np
        B, T, D, H = (64, 1024, 128, 128)
        MAX_SKIP = 4

        def _lstm_last(Wih, Whh, bih, bhh, xs):
            N, _, Hd = xs.shape
            bias = bih + bhh

            def step(carry, x_t):
                h, c = carry
                g = x_t @ Wih.T + h @ Whh.T + bias
                i, f, gg, o = jnp.split(g, 4, axis=-1)
                c = jax.nn.sigmoid(f) * c + jax.nn.sigmoid(i) * jnp.tanh(gg)
                h = jax.nn.sigmoid(o) * jnp.tanh(c)
                return ((h, c), None)
            init = (jnp.zeros((N, Hd), xs.dtype), jnp.zeros((N, Hd), xs.dtype))
            (h_last, _), _ = jax.lax.scan(step, init, jnp.swapaxes(xs, 0, 1))
            return h_last
        key = jax.random.key(seed)
        ks = jax.random.split(key, 8)
        s = 0.05
        x = jax.random.normal(ks[0], (B, T, D), jnp.float32)
        adj = jax.random.uniform(ks[1], (T, T), jnp.float32) / T
        Wg0 = jax.random.normal(ks[2], (D, H), jnp.float32) * s
        bg0 = jnp.zeros((H,), jnp.float32)
        Wg1 = jax.random.normal(ks[3], (H, H), jnp.float32) * s
        bg1 = jnp.zeros((H,), jnp.float32)
        Wih = jax.random.normal(ks[4], (MAX_SKIP, 4 * H, H), jnp.float32) * s
        Whh = jax.random.normal(ks[5], (MAX_SKIP, 4 * H, H), jnp.float32) * s
        bih = jax.random.normal(ks[6], (MAX_SKIP, 4 * H), jnp.float32) * s
        bhh = jax.random.normal(ks[7], (MAX_SKIP, 4 * H), jnp.float32) * s
        return dict(x=x, adj=adj, Wg0=Wg0, bg0=bg0, Wg1=Wg1, bg1=bg1, Wih=Wih, Whh=Whh, bih=bih, bhh=bhh)
    _L2_gnn_all = _L2_gnn_setup()
    _L2_gnn_in = {k: v for k, v in _L2_gnn_all.items() if k in ('Wg0', 'bg0', 'Wg1', 'bg1', 'Wih', 'Whh', 'bih', 'bhh')}
    del _L2_gnn_all

    def _L3_gnn_setup():
        import jax, jax.numpy as jnp
        import numpy as np
        EPS_LN = 1e-05

        def _layernorm(x, g, b):
            mu = x.mean(-1, keepdims=True)
            var = ((x - mu) ** 2).mean(-1, keepdims=True)
            return (x - mu) / jnp.sqrt(var + EPS_LN) * g + b
        key = jax.random.key(seed)
        B, N, D, H = (4, 1024, 128, 4)
        hid = int(D * 2.0)
        ks = jax.random.split(key, 12)
        x = jax.random.normal(ks[0], (B, N, D), jnp.float32)
        Au = jax.random.uniform(ks[1], (N, N)) < 0.004
        A = jnp.logical_or(Au, Au.T)
        A = A.at[jnp.arange(N), jnp.arange(N)].set(False)
        Af = A.astype(jnp.float32)
        deg = Af.sum(axis=1)
        L = jnp.diag(deg) - Af
        adjacency = Af + jnp.eye(N, dtype=jnp.float32)
        s = lambda k, sh, f: jax.random.normal(k, sh, jnp.float32) * f
        sc = 1.0 / np.sqrt(D)
        Wc = s(ks[2], (D, D), sc)
        bc = jnp.zeros((D,), jnp.float32)
        Wq = s(ks[3], (D, D), sc)
        Wk = s(ks[4], (D, D), sc)
        Wv = s(ks[5], (D, D), sc)
        Wo = s(ks[6], (D, D), sc)
        bo = jnp.zeros((D,), jnp.float32)
        W1 = s(ks[7], (D, hid), sc)
        b1 = jnp.zeros((hid,), jnp.float32)
        W2 = s(ks[8], (hid, D), 1.0 / np.sqrt(hid))
        b2 = jnp.zeros((D,), jnp.float32)
        g1 = jnp.ones((D,), jnp.float32)
        be1 = jnp.zeros((D,), jnp.float32)
        g2 = jnp.ones((D,), jnp.float32)
        be2 = jnp.zeros((D,), jnp.float32)
        g3 = jnp.ones((D,), jnp.float32)
        be3 = jnp.zeros((D,), jnp.float32)
        return dict(x=x, L=L, adjacency=adjacency, Wc=Wc, bc=bc, g1=g1, be1=be1, Wq=Wq, Wk=Wk, Wv=Wv, Wo=Wo, bo=bo, g2=g2, be2=be2, W1=W1, b1=b1, W2=W2, b2=b2, g3=g3, be3=be3)
    _L3_gnn_all = _L3_gnn_setup()
    _L3_gnn_in = {k: v for k, v in _L3_gnn_all.items() if k in ('Wc', 'bc', 'g1', 'be1', 'Wq', 'Wk', 'Wv', 'Wo', 'bo', 'g2', 'be2', 'W1', 'b1', 'W2', 'b2', 'g3', 'be3')}
    del _L3_gnn_all
    return {'x': x, 'adj': adj, 'L0_gnn_Wqkv': _L0_gnn_in['Wqkv'], 'L0_gnn_Wo': _L0_gnn_in['Wo'], 'L1_gnn_W': _L1_gnn_in['W'], 'L1_gnn_a': _L1_gnn_in['a'], 'L2_gnn_Wg0': _L2_gnn_in['Wg0'], 'L2_gnn_bg0': _L2_gnn_in['bg0'], 'L2_gnn_Wg1': _L2_gnn_in['Wg1'], 'L2_gnn_bg1': _L2_gnn_in['bg1'], 'L2_gnn_Wih': _L2_gnn_in['Wih'], 'L2_gnn_Whh': _L2_gnn_in['Whh'], 'L2_gnn_bih': _L2_gnn_in['bih'], 'L2_gnn_bhh': _L2_gnn_in['bhh'], 'L3_gnn_Wc': _L3_gnn_in['Wc'], 'L3_gnn_bc': _L3_gnn_in['bc'], 'L3_gnn_g1': _L3_gnn_in['g1'], 'L3_gnn_be1': _L3_gnn_in['be1'], 'L3_gnn_Wq': _L3_gnn_in['Wq'], 'L3_gnn_Wk': _L3_gnn_in['Wk'], 'L3_gnn_Wv': _L3_gnn_in['Wv'], 'L3_gnn_Wo': _L3_gnn_in['Wo'], 'L3_gnn_bo': _L3_gnn_in['bo'], 'L3_gnn_g2': _L3_gnn_in['g2'], 'L3_gnn_be2': _L3_gnn_in['be2'], 'L3_gnn_W1': _L3_gnn_in['W1'], 'L3_gnn_b1': _L3_gnn_in['b1'], 'L3_gnn_W2': _L3_gnn_in['W2'], 'L3_gnn_b2': _L3_gnn_in['b2'], 'L3_gnn_g3': _L3_gnn_in['g3'], 'L3_gnn_be3': _L3_gnn_in['be3']}

def reference(x, adj, L0_gnn_Wqkv, L0_gnn_Wo, L1_gnn_W, L1_gnn_a, L2_gnn_Wg0, L2_gnn_bg0, L2_gnn_Wg1, L2_gnn_bg1, L2_gnn_Wih, L2_gnn_Whh, L2_gnn_bih, L2_gnn_bhh, L3_gnn_Wc, L3_gnn_bc, L3_gnn_g1, L3_gnn_be1, L3_gnn_Wq, L3_gnn_Wk, L3_gnn_Wv, L3_gnn_Wo, L3_gnn_bo, L3_gnn_g2, L3_gnn_be2, L3_gnn_W1, L3_gnn_b1, L3_gnn_W2, L3_gnn_b2, L3_gnn_g3, L3_gnn_be3):
    import jax
    import jax.numpy as jnp

    def _L0_gnn_ref(x, adj_mask, Wqkv, Wo):
        import jax, jax.numpy as jnp
        import numpy as np
        NEG = -1e+30
        B, T, C = x.shape
        qkv = x @ Wqkv
        q, k, v = jnp.split(qkv, 3, axis=-1)
        scale = 1.0 / jnp.sqrt(jnp.asarray(C, dtype=x.dtype))
        scores = jnp.einsum('btd,bsd->bts', q, k) * scale + adj_mask
        causal = jnp.tril(jnp.ones((T, T), dtype=bool))
        scores = jnp.where(causal, scores, NEG)
        attn = jax.nn.softmax(scores, axis=-1)
        y = jnp.einsum('bts,bsd->btd', attn, v)
        return y @ Wo

    def _L1_gnn_ref(h, adj_matrix, W, a):
        import jax, jax.numpy as jnp
        import numpy as np
        ALPHA = 0.2
        Fout = W.shape[1]
        Wh = jnp.einsum('bnf,fo->bno', h, W)
        a1, a2 = (a[:Fout, 0], a[Fout:, 0])
        s1 = Wh @ a1
        s2 = Wh @ a2
        e = s1[:, :, None] + s2[:, None, :]
        e = jnp.where(e >= 0, e, ALPHA * e)
        e = jnp.where(adj_matrix[None] == 0, -jnp.inf, e)
        attention = jax.nn.softmax(e, axis=-1)
        h_prime = jnp.einsum('bij,bjo->bio', attention, Wh)
        return h_prime

    def _L2_gnn_ref(x, adj, Wg0, bg0, Wg1, bg1, Wih, Whh, bih, bhh):
        import jax, jax.numpy as jnp
        import numpy as np
        B, T, D, H = (64, 1024, 128, 128)
        MAX_SKIP = 4

        def _lstm_last(Wih, Whh, bih, bhh, xs):
            N, _, Hd = xs.shape
            bias = bih + bhh

            def step(carry, x_t):
                h, c = carry
                g = x_t @ Wih.T + h @ Whh.T + bias
                i, f, gg, o = jnp.split(g, 4, axis=-1)
                c = jax.nn.sigmoid(f) * c + jax.nn.sigmoid(i) * jnp.tanh(gg)
                h = jax.nn.sigmoid(o) * jnp.tanh(c)
                return ((h, c), None)
            init = (jnp.zeros((N, Hd), xs.dtype), jnp.zeros((N, Hd), xs.dtype))
            (h_last, _), _ = jax.lax.scan(step, init, jnp.swapaxes(xs, 0, 1))
            return h_last
        h = jax.nn.relu(jnp.einsum('ts,bsh->bth', adj, x @ Wg0 + bg0))
        h = jax.nn.relu(jnp.einsum('ts,bsh->bth', adj, h @ Wg1 + bg1))
        Bv, Tv, Hd = h.shape
        for p in range(1, MAX_SKIP + 1):
            nw = Tv // p
            wins = h[:, :nw * p, :].reshape(Bv * nw, p, Hd)
            last = _lstm_last(Wih[p - 1], Whh[p - 1], bih[p - 1], bhh[p - 1], wins)
            idx = jnp.arange(nw) * p + (p - 1)
            h = h.at[:, idx, :].set(last.reshape(Bv, nw, Hd))
        return h

    def _L3_gnn_ref(x, L, adjacency, Wc, bc, g1, be1, Wq, Wk, Wv, Wo, bo, g2, be2, W1, b1, W2, b2, g3, be3):
        import jax, jax.numpy as jnp
        import numpy as np
        EPS_LN = 1e-05

        def _layernorm(x, g, b):
            mu = x.mean(-1, keepdims=True)
            var = ((x - mu) ** 2).mean(-1, keepdims=True)
            return (x - mu) / jnp.sqrt(var + EPS_LN) * g + b
        B, N, D = x.shape
        H = 4
        hd = D // H
        eig = jnp.linalg.eigvalsh(L)
        lam_max = eig[-1] + 1e-08
        L_norm = 2.0 * L / lam_max - jnp.eye(N, dtype=L.dtype)
        xp = jnp.einsum('mn,bnf->bmf', L_norm, x)
        h = xp @ Wc + bc
        h = _layernorm(h, g1, be1)
        h = jax.nn.relu(h)
        x1 = h + x
        q = (x1 @ Wq).reshape(B, N, H, hd).transpose(0, 2, 1, 3)
        k = (x1 @ Wk).reshape(B, N, H, hd).transpose(0, 2, 1, 3)
        v = (x1 @ Wv).reshape(B, N, H, hd).transpose(0, 2, 1, 3)
        scores = jnp.einsum('bhnd,bhmd->bhnm', q, k) / np.sqrt(hd).astype(np.float32)
        scores = jnp.where(adjacency[None, None] > 0, scores, jnp.float32(-1000000000.0))
        attn = jax.nn.softmax(scores, axis=-1)
        o = jnp.einsum('bhnm,bhmd->bhnd', attn, v)
        o = o.transpose(0, 2, 1, 3).reshape(B, N, D)
        o = o @ Wo + bo
        x2 = _layernorm(x1 + o, g2, be2)
        m = jax.nn.gelu(x2 @ W1 + b1, approximate=False) @ W2 + b2
        return _layernorm(x2 + m, g3, be3)
    x = _layernorm(x + _L0_gnn_ref(x, adj, L0_gnn_Wqkv, L0_gnn_Wo), axis=-1)
    x = _layernorm(x + _L1_gnn_ref(x, adj, L1_gnn_W, L1_gnn_a), axis=-1)
    x = _layernorm(x + _L2_gnn_ref(x, adj, L2_gnn_Wg0, L2_gnn_bg0, L2_gnn_Wg1, L2_gnn_bg1, L2_gnn_Wih, L2_gnn_Whh, L2_gnn_bih, L2_gnn_bhh), axis=-1)
    x = _layernorm(x + _L3_gnn_ref(x, adj, adj, L3_gnn_Wc, L3_gnn_bc, L3_gnn_g1, L3_gnn_be1, L3_gnn_Wq, L3_gnn_Wk, L3_gnn_Wv, L3_gnn_Wo, L3_gnn_bo, L3_gnn_g2, L3_gnn_be2, L3_gnn_W1, L3_gnn_b1, L3_gnn_W2, L3_gnn_b2, L3_gnn_g3, L3_gnn_be3), axis=-1)
    return x

_drawn_inputs = setup_inputs


def setup_inputs(seed=0):
    import zlib

    import numpy as np

    out = dict(_drawn_inputs(seed))
    spreads = {'L2_gnn_bg0': (0.0, 0.1),
     'L2_gnn_bg1': (0.0, 0.1),
     'L3_gnn_bc': (0.0, 0.1),
     'L3_gnn_g1': (1.0, 0.2),
     'L3_gnn_be1': (0.0, 0.1),
     'L3_gnn_bo': (0.0, 0.1),
     'L3_gnn_g2': (1.0, 0.2),
     'L3_gnn_be2': (0.0, 0.1),
     'L3_gnn_b1': (0.0, 0.1),
     'L3_gnn_b2': (0.0, 0.1),
     'L3_gnn_g3': (1.0, 0.2),
     'L3_gnn_be3': (0.0, 0.1)}
    factors = {'L2_gnn_Whh': 7.014, 'L2_gnn_bih': 2.96, 'L2_gnn_bhh': 3.048}
    for name, (base, spread) in spreads.items():
        noise = np.random.default_rng([zlib.crc32(name.encode()), seed]).standard_normal(out[name].shape)
        drawn = base * np.exp(spread * noise) if base else spread * noise
        out[name] = jnp.asarray(drawn.astype(out[name].dtype))
    for name, factor in factors.items():
        out[name] = (out[name] * factor).astype(out[name].dtype)
    return out
```

```python
from contextlib import ExitStack, contextmanager

import concourse.bass as bass
from concourse import mybir

F32 = mybir.dt.float32
BF16 = mybir.dt.bfloat16
ALU = mybir.AluOpType
ACT = mybir.ActivationFunctionType
AX = mybir.AxisListType.X

P = 128
GROUP = 4
EPS = 1e-5
NEG = -1e30
NEG3 = -1e9
ALPHA = 0.2
HEADS = 4
HD = P // HEADS
WIDE = 128
SKIPS = 4
GATES = 4
POWER_ROUNDS = 8


def after(eng, sem, n):
    if isinstance(n, int) and n <= 0:
        return
    eng.wait_ge(sem, n)


def after_nop(eng, sem, n):
    if isinstance(n, int) and n <= 0:
        return
    eng.wait_ge(sem, n)
    eng.nop(nofuse=True)


def run_steps(eng, step, n, lag, head, tail=None):
    assert head % 2 == 0 and n % 2 == 0 and head >= lag
    for i in range(head):
        step(i, i % 2)
    tail = n if tail is None else tail
    with eng.Fori(head // 2, tail // 2) as pair:
        step(pair * 2, 0)
        step(pair * 2 + 1, 1)
    for i in range(tail, n + lag):
        step(i, i % 2)


def live(g, n):
    return not isinstance(g, int) or 0 <= g < n


def batches(buf, g, count=GROUP):
    return buf[:, bass.ds(g * count, count), :]


def over(ap, count=GROUP):
    return ap.unsqueeze(1).broadcast_to([ap.shape[0], count, ap.shape[-1]])


def landed(g, b):
    return (g - b) * 8 + 16


@contextmanager
def phase_semaphores(nc, prefix):
    held = []

    def sem(name):
        held.append(nc.alloc_semaphore(name=f"{prefix}_{name}"))
        return held[-1]
    yield sem
    nc.clear_and_free_semaphores(held)
    nc.all_engine_barrier()


def flat(ap):
    return ap.rearrange("p k c -> p (k c)")


def program(nc, a, out):
    x = a["x"]
    B = x.shape[0]
    NG = B // GROUP
    ctx = ExitStack()

    def sb(name, shape, dt=F32):
        return ctx.enter_context(nc.sbuf_tensor(name, shape, dt))

    with ctx:
        X = sb("X", [P, B, P])
        H = sb("H", [P, B, P])
        c = dict(
            ident=sb("ident", [P, P]), identb=sb("identb", [P, P], BF16), adjT=sb("adjT", [P, P]),
            causal=sb("causal", [P, P]), gat_mask=sb("gat_mask", [P, P], BF16),
            head_mask=sb("head_mask", [P, P], BF16), lapT=sb("lapT", [P, P]), ones3=sb("ones3", [3, P], BF16),
            half=sb("half", [P, GROUP]), Gqk=sb("Gqk", [P, P]), Gvo=sb("Gvo", [P, P]), W1g=sb("W1g", [P, P]),
            a1rep=sb("a1rep", [P, P]), a2rep=sb("a2rep", [P, P]), rowsum=sb("rowsum", [1, P]),
            bg=sb("bg", [1, 2, P]), Wg=sb("Wg", [P, 2, P]),
            cols=sb("cols", [P, 20]), bias3=sb("bias3", [3, 3, P], BF16), Wx=sb("Wx", [P, 5, P]),
            W1=sb("W1", [P, 2 * P]), W2=sb("W2", [P, 2, P]), rep=sb("rep", [P, 6, P]),
        )
        lstm_weights = ExitStack()
        c["WT"] = lstm_weights.enter_context(nc.sbuf_tensor("WT", [P, 2, SKIPS, GATES, P], F32))
        psum = [ctx.enter_context(nc.psum_tensor(f"bank{i}", [P, GROUP, P], F32)) for i in range(8)]
        setup(nc, a, c, X, H, psum)
        attention_layer(nc, c, X, psum, NG, x)
        attention_layer(nc, c, X, psum, NG, None)
        gcn_layer(nc, c, X, H, psum, NG)
        for p in range(1, SKIPS + 1):
            lstm_pass(nc, c, H, psum, B, p)
        lstm_weights.close()
        transformer_attention(nc, c, X, H, psum, NG)
        transformer_mlp(nc, c, X, H, psum, NG, out)


def setup(nc, a, c, X, H, psum):
    ctx = ExitStack()
    with ctx:
        def sb(name, shape, dt=F32):
            return ctx.enter_context(nc.sbuf_tensor(name, shape, dt))

        sem = ctx.enter_context(phase_semaphores(nc, "setup"))
        ident, adjT, ones = c["ident"], c["adjT"], sb("ones", [P, P])
        raw_ih, raw_hh = H[:, 0:16, :], H[:, 16:32, :]
        adj, Wqkv, Wo, W1g = H[:, 32, :], H[:, 33:36, :], H[:, 36, :], c["W1g"]
        wT = H[:, 40:44, :]
        avec = H[:, 44:46, :]
        rows_a, rows_b = sb("rows_a", [20, P]), sb("rows_b", [20, P])
        brow, bres, bpart = sb("brow", [1, 3, P]), sb("bres", [1, 3, P]), sb("bpart", [1, 3, 3, P], BF16)
        sym, power, scratch = sb("sym", [P, P]), sb("power", [P, P]), sb("scratch", [P, P])
        sums, stat, norm = sb("sums", [P, 2]), sb("stat", [P, 4]), sb("norm", [P, 1])
        powhalf = sb("powhalf", [P, 1])

        small_loaded, lstm_loaded, bias_moved = sem("small_loaded"), sem("lstm_loaded"), sem("bias_moved")
        rows_zeroed, zeroed, ident_ready = sem("rows_zeroed"), sem("zeroed"), sem("ident_ready")
        rows_loaded = sem("rows_loaded")
        masks_filled, copied, products = sem("masks_filled"), sem("copied"), sem("products")
        v = sem("setup_v")
        root_ready, split_ready, eig_pe, eig_v = sem("root_ready"), sem("split_ready"), sem("eig_pe"), sem("eig_v")

        SMALL = [
            (adj, a["adj"]), (Wqkv, a["L0_gnn_Wqkv"].rearrange("d (j e) -> d j e", j=3)), (Wo, a["L0_gnn_Wo"]),
            (W1g[:, :], a["L1_gnn_W"]),
            (c["bg"][0:1, 0, :], a["L2_gnn_bg0"].rearrange("(a n) -> a n", a=1)),
            (c["bg"][0:1, 1, :], a["L2_gnn_bg1"].rearrange("(a n) -> a n", a=1)),
            (c["Wg"][:, 0, :], a["L2_gnn_Wg0"]), (c["Wg"][:, 1, :], a["L2_gnn_Wg1"]),
            (c["W1"][:, :], a["L3_gnn_W1"]), (c["W2"][:, :, :], a["L3_gnn_W2"].rearrange("(j d) n -> d j n", j=2)),
        ]
        SMALL += [(c["Wx"][:, j, :], a["L3_gnn_" + w]) for j, w in enumerate(("Wc", "Wq", "Wk", "Wv", "Wo"))]
        SMALL += [(c["rep"][:, j, :], a["L3_gnn_" + w].rearrange("(a n) -> a n", a=1).broadcast_to([P, P]))
                  for j, w in enumerate(("g1", "be1", "g2", "be2", "g3", "be3"))]
        SMALL += [(brow[0:1, j, :], a["L3_gnn_" + w].rearrange("(a n) -> a n", a=1))
                  for j, w in enumerate(("bc", "bo", "b2"))]
        ROWS = [
            (rows_a[0:16, :], a["L2_gnn_bih"].rearrange("q (g d) -> (q g) d", d=P)),
            (rows_a[16:18, :], a["L3_gnn_b1"].rearrange("(j d) -> j d", j=2)),
            (rows_a[18:20, :], a["L1_gnn_a"].rearrange("(j d) o -> j (d o)", j=2)),
            (rows_b[0:16, :], a["L2_gnn_bhh"].rearrange("q (g d) -> (q g) d", d=P)),
        ]

        with nc.Block() as block:
            @block.sync
            def _(sync):
                for dst, src in SMALL:
                    sync.dma_start(dst, src).then_inc(small_loaded, 16)
                sync.wait_ge(rows_zeroed, 1)
                for dst, src in ROWS:
                    sync.dma_start(dst, src).then_inc(rows_loaded, 16)
                for raw, name in ((raw_ih, "L2_gnn_Wih"), (raw_hh, "L2_gnn_Whh")):
                    sync.dma_start(raw, a[name].rearrange("q (g o) i -> o (q g) i", g=GATES)).then_inc(lstm_loaded, 16)
                sync.wait_ge(split_ready, 1)
                for part in range(3):
                    sync.dma_start(c["bias3"][part:part + 1, :, :], bpart[0:1, part, :, :]).then_inc(bias_moved, 16)
                sync.wait_ge(bias_moved, 48)

            @block.gpsimd
            def _(pool):
                nc.gpsimd.memset(ident[:, :], 0.0).then_inc(zeroed, 1)
                nc.gpsimd.memset(powhalf[:, :], 0.5)
                nc.gpsimd.memset(c["half"][:, :], -0.5)
                nc.gpsimd.memset(ones[:, :], 1.0)
                nc.gpsimd.memset(c["ones3"][:, :], 1.0)
                pool.wait_ge(zeroed, 1)
                nc.gpsimd.affine_select(out=ident[:, :], in_=ident[:, :], compare_op=ALU.not_equal, fill=1.0,
                                        base=0, pattern=[[-1, P]], channel_multiplier=1).then_inc(ident_ready, 1)
                pool.wait_ge(small_loaded, 16 * len(SMALL))
                nc.gpsimd.affine_select(out=c["causal"][:, :], in_=adj, compare_op=ALU.is_ge, fill=NEG,
                                        base=0, pattern=[[-1, P]], channel_multiplier=1).then_inc(masks_filled, 1)
                pool.wait_ge(eig_v, 2)
                nc.gpsimd.tensor_tensor(norm[:, :], stat[:, 0:1], powhalf[:, :], ALU.pow).then_inc(root_ready, 1)

            TRANSPOSES = [(adj, adjT[:, :]), (Wqkv[:, 0, :], wT[:, 0, :]), (Wqkv[:, 1, :], wT[:, 1, :]),
                          (Wqkv[:, 2, :], wT[:, 2, :]), (W1g[:, :], wT[:, 3, :])]

            @block.tensor
            def _(pe):
                pe.wait_ge(ident_ready, 1)
                pe.wait_ge(small_loaded, 16 * len(SMALL))
                for n, (src, _) in enumerate(TRANSPOSES):
                    t = nc.tensor.transpose(psum[n // 4][:, n % 4, :], src, ident[:, :])
                t.then_inc(products, 1)
                pe.wait_ge(v, 1)
                nc.tensor.transpose(psum[2][:, 0, 0:20], rows_a[:, :], ident[0:20, 0:20]).then_inc(products, 1)
                pe.wait_ge(lstm_loaded, 32)
                for n in range(2 * SKIPS):
                    kind, q = n // SKIPS, n % SKIPS
                    raw = (raw_ih, raw_hh)[kind]
                    if n >= 2:
                        pe.wait_ge(copied, n - 1)
                    for g in range(GATES):
                        t = nc.tensor.transpose(psum[3 + n % 2][:, g, :], raw[:, q * GATES + g, :], ident[:, :])
                    t.then_inc(products, 1)
                pe.wait_ge(v, 4)
                nc.tensor.matmul(psum[5][:, 0, :], wT[:, 0, :], wT[:, 1, :], start=True, stop=True)
                nc.tensor.matmul(psum[5][:, 1, :], wT[:, 2, :], Wo, start=True, stop=True)
                for j in range(2):
                    nc.tensor.matmul(psum[5][:, 2 + j, :], wT[:, 3, :], avec[:, j, :], start=True, stop=True)
                nc.tensor.matmul(psum[6][0:1, 0, :], ones[:, 0:1], adjT[:, :], start=True, stop=True) \
                    .then_inc(products, 1)
                pe.wait_ge(eig_v, 1)
                nc.tensor.matmul(psum[7][:, 0, 0:1], ones[:, :], sums[:, 0:1], start=True, stop=True).then_inc(eig_pe, 1)
                with pe.Fori(0, POWER_ROUNDS) as r:
                    pe.wait_ge(eig_v, r * 6 + 4)
                    nc.tensor.matmul(psum[7][:, 0, 0:1], ones[:, :], sums[:, 0:1], start=True, stop=True) \
                        .then_inc(eig_pe, 1)
                    for s in range(3):
                        pe.wait_ge(eig_v, r * 6 + 6 + s)
                        nc.tensor.matmul(psum[7][:, 1, :], power[:, :], power[:, :], start=True, stop=True) \
                            .then_inc(eig_pe, 1)
                e = POWER_ROUNDS * 6
                pe.wait_ge(eig_v, e + 4)
                nc.tensor.matmul(psum[7][:, 0, 0:1], ones[:, :], sums[:, 0:1], start=True, stop=True).then_inc(eig_pe, 1)
                pe.wait_ge(eig_v, e + 6)
                nc.tensor.matmul(psum[7][:, 1, :], sym[:, :], power[:, :], start=True, stop=True).then_inc(eig_pe, 1)
                pe.wait_ge(eig_v, e + 8)
                nc.tensor.matmul(psum[7][:, 0, 0:2], ones[:, :], sums[:, 0:2], start=True, stop=True).then_inc(eig_pe, 1)

            @block.vector
            def _(dve):
                vec = nc.vector
                vec.memset(rows_b[:, :], 0.0).then_inc(rows_zeroed, 1)
                dve.wait_ge(rows_loaded, 16 * len(ROWS))
                vec.tensor_tensor(rows_a[:, :], rows_a[:, :], rows_b[:, :], ALU.add).then_inc(v, 1)
                dve.wait_ge(products, 1)
                for n, (_, dst) in enumerate(TRANSPOSES):
                    t = vec.tensor_copy(dst, psum[n // 4][:, n % 4, :])
                t.then_inc(v, 1)
                dve.wait_ge(products, 2)
                vec.tensor_copy(c["cols"][:, :], psum[2][:, 0, 0:20]).then_inc(v, 1)
                dve.wait_ge(v, 3)
                for j in range(2):
                    t = vec.tensor_scalar(avec[:, j, :], ones[:, :], c["cols"][:, 18 + j:19 + j], None, ALU.mult)
                t.then_inc(v, 1)
                vec.tensor_tensor(sym[:, :], adj, adjT[:, :], ALU.add).then_inc(v, 1)
                dve.wait_ge(v, 5)
                vec.tensor_scalar(sym[:, :], sym[:, :], 0.5, None, ALU.mult).then_inc(v, 1)
                dve.wait_ge(v, 6)
                vec.tensor_tensor_reduce(scratch[:, :], sym[:, :], sym[:, :], 1.0, 0.0, ALU.mult, ALU.add,
                                         sums[:, 0:1]).then_inc(eig_v, 1)
                for n in range(2 * SKIPS):
                    kind, q = n // SKIPS, n % SKIPS
                    dve.wait_ge(products, 3 + n)
                    vec.tensor_copy(c["WT"][:, kind, q, :, :], psum[3 + n % 2][:, :, :]).then_inc(copied, 1)
                dve.wait_ge(products, 3 + 2 * SKIPS)
                vec.tensor_scalar(c["Gqk"][:, :], psum[5][:, 0, :], float(P) ** -0.5, None, ALU.mult)
                vec.tensor_scalar(c["Wx"][:, 1, :], c["Wx"][:, 1, :], float(HD) ** -0.5, None, ALU.mult)
                vec.tensor_copy(c["Gvo"][:, :], psum[5][:, 1, :])
                vec.tensor_copy(c["a1rep"][:, :], psum[5][:, 2, :])
                vec.tensor_copy(c["a2rep"][:, :], psum[5][:, 3, :])
                vec.tensor_copy(c["rowsum"][:, :], psum[6][0:1, 0, :])
                vec.tensor_copy(c["identb"][:, :], ident[:, :])
                vec.tensor_scalar(c["gat_mask"][:, :], adj, 0.0, NEG, ALU.is_equal, ALU.mult)
                vec.tensor_scalar(c["head_mask"][:, :], adj, 0.0, NEG3, ALU.is_le, ALU.mult)
                dve.wait_ge(small_loaded, 16 * len(SMALL))
                vec.tensor_copy(bpart[:, 0, :, :], brow[:, :, :]).then_inc(v, 1)
                dve.wait_ge(v, 7)
                vec.tensor_tensor(bres[:, :, :], brow[:, :, :], bpart[:, 0, :, :], ALU.subtract).then_inc(v, 1)
                dve.wait_ge(v, 8)
                vec.tensor_copy(bpart[:, 1, :, :], bres[:, :, :]).then_inc(v, 1)
                dve.wait_ge(v, 9)
                vec.tensor_tensor(bres[:, :, :], bres[:, :, :], bpart[:, 1, :, :], ALU.subtract).then_inc(v, 1)
                dve.wait_ge(v, 10)
                vec.tensor_copy(bpart[:, 2, :, :], bres[:, :, :]).then_inc(split_ready, 1)
                dve.wait_ge(eig_pe, 1)
                vec.tensor_scalar(stat[:, 0:1], psum[7][:, 0, 0:1], 1e-30, None, ALU.add).then_inc(eig_v, 1)
                dve.wait_ge(root_ready, 1)
                vec.reciprocal(stat[:, 1:2], norm[:, :]).then_inc(v, 1)
                dve.wait_ge(v, 11)
                vec.scalar_tensor_tensor(power[:, :], sym[:, :], stat[:, 1:2], ident[:, :], ALU.mult, ALU.add) \
                    .then_inc(eig_v, 1)

                def normalise(r):
                    dve.wait_ge(eig_v, r * 6 + 3)
                    vec.tensor_tensor(scratch[:, :], power[:, :], ident[:, :], ALU.mult).then_inc(v, 1)
                    dve.wait_ge(v, r + 12)
                    vec.reduce_sum(sums[:, 0:1], scratch[:, :], AX).then_inc(eig_v, 1)
                    dve.wait_ge(eig_pe, r * 4 + 2)
                    vec.reciprocal(stat[:, 2:3], psum[7][:, 0, 0:1]).then_inc(eig_v, 1)
                    dve.wait_ge(eig_v, r * 6 + 5)
                    vec.tensor_scalar(power[:, :], power[:, :], stat[:, 2:3], None, ALU.mult).then_inc(eig_v, 1)

                with dve.Fori(0, POWER_ROUNDS) as r:
                    normalise(r)
                    for s in range(3):
                        dve.wait_ge(eig_pe, r * 4 + 3 + s)
                        vec.tensor_copy(power[:, :], psum[7][:, 1, :]).then_inc(eig_v, 1)
                e, m = POWER_ROUNDS * 6, POWER_ROUNDS * 4
                normalise(POWER_ROUNDS)
                dve.wait_ge(eig_pe, m + 3)
                dve.wait_ge(eig_v, e + 6)
                vec.tensor_tensor_reduce(scratch[:, :], psum[7][:, 1, :], power[:, :], 1.0, 0.0, ALU.mult,
                                         ALU.add, sums[:, 0:1]).then_inc(eig_v, 1)
                dve.wait_ge(eig_v, e + 7)
                vec.tensor_tensor_reduce(scratch[:, :], power[:, :], power[:, :], 1.0, 0.0, ALU.mult,
                                         ALU.add, sums[:, 1:2]).then_inc(eig_v, 1)
                dve.wait_ge(eig_pe, m + 4)
                n = POWER_ROUNDS + 12
                vec.reciprocal(stat[:, 0:1], psum[7][:, 0, 1:2]).then_inc(v, 1)
                dve.wait_ge(v, n + 1)
                vec.tensor_scalar(stat[:, 1:2], psum[7][:, 0, 0:1], stat[:, 0:1], 1e-8, ALU.mult, ALU.add) \
                    .then_inc(v, 1)
                dve.wait_ge(v, n + 2)
                vec.reciprocal(stat[:, 2:3], stat[:, 1:2]).then_inc(v, 1)
                dve.wait_ge(v, n + 3)
                vec.tensor_scalar(stat[:, 3:4], stat[:, 2:3], 2.0, None, ALU.mult).then_inc(v, 1)
                dve.wait_ge(v, n + 4)
                vec.scalar_tensor_tensor(c["lapT"][:, :], adjT[:, :], stat[:, 3:4], ident[:, :], ALU.mult,
                                         ALU.subtract)


def attention_layer(nc, c, X, psum, NG, x):
    layer = 0 if x is not None else 1
    ctx = ExitStack()
    with ctx:
        def sb(name, shape, dt=F32):
            return ctx.enter_context(nc.sbuf_tensor(f"{name}_{layer}", shape, dt))

        sem = ctx.enter_context(phase_semaphores(nc, f"layer{layer}"))

        ring = [P, 2, GROUP, P]
        xin, xT, val, prob, probT, res = (sb(n, ring) for n in ("xin", "xT", "val", "prob", "probT", "res"))
        keyT = sb("keyT", ring) if layer == 0 else None
        score = sb("score", ring)
        top, total, inv = (sb(n, [P, 2, GROUP]) for n in ("top", "total", "inv"))
        st6, mv, rstd = sb("st6", [P, 2, GROUP, 6]), sb("mv", [P, 2, GROUP, 2]), sb("rstd", [P, 2, GROUP])
        var, shift = sb("var", [P, 2, 2, GROUP]), sb("shift", [P, 2, GROUP])

        loaded, staged = ([sem(f"{n}{b}") for b in range(2)] for n in ("loaded", "staged"))
        xT_done, xT_copied = sem("xT_done"), sem("xT_copied")
        key_done, key_copied, val_done, val_copied = sem("key_done"), sem("key_copied"), sem("val_done"), sem("val_copied")
        scores_done, scores_ready, top_ready = sem("scores_done"), sem("scores_ready"), sem("top_ready")
        probs_ready, probT_done, probT_copied = sem("probs_ready"), sem("probT_done"), sem("probT_copied")
        mixed, inv_ready, res_ready = sem("mixed"), sem("inv_ready"), sem("res_ready")
        st6_ready, stats_ready, var_ready = sem("st6_ready"), sem("stats_ready"), sem("var_ready")
        scale_ready, rstd_ready, normed = sem("scale_ready"), sem("rstd_ready"), sem("normed")
        b_xT, b_key, b_val, b_score, b_probT, b_mix = psum[0:6]
        small_slope = sem("small_slope")
        LAG, HEAD = 2, 6

        with nc.Block() as block:
            @block.sync
            def _(sync):
                def step(i, u):
                    if live(i, NG):
                        if layer == 0:
                            after_nop(sync, loaded[u], landed(i, u))
                        after_nop(sync, xT_done, i - 1)
                        sync.dma_start(xin[:, u], batches(X, i)).then_inc(staged[u], 16)
                        if layer == 0 and (not isinstance(i, int) or i + 2 < NG):
                            load(i + 2, u)

                def load(g, b):
                    sync.dma_start(batches(X, g), x[bass.ds(g * GROUP, GROUP), :, :].rearrange("b t c -> t b c")) \
                        .then_inc(loaded[b], 16)

                if layer == 0:
                    load(0, 0)
                    load(1, 1)
                run_steps(sync, step, NG, 0, HEAD, NG - 2)

            @block.tensor
            def _(pe):
                def transpose_x(g, b):
                    after(pe, staged[b], landed(g, b))
                    after(pe, xT_copied, g)
                    for k in range(GROUP):
                        t = nc.tensor.transpose(b_xT[:, k, :], xin[:, b, k, :], c["ident"][:, :])
                    t.then_inc(xT_done, 1)

                def mix(g, b):
                    after(pe, probT_copied, g + 1)
                    after(pe, val_copied, g + 1)
                    after(pe, res_ready, g)
                    for k in range(GROUP):
                        t = nc.tensor.matmul(b_mix[:, k, :], probT[:, b, k, :], val[:, b, k, :], start=True, stop=True)
                    t.then_inc(mixed, 1)

                def keys(g, b):
                    after(pe, xT_copied, g + 1)
                    after(pe, key_copied, g)
                    nc.tensor.matmul(b_key[:, :, :], c["Gqk"][:, :], xT[:, b], start=True, stop=True) \
                        .then_inc(key_done, 1)

                def values(g, b):
                    after(pe, xT_copied, g + 1)
                    after(pe, val_copied, g)
                    w = c["Gvo"] if layer == 0 else c["W1g"]
                    for k in range(GROUP):
                        t = nc.tensor.matmul(b_val[:, k, :], xT[:, b, k, :], w[:, :], start=True, stop=True)
                    t.then_inc(val_done, 1)

                def transpose_probs(g, b):
                    after(pe, probs_ready, g + 1)
                    after(pe, probT_copied, g)
                    for k in range(GROUP):
                        t = nc.tensor.transpose(b_probT[:, k, :], prob[:, b, k, :], c["ident"][:, :])
                    t.then_inc(probT_done, 1)

                def scores(g, b):
                    after(pe, scores_ready, g)
                    if layer == 0:
                        after(pe, key_copied, g + 1)
                        for k in range(GROUP):
                            t = nc.tensor.matmul(b_score[:, k, :], keyT[:, b, k, :], xT[:, b, k, :],
                                                 start=True, stop=True)
                    else:
                        nc.tensor.matmul(b_score[:, :, :], c["identb"][:, :], over(c["gat_mask"][:, :]),
                                         start=True, stop=True)
                        nc.tensor.matmul(b_score[:, :, :], c["a2rep"][:, :], xT[:, b], start=False, stop=True, skip_group_check=True)
                        for k in range(GROUP):
                            t = nc.tensor.matmul(b_score[:, k, :], xT[:, b, k, :], c["a1rep"][:, :],
                                                 start=False, stop=True, skip_group_check=True)
                    t.then_inc(scores_done, 1)

                def step(i, u):
                    if live(i, NG):
                        transpose_x(i, u)
                    if live(i - 2, NG):
                        mix(i - 2, u)
                    if live(i, NG):
                        if layer == 0:
                            keys(i, u)
                        values(i, u)
                    if live(i - 1, NG):
                        transpose_probs(i - 1, 1 - u)
                    if live(i, NG):
                        scores(i, u)
                run_steps(pe, step, NG, LAG, HEAD)

            @block.scalar
            def _(act):
                def copy_xT(g, b):
                    after(act, xT_done, g + 1)
                    after(act, scores_done, g - 1)
                    nc.scalar.activation(xT[:, b], b_xT[:, :, :], ACT.Copy).then_inc(xT_copied, 1)

                def exps(g, b):
                    after(act, top_ready, g + 1)
                    after(act, probT_done, g - 1)
                    after(act, inv_ready, g - 1)
                    for k in range(GROUP):
                        t = nc.scalar.activation(prob[:, b, k, :], score[:, b, k, :], ACT.Exp,
                                                 bias=top[:, b, k:k + 1], accum_out=total[:, b, k:k + 1])
                    t.then_inc(probs_ready, 1)

                def copy_values(g, b):
                    after(act, val_done, g + 1)
                    after(act, mixed, g - 1)
                    nc.scalar.activation(val[:, b], b_val[:, :, :], ACT.Copy).then_inc(val_copied, 1)

                def copy_probT(g, b):
                    after(act, probT_done, g + 1)
                    after(act, mixed, g - 1)
                    nc.scalar.activation(probT[:, b], b_probT[:, :, :], ACT.Copy).then_inc(probT_copied, 1)

                def leaky(g, b):
                    after(act, scores_done, g + 1)
                    after(act, probs_ready, g - 1)
                    nc.scalar.activation(score[:, b], b_score[:, :, :], ACT.Copy, scale=ALPHA) \
                        .then_inc(small_slope, 1)

                def copy_keys(g, b):
                    after(act, key_done, g + 1)
                    after(act, scores_done, g - 1)
                    nc.scalar.activation(keyT[:, b], b_key[:, :, :], ACT.Copy).then_inc(key_copied, 1)

                def normalise(g, b):
                    after(act, rstd_ready, g + 1)
                    for k in range(GROUP):
                        t = nc.scalar.activation(
                            X[:, bass.ds(g * GROUP + k, 1), :].rearrange("p a c -> p (a c)"), res[:, b, k, :],
                            ACT.Identity, bias=shift[:, b, k:k + 1], scale=rstd[:, b, k:k + 1])
                    t.then_inc(normed, 1)

                def step(i, u):
                    if live(i, NG):
                        copy_xT(i, u)
                    if live(i - 1, NG):
                        exps(i - 1, 1 - u)
                    if live(i, NG):
                        if layer == 0:
                            copy_keys(i, u)
                        copy_values(i, u)
                    if live(i - 1, NG):
                        copy_probT(i - 1, 1 - u)
                    if live(i, NG) and layer == 1:
                        leaky(i, u)
                    if live(i - 3, NG):
                        normalise(i - 3, 1 - u)
                run_steps(act, step, NG, LAG + 1, HEAD)

            @block.vector
            def _(dve):
                def biased(g, b):
                    after(dve, scores_done, g + 1)
                    after(dve, probs_ready, g - 1)
                    nc.vector.tensor_tensor(score[:, b], b_score[:, :, :], over(c["causal"][:, :]), ALU.add) \
                        .then_inc(scores_ready, 1)

                def row_max(g, b):
                    after(dve, scores_ready, g + 1)
                    after(dve, probs_ready, g - 1)
                    nc.vector.tensor_reduce(top[:, b, :], score[:, b], AX, ALU.max, negate=True).then_inc(top_ready, 1)

                def residual(g, b):
                    after(dve, probs_ready, g + 1)
                    nc.vector.reciprocal(inv[:, b, :], total[:, b, :]).then_inc(inv_ready, 1)
                    after(dve, inv_ready, g + 1)
                    after(dve, mixed, g + 1)
                    after(dve, normed, g - 1)
                    for k in range(GROUP):
                        t = nc.vector.scalar_tensor_tensor(
                            res[:, b, k, :], b_mix[:, k, :], inv[:, b, k:k + 1],
                            X[:, bass.ds(g * GROUP + k, 1), :].rearrange("p a c -> p (a c)"), ALU.mult, ALU.add)
                    t.then_inc(res_ready, 1)

                def leaky(g, b):
                    after(dve, small_slope, g + 1)
                    nc.vector.tensor_tensor(score[:, b], b_score[:, :, :], score[:, b], ALU.max) \
                        .then_inc(scores_ready, 1)

                def step(i, u):
                    if live(i - 1, NG):
                        if layer == 0:
                            biased(i - 1, 1 - u)
                        else:
                            leaky(i - 1, 1 - u)
                        row_max(i - 1, 1 - u)
                    if live(i - 2, NG):
                        residual(i - 2, u)
                        tile_stats(nc, dve, res[:, u], st6, u, i - 2, res_ready, st6_ready)
                        tile_moments(nc, dve, st6, mv, u, i - 2, st6_ready, normed, stats_ready)
                run_steps(dve, step, NG, LAG, HEAD)

            @block.gpsimd
            def _(pool):
                def step(i, u):
                    layer_rstd(nc, pool, c, mv, var, rstd, shift, u, i, stats_ready, normed, var_ready, scale_ready,
                               rstd_ready)
                run_steps(pool, step, NG, 0, HEAD)


def tile_stats(nc, dve, tiles, st6, b, g, res_ready, st6_ready):
    if res_ready is not None:
        after(dve, res_ready, g + 1)
    for k in range(GROUP):
        t = nc.vector.bn_stats(st6[:, b, k, :], tiles[:, k, :])
    t.then_inc(st6_ready, 1)


def tile_moments(nc, dve, st6, mv, b, g, st6_ready, mv_free, stats_ready):
    after_nop(dve, mv_free, g - 1)
    after_nop(dve, st6_ready, g + 1)
    for k in range(GROUP):
        t = nc.vector.bn_aggr(mv[:, b, k, :], st6[:, b, k, :])
    t.then_inc(stats_ready, 1)


def layer_rstd(nc, pool, c, mv, var, rstd, shift, b, g, stats_ready, normed, var_ready, scale_ready, rstd_ready):
    after_nop(pool, stats_ready, g + 1)
    nc.gpsimd.tensor_scalar(var[:, b, 0, :], mv[:, b, :, 1], EPS, None, ALU.add)
    nc.gpsimd.tensor_scalar(var[:, b, 1, :], mv[:, b, :, 0], -1.0, None, ALU.mult).then_inc(var_ready, 1)
    after_nop(pool, normed, g - 1)
    after_nop(pool, var_ready, g + 1)
    nc.gpsimd.tensor_tensor(rstd[:, b, :], var[:, b, 0, :], c["half"][:, :], ALU.pow).then_inc(scale_ready, 1)
    after(pool, scale_ready, g + 1)
    nc.gpsimd.tensor_tensor(shift[:, b, :], var[:, b, 1, :], rstd[:, b, :], ALU.mult).then_inc(rstd_ready, 1)


def gcn_layer(nc, c, X, H, psum, NG):
    ctx = ExitStack()
    with ctx:
        def sb(name):
            return ctx.enter_context(nc.sbuf_tensor(f"gcn_{name}", [P, 2, GROUP, P], F32))

        sem = ctx.enter_context(phase_semaphores(nc, "gcn"))

        xin, m1, h1, m2 = sb("xin"), sb("m1"), sb("h1"), sb("m2")
        staged = [sem(f"staged{b}") for b in range(2)]
        m1_done, m1_copied, h1_done, h1_ready = sem("m1_done"), sem("m1_copied"), sem("h1_done"), sem("h1_ready")
        m2_done, m2_copied, h2_done, h2_ready = sem("m2_done"), sem("m2_copied"), sem("h2_done"), sem("h2_ready")
        LAG, HEAD = 1, 4

        with nc.Block() as block:
            @block.sync
            def _(sync):
                def step(i, u):
                    after_nop(sync, m1_done, i - 1)
                    sync.dma_start(xin[:, u], batches(X, i)).then_inc(staged[u], 16)
                run_steps(sync, step, NG, 0, HEAD)

            @block.tensor
            def _(pe):
                def spread_x(g, b):
                    after(pe, staged[b], landed(g, b))
                    after(pe, m1_copied, g - 1)
                    for k in range(GROUP):
                        t = nc.tensor.matmul(psum[b][:, k, :], xin[:, b, k, :], c["adjT"][:, :], start=True, stop=True)
                    t.then_inc(m1_done, 1)

                def project_1(g, b):
                    after(pe, h1_ready, g - 1)
                    nc.tensor.matmul(psum[2 + b][:, :, :], c["rowsum"][:, :], over(c["bg"][:, 0, :]),
                                     start=True, stop=True)
                    after(pe, m1_copied, g + 1)
                    for k in range(GROUP):
                        t = nc.tensor.matmul(psum[2 + b][:, k, :], m1[:, b, k, :], c["Wg"][:, 0, :],
                                             start=False, stop=True, skip_group_check=True)
                    t.then_inc(h1_done, 1)

                def spread_h(g, b):
                    after(pe, h1_ready, g + 1)
                    after(pe, m2_copied, g - 1)
                    for k in range(GROUP):
                        t = nc.tensor.matmul(psum[4 + b][:, k, :], h1[:, b, k, :], c["adjT"][:, :],
                                             start=True, stop=True)
                    t.then_inc(m2_done, 1)

                def project_2(g, b):
                    after(pe, h2_ready, g - 1)
                    nc.tensor.matmul(psum[6 + b][:, :, :], c["bg"][:, 1, :], over(c["rowsum"][:, :]),
                                     start=True, stop=False)
                    after(pe, m2_copied, g + 1)
                    nc.tensor.matmul(psum[6 + b][:, :, :], c["Wg"][:, 1, :], m2[:, b], start=False, stop=True) \
                        .then_inc(h2_done, 1)

                def step(i, u):
                    if live(i, NG):
                        spread_x(i, u)
                    if live(i - 1, NG):
                        spread_h(i - 1, 1 - u)
                    if live(i, NG):
                        project_1(i, u)
                    if live(i - 1, NG):
                        project_2(i - 1, 1 - u)
                run_steps(pe, step, NG, LAG, HEAD)

            @block.scalar
            def _(act):
                def step(i, u):
                    if live(i, NG):
                        after(act, m1_done, i + 1)
                        after(act, h1_done, i - 1)
                        nc.scalar.activation(m1[:, u], psum[u][:, :, :], ACT.Copy).then_inc(m1_copied, 1)
                    if live(i - 1, NG):
                        after(act, h2_done, i)
                        nc.scalar.activation(batches(H, i - 1), psum[7 - u][:, :, :], ACT.Relu).then_inc(h2_ready, 1)
                run_steps(act, step, NG, LAG, HEAD)

            @block.vector
            def _(dve):
                def step(i, u):
                    if live(i - 1, NG):
                        after(dve, m2_done, i)
                        after(dve, h2_done, i - 2)
                        nc.vector.tensor_copy(m2[:, 1 - u], psum[5 - u][:, :, :]).then_inc(m2_copied, 1)
                    if live(i, NG):
                        after(dve, h1_done, i + 1)
                        after(dve, m2_done, i - 1)
                        nc.vector.tensor_scalar(h1[:, u], psum[2 + u][:, :, :], 0.0, None, ALU.max) \
                            .then_inc(h1_ready, 1)
                run_steps(dve, step, NG, LAG, HEAD)


def lstm_pass(nc, c, H, psum, B, p):
    nb = {1: 4, 2: 8, 3: 8, 4: 16}[p]
    nw = P // p
    cols = nb * nw
    pairs = B // nb // 2
    I, F, G, O = range(GATES)
    gates = [[I, G, O]] + [[I, G, F, O]] * (p - 1)
    per_chunk = sum(len(g) for g in gates)
    q = p - 1
    ctx = ExitStack()
    with ctx:
        def sb(name):
            return ctx.enter_context(nc.sbuf_tensor(f"lstm{p}_{name}", [P, 2, nb, nw], F32))

        sem = ctx.enter_context(phase_semaphores(nc, f"lstm{p}"))

        def sems(name):
            return [sem(f"{name}{b}") for b in range(2)]

        gate = [sb(f"gate{g}") for g in range(GATES)]
        cell, kept, tanh_c, hidden = sb("cell"), sb("kept"), sb("tanh_c"), sb("hidden")
        gate_done, gate_ready, fresh_ready, kept_ready = sems("gate_done"), sems("gate_ready"), sems("fresh"), sems("kept")
        cell_ready, tanh_ready, hidden_ready = sems("cell"), sems("tanh"), sems("hidden")

        def bank(b, g):
            return flat(psum[4 * b + g])[:, 0:cols].rearrange("p (b w) -> p b w", b=nb)

        def tokens(j, b, t):
            return H[:, bass.ds((j * 2 + b) * nb, nb), t:t + (nw - 1) * p + 1:p]

        def gates_before(j, t):
            return j * per_chunk + sum(len(g) for g in gates[:t])

        cells = [(t, b) for t in range(p) for b in range(2)]

        def run_pairs(eng, head, tail=None):
            def body(j, first):
                for n, (t, b) in enumerate(cells):
                    head(j, t, b)
                    if tail is not None and (n or not first):
                        tail(*((j, *cells[n - 1]) if n else (j - 1, *cells[-1])))
            body(0, True)
            with eng.Fori(1, pairs) as j:
                body(j, False)
            if tail is not None:
                tail(pairs - 1, *cells[-1])

        with nc.Block() as block:
            @block.tensor
            def _(pe):
                def products(j, t, b):
                    after(pe, gate_ready[b], gates_before(j, t))
                    for g in gates[t]:
                        m = nc.tensor.matmul(bank(b, g), c["WT"][:, 0, q, g, :], tokens(j, b, t),
                                             start=True, stop=(t == 0))
                        if t == 0:
                            m.then_inc(gate_done[b], 1)
                    if t:
                        after(pe, hidden_ready[b], j * p + t)
                        for g in gates[t]:
                            nc.tensor.matmul(bank(b, g), c["WT"][:, 1, q, g, :], hidden[:, b],
                                             start=False, stop=True).then_inc(gate_done[b], 1)
                run_pairs(pe, products)

            @block.scalar
            def _(act):
                def gate_functions(j, t, b):
                    after(act, hidden_ready[b], j * p + t)
                    for n, g in enumerate(gates[t]):
                        after(act, gate_done[b], gates_before(j, t) + n + 1)
                        nc.scalar.activation(gate[g][:, b], bank(b, g), ACT.Tanh if g == G else ACT.Sigmoid,
                                             bias=c["cols"][:, q * GATES + g:q * GATES + g + 1]) \
                            .then_inc(gate_ready[b], 1)

                def tanh_cell(j, t, b):
                    after(act, cell_ready[b], j * p + t + 1)
                    nc.scalar.activation(tanh_c[:, b], cell[:, b], ACT.Tanh).then_inc(tanh_ready[b], 1)
                run_pairs(act, gate_functions, tanh_cell)

            @block.vector
            def _(dve):
                def update_cell(j, t, b):
                    if t == 0:
                        after(dve, tanh_ready[b], j * p)
                        after(dve, gate_ready[b], gates_before(j, t) + 2)
                        nc.vector.tensor_tensor(cell[:, b], gate[I][:, b], gate[G][:, b], ALU.mult) \
                            .then_inc(cell_ready[b], 1)
                        return
                    after(dve, gate_ready[b], gates_before(j, t) + 2)
                    nc.vector.tensor_tensor(gate[G][:, b], gate[I][:, b], gate[G][:, b], ALU.mult) \
                        .then_inc(fresh_ready[b], 1)
                    after(dve, gate_ready[b], gates_before(j, t) + 3)
                    after(dve, cell_ready[b], j * p + t)
                    nc.vector.tensor_tensor(kept[:, b], gate[F][:, b], cell[:, b], ALU.mult) \
                        .then_inc(kept_ready[b], 1)
                    after(dve, fresh_ready[b], j * (p - 1) + t)
                    after(dve, kept_ready[b], j * (p - 1) + t)
                    nc.vector.tensor_tensor(cell[:, b], kept[:, b], gate[G][:, b], ALU.add) \
                        .then_inc(cell_ready[b], 1)

                def update_hidden(j, t, b):
                    after(dve, tanh_ready[b], j * p + t + 1)
                    after(dve, gate_ready[b], gates_before(j, t + 1))
                    dst = hidden[:, b] if t < p - 1 else tokens(j, b, t)
                    nc.vector.tensor_tensor(dst, gate[O][:, b], tanh_c[:, b], ALU.mult).then_inc(hidden_ready[b], 1)
                run_pairs(dve, update_cell, update_hidden)


def transformer_attention(nc, c, X, H, psum, NG):
    ctx = ExitStack()
    with ctx:
        def sb(name, shape, dt=F32):
            return ctx.enter_context(nc.sbuf_tensor(f"tr_{name}", shape, dt))

        sem = ctx.enter_context(phase_semaphores(nc, "tr"))

        tile, ring = [P, GROUP, P], [P, 2, GROUP, P]
        hin, x3, val = sb("hin", ring), sb("x3", ring), sb("val", ring)
        res0, m1, hidden, x1, x1T, qT, kT = (sb(n, tile) for n in ("res0", "m1", "hidden", "x1", "x1T", "qT", "kT"))
        prob, probT = sb("prob", [P, HEADS, GROUP, P]), sb("probT", [P, HEADS, GROUP, P])
        mixed, mixedT, res2, x2 = (sb(n, tile) for n in ("mixed", "mixedT", "res2", "x2"))
        top, total, inv = (sb(n, [P, HEADS, GROUP]) for n in ("top", "total", "inv"))
        norms = [(sb(f"st6_{n}", [P, 1, GROUP, 6]), sb(f"mv_{n}", [P, 1, GROUP, 2]), sb(f"var_{n}", [P, GROUP]),
                  sb(f"rstd_{n}", [P, GROUP])) for n in range(3)]
        norm_sems = [tuple(sem(f"{s}_{n}") for s in ("st6_ready", "stats_ready", "var_ready", "rstd_ready", "normed"))
                     for n in range(3)]
        hin_staged, x3_stored, x1_stored, x2_stored = ([sem(f"{n}{b}") for b in range(2)] for n in
                                                       ("hin_staged", "x3_stored", "x1_stored", "x2_stored"))
        h_turned, res0_ready, m1_done, m1_copied, h_done = (
            sem(n) for n in ("h_turned", "res0_ready", "m1_done", "m1_copied", "h_done"))
        scaled, affine, x1_ready, x1_turned, x1T_copied = (
            sem(n) for n in ("scaled", "affine", "x1_ready", "x1_turned", "x1T_copied"))
        q_done, q_copied, k_done, k_copied, v_done, v_copied = (
            sem(n) for n in ("q_done", "q_copied", "k_done", "k_copied", "v_done", "v_copied"))
        scores_done, top_ready, probs_ready, inv_ready = (
            sem(n) for n in ("scores_done", "top_ready", "probs_ready", "inv_ready"))
        p_turned, pT_copied_a, pT_copied_v, mix_done, mix_ready = (
            sem(n) for n in ("p_turned", "pT_copied_a", "pT_copied_v", "mix_done", "mix_ready"))
        mix_turned, mixT_copied, o_done, res2_ready, scaled2, x2_ready = (
            sem(n) for n in ("mix_turned", "mixT_copied", "o_done", "res2_ready", "scaled2", "x2_ready"))
        Wc, Wq, Wk, Wv, Wo = (c["Wx"][:, j, :] for j in range(5))
        g1, be1, g2, be2 = (c["rep"][:, j, :] for j in range(4))
        b_x1T, b_hT, b_o, b_q, b_k, b_m1, b_v, b_h, b_mix, b_mixT = (
            psum[n] for n in (4, 5, 6, 7, 4, 5, 6, 7, 5, 6))
        b_pT = [psum[n] for n in (4, 5, 6, 4)]
        LAG, HEAD = 3, 6

        def up_to(n):
            return min(n, NG) if isinstance(n, int) else n

        with nc.Block() as block:
            @block.sync
            def _(sync):
                def step(i, u):
                    if live(i, NG):
                        after_nop(sync, h_turned, i - 1)
                        sync.dma_start(hin[:, u], batches(H, i)).then_inc(hin_staged[u], 16)
                    if live(i - 1, NG):
                        after_nop(sync, norm_sems[0][4], i)
                        sync.dma_start(batches(X, i - 1), x3[:, 1 - u]).then_inc(x3_stored[1 - u], 16)
                    if live(i - 2, NG):
                        after_nop(sync, x1_ready, i - 1)
                        sync.dma_start(batches(H, i - 2), x1[:, :, :]).then_inc(x1_stored[u], 16)
                    if live(i - 5, NG):
                        after_nop(sync, x2_ready, i - 4)
                        sync.dma_start(batches(H, i - 5), x2[:, :, :]).then_inc(x2_stored[1 - u], 16)
                run_steps(sync, step, NG, 5, HEAD)
                for b in range(2):
                    sync.wait_ge(x3_stored[b], landed(NG - 2 + b, b))
                    sync.wait_ge(x2_stored[b], landed(NG - 2 + b, b))

            @block.tensor
            def _(pe):
                def bias_rows(bank, j):
                    nc.tensor.matmul(bank[:, :, :], c["ones3"][:, :], over(c["bias3"][:, j, :]), start=True, stop=True)

                def turn_x1(g):
                    after(pe, x1_ready, g + 1)
                    after(pe, k_copied, g)
                    after(pe, pT_copied_a, (g - 1) * 2)
                    for k in range(GROUP):
                        t = nc.tensor.transpose(b_x1T[:, k, :], x1[:, k, :], c["ident"][:, :])
                    t.then_inc(x1_turned, 1)

                def turn_h(g, b):
                    after(pe, hin_staged[b], landed(g, b))
                    after(pe, mix_ready, g - 3)
                    after(pe, m1_copied, g - 1)
                    after(pe, res0_ready, g)
                    for k in range(GROUP):
                        t = nc.tensor.transpose(b_hT[:, k, :], hin[:, b, k, :], c["ident"][:, :])
                    t.then_inc(h_turned, 1)

                def project_out(g):
                    after(pe, mixT_copied, g + 1)
                    bias_rows(b_o, 1)
                    for k in range(GROUP):
                        t = nc.tensor.matmul(b_o[:, k, :], mixedT[:, k, :], Wo, start=False, stop=True, skip_group_check=True)
                    t.then_inc(o_done, 1)

                def queries(g):
                    after(pe, x1T_copied, g + 1)
                    after(pe, norm_sems[1][4], g + 1)
                    nc.tensor.matmul(b_q[:, :, :], Wq, x1T[:, :, :], start=True, stop=True).then_inc(q_done, 1)

                def keys(g):
                    nc.tensor.matmul(b_k[:, :, :], Wk, x1T[:, :, :], start=True, stop=True).then_inc(k_done, 1)

                def spread_x(g, b):
                    after(pe, norm_sems[0][4], g + 1)
                    after(pe, res0_ready, up_to(g + 2))
                    after(pe, mix_ready, g - 2)
                    for k in range(GROUP):
                        t = nc.tensor.matmul(b_m1[:, k, :], x3[:, b, k, :], c["lapT"][:, :], start=True, stop=True)
                    t.then_inc(m1_done, 1)

                def values(g):
                    after(pe, res2_ready, g - 1)
                    after(pe, v_copied, g)
                    for k in range(GROUP):
                        t = nc.tensor.matmul(b_v[:, k, :], x1T[:, k, :], Wv, start=True, stop=True)
                    t.then_inc(v_done, 1)

                def project_h(g):
                    after(pe, q_copied, g)
                    bias_rows(b_h, 0)
                    after(pe, m1_copied, g + 1)
                    for k in range(GROUP):
                        t = nc.tensor.matmul(b_h[:, k, :], m1[:, k, :], Wc, start=False, stop=True, skip_group_check=True)
                    t.then_inc(h_done, 1)

                def turn_probs(g, h):
                    after(pe, probs_ready, g * HEADS + h + 1)
                    if h == 0:
                        after(pe, k_copied, up_to(g + 2))
                        after(pe, pT_copied_a, g * 2)
                    if h == 1:
                        after(pe, m1_copied, up_to(g + 3))
                        after(pe, mix_ready, g)
                    if h == 2:
                        after(pe, v_copied, up_to(g + 2))
                        after(pe, res2_ready, g)
                    if h == 3:
                        after(pe, pT_copied_v, g * 2 + 1)
                    for k in range(GROUP):
                        t = nc.tensor.transpose(b_pT[h][:, k, :], prob[:, h, k, :], c["ident"][:, :])
                    t.then_inc(p_turned, 1)

                def mask(g, h):
                    after(pe, probs_ready, (g - 1) * HEADS + h + 1)
                    nc.tensor.matmul(psum[h][:, :, :], c["identb"][:, :], over(c["head_mask"][:, :]),
                                     start=True, stop=True)

                def mix(g, b):
                    after(pe, pT_copied_a, g * 2 + 2)
                    after(pe, pT_copied_v, g * 2 + 2)
                    for k in range(GROUP):
                        for h in range(HEADS):
                            a = k * P + h * HD
                            cols = slice(a, min(a + WIDE, GROUP * P))
                            t = nc.tensor.matmul(flat(b_mix)[:, cols], probT[:, h, k, :], flat(val[:, b])[:, cols],
                                                 start=True, stop=True)
                    t.then_inc(mix_done, 1)

                def scores(g):
                    after(pe, q_copied, g + 1)
                    after(pe, k_copied, g + 1)
                    for k in range(GROUP):
                        for h in range(HEADS):
                            rows = slice(h * HD, (h + 1) * HD)
                            t = nc.tensor.matmul(psum[h][:, k, :], qT[rows, k, :], kT[rows, k, :],
                                                 start=False, stop=True, skip_group_check=True)
                    t.then_inc(scores_done, 1)

                def turn_mixed(g):
                    after(pe, mix_ready, g + 1)
                    for k in range(GROUP):
                        t = nc.tensor.transpose(b_mixT[:, k, :], mixed[:, k, :], c["ident"][:, :])
                    t.then_inc(mix_turned, 1)

                def step(i, u):
                    if live(i - 2, NG):
                        turn_x1(i - 2)
                    if live(i, NG):
                        turn_h(i, u)
                    if live(i - 4, NG):
                        project_out(i - 4)
                    if live(i - 2, NG):
                        queries(i - 2)
                        keys(i - 2)
                    if live(i - 1, NG):
                        spread_x(i - 1, 1 - u)
                    if live(i - 2, NG):
                        values(i - 2)
                    if live(i - 1, NG):
                        project_h(i - 1)
                    for h in range(HEADS):
                        if live(i - 3, NG):
                            turn_probs(i - 3, h)
                        if live(i - 2, NG):
                            mask(i - 2, h)
                    if live(i - 3, NG):
                        mix(i - 3, 1 - u)
                    if live(i - 2, NG):
                        scores(i - 2)
                    if live(i - 3, NG):
                        turn_mixed(i - 3)
                run_steps(pe, step, NG, LAG + 1, HEAD)

            @block.scalar
            def _(act):
                def copy(bank, dst, done, n, copied):
                    after(act, done, n)
                    nc.scalar.activation(dst, bank[:, :, :], ACT.Copy).then_inc(copied, 1)

                def exps(g, h):
                    after(act, top_ready, g * HEADS + h + 1)
                    if h == 0:
                        after(act, p_turned, g * HEADS)
                        after(act, inv_ready, g)
                    for k in range(GROUP):
                        t = nc.scalar.activation(prob[:, h, k, :], psum[h][:, k, :], ACT.Exp,
                                                 bias=top[:, h, k:k + 1], accum_out=total[:, h, k:k + 1])
                    t.then_inc(probs_ready, 1)

                def step(i, u):
                    g2, g3 = i - 2, i - 3
                    if live(g2, NG):
                        after(act, v_done, g2)
                        copy(b_x1T, x1T[:, :, :], x1_turned, g2 + 1, x1T_copied)
                    if live(g3, NG):
                        exps(g3, 0)
                    if live(g2, NG):
                        copy(b_q, qT[:, :, :], q_done, g2 + 1, q_copied)
                    if live(g3, NG):
                        exps(g3, 1)
                    if live(g2, NG):
                        copy(b_k, kT[:, :, :], k_done, g2 + 1, k_copied)
                    if live(i - 1, NG):
                        after(act, h_done, i - 1)
                        copy(b_m1, m1[:, :, :], m1_done, i, m1_copied)
                    if live(g3, NG):
                        exps(g3, 2)
                    if live(g2, NG):
                        after(act, mix_done, g2 - 1)
                        copy(b_v, val[:, u], v_done, g2 + 1, v_copied)
                    if live(g3, NG):
                        exps(g3, 3)
                        after(act, mix_done, g3)
                        copy(b_pT[2], probT[:, 2], p_turned, g3 * HEADS + 3, pT_copied_a)
                        copy(b_pT[3], probT[:, 3], p_turned, g3 * HEADS + 4, pT_copied_a)
                        after(act, o_done, g3)
                        copy(b_mixT, mixedT[:, :, :], mix_turned, g3 + 1, mixT_copied)
                run_steps(act, step, NG, LAG, HEAD)

            @block.vector
            def _(dve):
                def stats(n, tiles, g, ready):
                    tile_stats(nc, dve, tiles, norms[n][0], 0, g, ready, norm_sems[n][0])

                def moments(n, g):
                    tile_moments(nc, dve, norms[n][0], norms[n][1], 0, g, norm_sems[n][0], norm_sems[n][4],
                                 norm_sems[n][1])

                def normalise(n, dst, src, g):
                    after(dve, norm_sems[n][3], g + 1)
                    for k in range(GROUP):
                        t = nc.vector.tensor_scalar(dst[:, k, :], src[:, k, :], norms[n][1][:, 0, k, 0:1],
                                                    norms[n][3][:, k:k + 1], ALU.subtract, ALU.mult)
                    t.then_inc(norm_sems[n][4], 1)

                def row_max(g, h):
                    if h == 0:
                        after(dve, scores_done, g + 1)
                    nc.vector.tensor_reduce(top[:, h, :], psum[h][:, :, :], AX, ALU.max, negate=True) \
                        .then_inc(top_ready, 1)

                def residual_0(g):
                    after(dve, h_turned, g + 1)
                    after(dve, norm_sems[0][4], g)
                    nc.vector.tensor_tensor(res0[:, :, :], b_hT[:, :, :], batches(X, g), ALU.add).then_inc(res0_ready, 1)

                def residual_2(g, b):
                    after(dve, o_done, g + 1)
                    after_nop(dve, x1_stored[b], landed(g, b))
                    after(dve, scaled2, g)
                    nc.vector.tensor_tensor(res2[:, :, :], b_o[:, :, :], batches(H, g), ALU.add).then_inc(res2_ready, 1)

                def copy_probT(g, h):
                    if h == 0:
                        after(dve, mix_done, g)
                    after(dve, p_turned, g * HEADS + h + 1)
                    nc.vector.tensor_copy(probT[:, h], b_pT[h][:, :, :]).then_inc(pT_copied_v, 1)

                def weigh_mixed(g):
                    after(dve, probs_ready, (g + 1) * HEADS)
                    nc.vector.reciprocal(inv[:, :, :], total[:, :, :]).then_inc(inv_ready, 1)
                    after(dve, inv_ready, g + 1)
                    after(dve, mix_done, g + 1)
                    after(dve, mix_turned, g)
                    nc.vector.tensor_tensor(
                        mixed[:, :, :].rearrange("p k (h d) -> p k h d", h=HEADS),
                        b_mix[:, :, :].rearrange("p k (h d) -> p k h d", h=HEADS),
                        inv[:, :, :].rearrange("p h k -> p k h").unsqueeze(3).broadcast_to([P, GROUP, HEADS, HD]),
                        ALU.mult).then_inc(mix_ready, 1)

                def step(i, u):
                    g1_, g3, g4 = i - 1, i - 3, i - 4
                    if live(g3, NG):
                        row_max(g3, 0)
                    if live(i, NG):
                        residual_0(i)
                    if live(g3, NG):
                        row_max(g3, 1)
                    if live(i, NG):
                        stats(0, res0, i, res0_ready)
                    if live(g3, NG):
                        row_max(g3, 2)
                    if live(i, NG):
                        moments(0, i)
                    if live(g4, NG):
                        residual_2(g4, u)
                    if live(g3, NG):
                        row_max(g3, 3)
                    if live(i, NG):
                        after(dve, x1_ready, i - 1)
                        after_nop(dve, x3_stored[u], landed(i - 2, u))
                        after(dve, m1_done, i - 1)
                        normalise(0, x3[:, u], res0, i)
                    if live(g4, NG):
                        stats(2, res2, g4, res2_ready)
                    if live(g1_, NG):
                        stats(1, b_h, g1_, h_done)
                    if live(g4, NG):
                        moments(2, g4)
                    if live(g1_, NG):
                        moments(1, g1_)
                    if live(g3, NG):
                        copy_probT(g3, 0)
                        copy_probT(g3, 1)
                    if live(g4, NG):
                        normalise(2, res2, res2, g4)
                    if live(g1_, NG):
                        after(dve, x1_ready, g1_)
                        normalise(1, hidden, b_h, g1_)
                    if live(g3, NG):
                        weigh_mixed(g3)
                    if live(g1_, NG):
                        after(dve, affine, i)
                        after(dve, x1_turned, g1_)
                        after_nop(dve, x1_stored[u], landed(i - 2, u))
                        nc.vector.scalar_tensor_tensor(flat(x1), flat(hidden), 0.0, flat(x3[:, 1 - u]), ALU.max, ALU.add) \
                            .then_inc(x1_ready, 1)
                run_steps(dve, step, NG, LAG + 1, HEAD)

            @block.gpsimd
            def _(pool):
                def rstd(n, g):
                    st6_ready, stats_ready, var_ready, rstd_ready, normed = norm_sems[n]
                    mv, var, rs = norms[n][1:]
                    after_nop(pool, stats_ready, g + 1)
                    nc.gpsimd.tensor_scalar(var[:, :], mv[:, 0, :, 1], EPS, None, ALU.add).then_inc(var_ready, 1)
                    after_nop(pool, var_ready, g + 1)
                    nc.gpsimd.tensor_tensor(rs[:, :], var[:, :], c["half"][:, :], ALU.pow).then_inc(rstd_ready, 1)

                def step(i, u):
                    if live(i, NG):
                        rstd(0, i)
                    if live(i - 4, NG):
                        rstd(2, i - 4)
                    if live(i - 1, NG):
                        rstd(1, i - 1)
                    if live(i - 1, NG):
                        after(pool, norm_sems[1][4], i)
                        nc.gpsimd.tensor_tensor(hidden[:, :, :], hidden[:, :, :], over(g1), ALU.mult).then_inc(scaled, 1)
                        after(pool, scaled, i)
                        nc.gpsimd.tensor_tensor(hidden[:, :, :], hidden[:, :, :], over(be1), ALU.add).then_inc(affine, 1)
                    if live(i - 4, NG):
                        after(pool, norm_sems[2][4], i - 3)
                        after(pool, x2_stored[1 - u], landed(i - 5, 1 - u))
                        nc.gpsimd.tensor_tensor(x2[:, :, :], res2[:, :, :], over(g2), ALU.mult).then_inc(scaled2, 1)
                        after(pool, scaled2, i - 3)
                        nc.gpsimd.tensor_tensor(x2[:, :, :], x2[:, :, :], over(be2), ALU.add).then_inc(x2_ready, 1)
                run_steps(pool, step, NG, LAG + 1, HEAD)


def transformer_mlp(nc, c, X, H, psum, NG, out):
    ctx = ExitStack()
    with ctx:
        def sb(name, shape, dt=F32):
            return ctx.enter_context(nc.sbuf_tensor(f"mlp_{name}", shape, dt))

        sem = ctx.enter_context(phase_semaphores(nc, "mlp"))

        ring = [P, 2, GROUP, P]
        x2, x2T, res3, part, res4, done = (sb(n, ring) for n in ("x2", "x2T", "res3", "part", "res4", "done"))
        act_h = sb("act_h", [P, 2, 2, GROUP, P])
        norms = [(sb(f"st6_{n}", [P, 2, GROUP, 6]), sb(f"mv_{n}", [P, 2, GROUP, 2]), sb(f"var_{n}", [P, 2, 2, GROUP]),
                  sb(f"rstd_{n}", [P, 2, GROUP]), sb(f"shift_{n}", [P, 2, GROUP])) for n in range(2)]
        norm_sems = [tuple(sem(f"{s}_{n}") for s in ("st6_ready", "stats_ready", "var_ready", "rstd_ready", "normed", "scale_ready"))
                     for n in range(2)]
        staged, stored = ([sem(f"{n}{b}") for b in range(2)] for n in ("staged", "stored"))
        turned, turned_copied, up_done, gelu_ready, down_done = (
            sem(n) for n in ("turned", "turned_copied", "up_done", "gelu_ready", "down_done"))
        res3_ready, scaled, affine, res4_ready = (sem(n) for n in ("res3_ready", "scaled", "affine", "res4_ready"))
        g3, be3 = c["rep"][:, 4, :], c["rep"][:, 5, :]
        LAG, HEAD = 1, 6

        with nc.Block() as block:
            @block.sync
            def _(sync):
                def step(i, u):
                    if live(i, NG):
                        after_nop(sync, res3_ready, i - 1)
                        sync.dma_start(x2[:, u], batches(H, i)).then_inc(staged[u], 16)
                    if live(i - 5, NG):
                        after_nop(sync, norm_sems[1][4], i - 4)
                        sync.dma_start(out[bass.ds((i - 5) * GROUP, GROUP), :, :].rearrange("b t c -> t b c"),
                                       done[:, 1 - u]).then_inc(stored[1 - u], 16)
                run_steps(sync, step, NG, 5, HEAD)
                for b in range(2):
                    sync.wait_ge(stored[b], landed(NG - 2 + b, b))

            @block.tensor
            def _(pe):
                def turn(g, b):
                    after(pe, staged[b], landed(g, b))
                    after(pe, turned_copied, g)
                    for k in range(GROUP):
                        t = nc.tensor.transpose(psum[0][:, k, :], x2[:, b, k, :], c["ident"][:, :])
                    t.then_inc(turned, 1)

                def down(g, b):
                    after(pe, res3_ready, g - 1)
                    nc.tensor.matmul(psum[5 + b][:, :, :], c["ones3"][:, :], over(c["bias3"][:, 2, :]),
                                     start=True, stop=True)
                    after(pe, gelu_ready, g * 2 + 2)
                    for k in range(GROUP):
                        for j in range(2):
                            t = nc.tensor.matmul(psum[5 + b][:, k, :], act_h[:, b, j, k, :], c["W2"][:, j, :],
                                                 start=False, stop=(j == 1), skip_group_check=True)
                    t.then_inc(down_done, 1)

                def up(g, b):
                    after(pe, turned_copied, g + 1)
                    after(pe, gelu_ready, g * 2 - 2)
                    for j in range(2):
                        nc.tensor.matmul(psum[1 + 2 * b + j][:, :, :], c["W1"][:, j * P:(j + 1) * P], x2T[:, b],
                                         start=True, stop=True).then_inc(up_done, 1)

                def step(i, u):
                    if live(i, NG):
                        turn(i, u)
                    if live(i - 1, NG):
                        down(i - 1, 1 - u)
                    if live(i, NG):
                        up(i, u)
                run_steps(pe, step, NG, LAG, HEAD)

            @block.scalar
            def _(act):
                def normalise(n, dst, src, g, b):
                    after(act, norm_sems[n][3], g + 1)
                    for k in range(GROUP):
                        t = nc.scalar.activation(dst[:, k, :], src[:, k, :], ACT.Identity,
                                                 bias=norms[n][4][:, b, k:k + 1], scale=norms[n][3][:, b, k:k + 1])
                    t.then_inc(norm_sems[n][4], 1)

                def step(i, u):
                    if live(i, NG):
                        after(act, turned, i + 1)
                        after(act, up_done, i * 2 - 2)
                        nc.scalar.activation(x2T[:, u], psum[0][:, :, :], ACT.Copy).then_inc(turned_copied, 1)
                        after(act, down_done, i - 1)
                        for j in range(2):
                            after(act, up_done, i * 2 + j + 1)
                            nc.scalar.activation(act_h[:, u, j], psum[1 + 2 * u + j][:, :, :], ACT.Gelu,
                                                 bias=c["cols"][:, 16 + j:17 + j]).then_inc(gelu_ready, 1)
                    if live(i - 2, NG):
                        after(act, res4_ready, i - 3)
                        normalise(0, part[:, u], res3[:, u], i - 2, u)
                    if live(i - 4, NG):
                        after_nop(act, stored[u], landed(i - 6, u))
                        normalise(1, done[:, u], res4[:, u], i - 4, u)
                run_steps(act, step, NG, 4, HEAD)

            @block.vector
            def _(dve):
                def stats(n, tiles, g, b, ready):
                    tile_stats(nc, dve, tiles, norms[n][0], b, g, ready, norm_sems[n][0])
                    tile_moments(nc, dve, norms[n][0], norms[n][1], b, g, norm_sems[n][0], norm_sems[n][4],
                                 norm_sems[n][1])

                def step(i, u):
                    w = 1 - u
                    if live(i - 1, NG):
                        after(dve, down_done, i)
                        after(dve, norm_sems[0][4], i - 2)
                        nc.vector.tensor_tensor(res3[:, w], psum[5 + w][:, :, :], x2[:, w], ALU.add) \
                            .then_inc(res3_ready, 1)
                        stats(0, res3[:, w], i - 1, w, res3_ready)
                    if live(i - 3, NG):
                        after(dve, affine, i - 2)
                        after(dve, norm_sems[1][4], i - 4)
                        nc.vector.tensor_tensor(res4[:, w], part[:, w], batches(X, i - 3), ALU.add) \
                            .then_inc(res4_ready, 1)
                        stats(1, res4[:, w], i - 3, w, res4_ready)
                run_steps(dve, step, NG, 3, HEAD)

            @block.gpsimd
            def _(pool):
                def rstd(n, g, b):
                    _, stats_ready, var_ready, rstd_ready, normed, scale_ready = norm_sems[n]
                    layer_rstd(nc, pool, c, *norms[n][1:], b, g, stats_ready, normed, var_ready, scale_ready,
                               rstd_ready)

                def step(i, u):
                    w = 1 - u
                    if live(i - 2, NG):
                        after(pool, norm_sems[0][4], i - 1)
                        nc.gpsimd.tensor_tensor(part[:, u], part[:, u], over(g3), ALU.mult).then_inc(scaled, 1)
                        after(pool, scaled, i - 1)
                        nc.gpsimd.tensor_tensor(part[:, u], part[:, u], over(be3), ALU.add).then_inc(affine, 1)
                    if live(i - 1, NG):
                        rstd(0, i - 1, w)
                    if live(i - 3, NG):
                        rstd(1, i - 3, w)
                run_steps(pool, step, NG, 3, HEAD)


_INS = ['x', 'adj', 'L0_gnn_Wqkv', 'L0_gnn_Wo', 'L1_gnn_W', 'L1_gnn_a', 'L2_gnn_Wg0', 'L2_gnn_bg0', 'L2_gnn_Wg1',
        'L2_gnn_bg1', 'L2_gnn_Wih', 'L2_gnn_Whh', 'L2_gnn_bih', 'L2_gnn_bhh', 'L3_gnn_Wc', 'L3_gnn_bc', 'L3_gnn_g1',
        'L3_gnn_be1', 'L3_gnn_Wq', 'L3_gnn_Wk', 'L3_gnn_Wv', 'L3_gnn_Wo', 'L3_gnn_bo', 'L3_gnn_g2', 'L3_gnn_be2',
        'L3_gnn_W1', 'L3_gnn_b1', 'L3_gnn_W2', 'L3_gnn_b2', 'L3_gnn_g3', 'L3_gnn_be3']


def kernel(**inputs):
    import numpy as _np
    import concourse.bacc as _bacc
    from concourse import mybir as _mybir
    from concourse.bass_utils import run_bass_kernel_spmd as _run

    nc = _bacc.Bacc("TRN2", target_bir_lowering=False, num_devices=1)
    arrays, args = {}, {}
    for name in _INS:
        arr = _np.ascontiguousarray(inputs[name])
        arrays[f"in_{name}_dram"] = arr
        args[name] = nc.dram_tensor(f"in_{name}_dram", arr.shape, _mybir.dt.from_np(arr.dtype),
                                    kind="ExternalInput").ap()
    out = nc.dram_tensor("out_0_dram", inputs["x"].shape, _mybir.dt.float32, kind="ExternalOutput").ap()
    program(nc, args, out)
    r = _run(nc, [arrays], core_ids=[0])
    return r.results[0]["out_0_dram"]
```

```python
from contextlib import ExitStack, contextmanager

import concourse.bass as bass
from concourse import mybir

F32 = mybir.dt.float32
BF16 = mybir.dt.bfloat16
ALU = mybir.AluOpType
ACT = mybir.ActivationFunctionType
AX = mybir.AxisListType.X

P = 128
GROUP = 4
EPS = 1e-5
NEG = -1e30
NEG3 = -1e9
ALPHA = 0.2
HEADS = 4
HD = P // HEADS
WIDE = 128
SKIPS = 4
GATES = 4
POWER_ROUNDS = 8


def after(eng, sem, n):
    if isinstance(n, int) and n <= 0:
        return
    eng.wait_ge(sem, n)


def after_nop(eng, sem, n):
    if isinstance(n, int) and n <= 0:
        return
    eng.wait_ge(sem, n)
    eng.nop(nofuse=True)


def run_steps(eng, step, n, lag, head, tail=None):
    assert head % 2 == 0 and n % 2 == 0 and head >= lag
    for i in range(head):
        step(i, i % 2)
    tail = n if tail is None else tail
    with eng.Fori(head // 2, tail // 2) as pair:
        step(pair * 2, 0)
        step(pair * 2 + 1, 1)
    for i in range(tail, n + lag):
        step(i, i % 2)


def live(g, n):
    return not isinstance(g, int) or 0 <= g < n


def batches(buf, g, count=GROUP):
    return buf[:, bass.ds(g * count, count), :]


def over(ap, count=GROUP):
    return ap.unsqueeze(1).broadcast_to([ap.shape[0], count, ap.shape[-1]])


def landed(g, b):
    return (g - b) * 8 + 16


@contextmanager
def phase_semaphores(nc, prefix):
    held = []

    def sem(name):
        held.append(nc.alloc_semaphore(name=f"{prefix}_{name}"))
        return held[-1]
    yield sem
    nc.clear_and_free_semaphores(held)
    nc.all_engine_barrier()


def flat(ap):
    return ap.rearrange("p k c -> p (k c)")


def program(nc, a, out):
    x = a["x"]
    B = x.shape[0]
    NG = B // GROUP
    ctx = ExitStack()

    def sb(name, shape, dt=F32):
        return ctx.enter_context(nc.sbuf_tensor(name, shape, dt))

    with ctx:
        X = sb("X", [P, B, P])
        H = sb("H", [P, B, P])
        c = dict(
            ident=sb("ident", [P, P]), identb=sb("identb", [P, P], BF16), adjT=sb("adjT", [P, P]),
            causal=sb("causal", [P, P]), gat_mask=sb("gat_mask", [P, P], BF16),
            head_mask=sb("head_mask", [P, P], BF16), lapT=sb("lapT", [P, P]), ones3=sb("ones3", [3, P], BF16),
            half=sb("half", [P, GROUP]), Gqk=sb("Gqk", [P, P]), Gvo=sb("Gvo", [P, P]), W1g=sb("W1g", [P, P]),
            a1rep=sb("a1rep", [P, P]), a2rep=sb("a2rep", [P, P]), rowsum=sb("rowsum", [1, P]),
            bg=sb("bg", [1, 2, P]), Wg=sb("Wg", [P, 2, P]),
            cols=sb("cols", [P, 20]), bias3=sb("bias3", [3, 3, P], BF16), Wx=sb("Wx", [P, 5, P]),
            W1=sb("W1", [P, 2 * P]), W2=sb("W2", [P, 2, P]), rep=sb("rep", [P, 6, P]),
        )
        lstm_weights = ExitStack()
        c["WT"] = lstm_weights.enter_context(nc.sbuf_tensor("WT", [P, 2, SKIPS, GATES, P], F32))
        psum = [ctx.enter_context(nc.psum_tensor(f"bank{i}", [P, GROUP, P], F32)) for i in range(8)]
        setup(nc, a, c, X, H, psum)
        attention_layer(nc, c, X, psum, NG, x)
        attention_layer(nc, c, X, psum, NG, None)
        gcn_layer(nc, c, X, H, psum, NG)
        for p in range(1, SKIPS + 1):
            lstm_pass(nc, c, H, psum, B, p)
        lstm_weights.close()
        transformer_attention(nc, c, X, H, psum, NG)
        transformer_mlp(nc, c, X, H, psum, NG, out)


def setup(nc, a, c, X, H, psum):
    ctx = ExitStack()
    with ctx:
        def sb(name, shape, dt=F32):
            return ctx.enter_context(nc.sbuf_tensor(name, shape, dt))

        sem = ctx.enter_context(phase_semaphores(nc, "setup"))
        ident, adjT, ones = c["ident"], c["adjT"], sb("ones", [P, P])
        raw_ih, raw_hh = H[:, 0:16, :], H[:, 16:32, :]
        adj, Wqkv, Wo, W1g = H[:, 32, :], H[:, 33:36, :], H[:, 36, :], c["W1g"]
        wT = H[:, 40:44, :]
        avec = H[:, 44:46, :]
        rows_a, rows_b = sb("rows_a", [20, P]), sb("rows_b", [20, P])
        brow, bres, bpart = sb("brow", [1, 3, P]), sb("bres", [1, 3, P]), sb("bpart", [1, 3, 3, P], BF16)
        sym, power, scratch = sb("sym", [P, P]), sb("power", [P, P]), sb("scratch", [P, P])
        sums, stat, norm = sb("sums", [P, 2]), sb("stat", [P, 4]), sb("norm", [P, 1])
        powhalf = sb("powhalf", [P, 1])

        small_loaded, lstm_loaded, bias_moved = sem("small_loaded"), sem("lstm_loaded"), sem("bias_moved")
        rows_zeroed, zeroed, ident_ready = sem("rows_zeroed"), sem("zeroed"), sem("ident_ready")
        rows_loaded = sem("rows_loaded")
        masks_filled, copied, products = sem("masks_filled"), sem("copied"), sem("products")
        v = sem("setup_v")
        root_ready, split_ready, eig_pe, eig_v = sem("root_ready"), sem("split_ready"), sem("eig_pe"), sem("eig_v")

        SMALL = [
            (adj, a["adj"]), (Wqkv, a["L0_gnn_Wqkv"].rearrange("d (j e) -> d j e", j=3)), (Wo, a["L0_gnn_Wo"]),
            (W1g[:, :], a["L1_gnn_W"]),
            (c["bg"][0:1, 0, :], a["L2_gnn_bg0"].rearrange("(a n) -> a n", a=1)),
            (c["bg"][0:1, 1, :], a["L2_gnn_bg1"].rearrange("(a n) -> a n", a=1)),
            (c["Wg"][:, 0, :], a["L2_gnn_Wg0"]), (c["Wg"][:, 1, :], a["L2_gnn_Wg1"]),
            (c["W1"][:, :], a["L3_gnn_W1"]), (c["W2"][:, :, :], a["L3_gnn_W2"].rearrange("(j d) n -> d j n", j=2)),
        ]
        SMALL += [(c["Wx"][:, j, :], a["L3_gnn_" + w]) for j, w in enumerate(("Wc", "Wq", "Wk", "Wv", "Wo"))]
        SMALL += [(c["rep"][:, j, :], a["L3_gnn_" + w].rearrange("(a n) -> a n", a=1).broadcast_to([P, P]))
                  for j, w in enumerate(("g1", "be1", "g2", "be2", "g3", "be3"))]
        SMALL += [(brow[0:1, j, :], a["L3_gnn_" + w].rearrange("(a n) -> a n", a=1))
                  for j, w in enumerate(("bc", "bo", "b2"))]
        ROWS = [
            (rows_a[0:16, :], a["L2_gnn_bih"].rearrange("q (g d) -> (q g) d", d=P)),
            (rows_a[16:18, :], a["L3_gnn_b1"].rearrange("(j d) -> j d", j=2)),
            (rows_a[18:20, :], a["L1_gnn_a"].rearrange("(j d) o -> j (d o)", j=2)),
            (rows_b[0:16, :], a["L2_gnn_bhh"].rearrange("q (g d) -> (q g) d", d=P)),
        ]

        with nc.Block() as block:
            @block.sync
            def _(sync):
                for dst, src in SMALL:
                    sync.dma_start(dst, src).then_inc(small_loaded, 16)
                sync.wait_ge(rows_zeroed, 1)
                for dst, src in ROWS:
                    sync.dma_start(dst, src).then_inc(rows_loaded, 16)
                for raw, name in ((raw_ih, "L2_gnn_Wih"), (raw_hh, "L2_gnn_Whh")):
                    sync.dma_start(raw, a[name].rearrange("q (g o) i -> o (q g) i", g=GATES)).then_inc(lstm_loaded, 16)
                sync.wait_ge(split_ready, 1)
                for part in range(3):
                    sync.dma_start(c["bias3"][part:part + 1, :, :], bpart[0:1, part, :, :]).then_inc(bias_moved, 16)
                sync.wait_ge(bias_moved, 48)

            @block.gpsimd
            def _(pool):
                nc.gpsimd.memset(ident[:, :], 0.0).then_inc(zeroed, 1)
                nc.gpsimd.memset(powhalf[:, :], 0.5)
                nc.gpsimd.memset(c["half"][:, :], -0.5)
                nc.gpsimd.memset(ones[:, :], 1.0)
                nc.gpsimd.memset(c["ones3"][:, :], 1.0)
                pool.wait_ge(zeroed, 1)
                nc.gpsimd.affine_select(out=ident[:, :], in_=ident[:, :], compare_op=ALU.not_equal, fill=1.0,
                                        base=0, pattern=[[-1, P]], channel_multiplier=1).then_inc(ident_ready, 1)
                pool.wait_ge(small_loaded, 16 * len(SMALL))
                nc.gpsimd.affine_select(out=c["causal"][:, :], in_=adj, compare_op=ALU.is_ge, fill=NEG,
                                        base=0, pattern=[[-1, P]], channel_multiplier=1).then_inc(masks_filled, 1)
                pool.wait_ge(eig_v, 2)
                nc.gpsimd.tensor_tensor(norm[:, :], stat[:, 0:1], powhalf[:, :], ALU.pow).then_inc(root_ready, 1)

            TRANSPOSES = [(adj, adjT[:, :]), (Wqkv[:, 0, :], wT[:, 0, :]), (Wqkv[:, 1, :], wT[:, 1, :]),
                          (Wqkv[:, 2, :], wT[:, 2, :]), (W1g[:, :], wT[:, 3, :])]

            @block.tensor
            def _(pe):
                pe.wait_ge(ident_ready, 1)
                pe.wait_ge(small_loaded, 16 * len(SMALL))
                for n, (src, _) in enumerate(TRANSPOSES):
                    t = nc.tensor.transpose(psum[n // 4][:, n % 4, :], src, ident[:, :])
                t.then_inc(products, 1)
                pe.wait_ge(v, 1)
                nc.tensor.transpose(psum[2][:, 0, 0:20], rows_a[:, :], ident[0:20, 0:20]).then_inc(products, 1)
                pe.wait_ge(lstm_loaded, 32)
                for n in range(2 * SKIPS):
                    kind, q = n // SKIPS, n % SKIPS
                    raw = (raw_ih, raw_hh)[kind]
                    if n >= 2:
                        pe.wait_ge(copied, n - 1)
                    for g in range(GATES):
                        t = nc.tensor.transpose(psum[3 + n % 2][:, g, :], raw[:, q * GATES + g, :], ident[:, :])
                    t.then_inc(products, 1)
                pe.wait_ge(v, 4)
                nc.tensor.matmul(psum[5][:, 0, :], wT[:, 0, :], wT[:, 1, :], start=True, stop=True)
                nc.tensor.matmul(psum[5][:, 1, :], wT[:, 2, :], Wo, start=True, stop=True)
                for j in range(2):
                    nc.tensor.matmul(psum[5][:, 2 + j, :], wT[:, 3, :], avec[:, j, :], start=True, stop=True)
                nc.tensor.matmul(psum[6][0:1, 0, :], ones[:, 0:1], adjT[:, :], start=True, stop=True) \
                    .then_inc(products, 1)
                pe.wait_ge(eig_v, 1)
                nc.tensor.matmul(psum[7][:, 0, 0:1], ones[:, :], sums[:, 0:1], start=True, stop=True).then_inc(eig_pe, 1)
                with pe.Fori(0, POWER_ROUNDS) as r:
                    pe.wait_ge(eig_v, r * 6 + 4)
                    nc.tensor.matmul(psum[7][:, 0, 0:1], ones[:, :], sums[:, 0:1], start=True, stop=True) \
                        .then_inc(eig_pe, 1)
                    for s in range(3):
                        pe.wait_ge(eig_v, r * 6 + 6 + s)
                        nc.tensor.matmul(psum[7][:, 1, :], power[:, :], power[:, :], start=True, stop=True) \
                            .then_inc(eig_pe, 1)
                e = POWER_ROUNDS * 6
                pe.wait_ge(eig_v, e + 4)
                nc.tensor.matmul(psum[7][:, 0, 0:1], ones[:, :], sums[:, 0:1], start=True, stop=True).then_inc(eig_pe, 1)
                pe.wait_ge(eig_v, e + 6)
                nc.tensor.matmul(psum[7][:, 1, :], sym[:, :], power[:, :], start=True, stop=True).then_inc(eig_pe, 1)
                pe.wait_ge(eig_v, e + 8)
                nc.tensor.matmul(psum[7][:, 0, 0:2], ones[:, :], sums[:, 0:2], start=True, stop=True).then_inc(eig_pe, 1)

            @block.vector
            def _(dve):
                vec = nc.vector
                vec.memset(rows_b[:, :], 0.0).then_inc(rows_zeroed, 1)
                dve.wait_ge(rows_loaded, 16 * len(ROWS))
                vec.tensor_tensor(rows_a[:, :], rows_a[:, :], rows_b[:, :], ALU.add).then_inc(v, 1)
                dve.wait_ge(products, 1)
                for n, (_, dst) in enumerate(TRANSPOSES):
                    t = vec.tensor_copy(dst, psum[n // 4][:, n % 4, :])
                t.then_inc(v, 1)
                dve.wait_ge(products, 2)
                vec.tensor_copy(c["cols"][:, :], psum[2][:, 0, 0:20]).then_inc(v, 1)
                dve.wait_ge(v, 3)
                for j in range(2):
                    t = vec.tensor_scalar(avec[:, j, :], ones[:, :], c["cols"][:, 18 + j:19 + j], None, ALU.mult)
                t.then_inc(v, 1)
                vec.tensor_tensor(sym[:, :], adj, adjT[:, :], ALU.add).then_inc(v, 1)
                dve.wait_ge(v, 5)
                vec.tensor_scalar(sym[:, :], sym[:, :], 0.5, None, ALU.mult).then_inc(v, 1)
                dve.wait_ge(v, 6)
                vec.tensor_tensor_reduce(scratch[:, :], sym[:, :], sym[:, :], 1.0, 0.0, ALU.mult, ALU.add,
                                         sums[:, 0:1]).then_inc(eig_v, 1)
                for n in range(2 * SKIPS):
                    kind, q = n // SKIPS, n % SKIPS
                    dve.wait_ge(products, 3 + n)
                    vec.tensor_copy(c["WT"][:, kind, q, :, :], psum[3 + n % 2][:, :, :]).then_inc(copied, 1)
                dve.wait_ge(products, 3 + 2 * SKIPS)
                vec.tensor_scalar(c["Gqk"][:, :], psum[5][:, 0, :], float(P) ** -0.5, None, ALU.mult)
                vec.tensor_scalar(c["Wx"][:, 1, :], c["Wx"][:, 1, :], float(HD) ** -0.5, None, ALU.mult)
                vec.tensor_copy(c["Gvo"][:, :], psum[5][:, 1, :])
                vec.tensor_copy(c["a1rep"][:, :], psum[5][:, 2, :])
                vec.tensor_copy(c["a2rep"][:, :], psum[5][:, 3, :])
                vec.tensor_copy(c["rowsum"][:, :], psum[6][0:1, 0, :])
                vec.tensor_copy(c["identb"][:, :], ident[:, :])
                vec.tensor_scalar(c["gat_mask"][:, :], adj, 0.0, NEG, ALU.is_equal, ALU.mult)
                vec.tensor_scalar(c["head_mask"][:, :], adj, 0.0, NEG3, ALU.is_le, ALU.mult)
                dve.wait_ge(small_loaded, 16 * len(SMALL))
                vec.tensor_copy(bpart[:, 0, :, :], brow[:, :, :]).then_inc(v, 1)
                dve.wait_ge(v, 7)
                vec.tensor_tensor(bres[:, :, :], brow[:, :, :], bpart[:, 0, :, :], ALU.subtract).then_inc(v, 1)
                dve.wait_ge(v, 8)
                vec.tensor_copy(bpart[:, 1, :, :], bres[:, :, :]).then_inc(v, 1)
                dve.wait_ge(v, 9)
                vec.tensor_tensor(bres[:, :, :], bres[:, :, :], bpart[:, 1, :, :], ALU.subtract).then_inc(v, 1)
                dve.wait_ge(v, 10)
                vec.tensor_copy(bpart[:, 2, :, :], bres[:, :, :]).then_inc(split_ready, 1)
                dve.wait_ge(eig_pe, 1)
                vec.tensor_scalar(stat[:, 0:1], psum[7][:, 0, 0:1], 1e-30, None, ALU.add).then_inc(eig_v, 1)
                dve.wait_ge(root_ready, 1)
                vec.reciprocal(stat[:, 1:2], norm[:, :]).then_inc(v, 1)
                dve.wait_ge(v, 11)
                vec.scalar_tensor_tensor(power[:, :], sym[:, :], stat[:, 1:2], ident[:, :], ALU.mult, ALU.add) \
                    .then_inc(eig_v, 1)

                def normalise(r):
                    dve.wait_ge(eig_v, r * 6 + 3)
                    vec.tensor_tensor(scratch[:, :], power[:, :], ident[:, :], ALU.mult).then_inc(v, 1)
                    dve.wait_ge(v, r + 12)
                    vec.reduce_sum(sums[:, 0:1], scratch[:, :], AX).then_inc(eig_v, 1)
                    dve.wait_ge(eig_pe, r * 4 + 2)
                    vec.reciprocal(stat[:, 2:3], psum[7][:, 0, 0:1]).then_inc(eig_v, 1)
                    dve.wait_ge(eig_v, r * 6 + 5)
                    vec.tensor_scalar(power[:, :], power[:, :], stat[:, 2:3], None, ALU.mult).then_inc(eig_v, 1)

                with dve.Fori(0, POWER_ROUNDS) as r:
                    normalise(r)
                    for s in range(3):
                        dve.wait_ge(eig_pe, r * 4 + 3 + s)
                        vec.tensor_copy(power[:, :], psum[7][:, 1, :]).then_inc(eig_v, 1)
                e, m = POWER_ROUNDS * 6, POWER_ROUNDS * 4
                normalise(POWER_ROUNDS)
                dve.wait_ge(eig_pe, m + 3)
                dve.wait_ge(eig_v, e + 6)
                vec.tensor_tensor_reduce(scratch[:, :], psum[7][:, 1, :], power[:, :], 1.0, 0.0, ALU.mult,
                                         ALU.add, sums[:, 0:1]).then_inc(eig_v, 1)
                dve.wait_ge(eig_v, e + 7)
                vec.tensor_tensor_reduce(scratch[:, :], power[:, :], power[:, :], 1.0, 0.0, ALU.mult,
                                         ALU.add, sums[:, 1:2]).then_inc(eig_v, 1)
                dve.wait_ge(eig_pe, m + 4)
                n = POWER_ROUNDS + 12
                vec.reciprocal(stat[:, 0:1], psum[7][:, 0, 1:2]).then_inc(v, 1)
                dve.wait_ge(v, n + 1)
                vec.tensor_scalar(stat[:, 1:2], psum[7][:, 0, 0:1], stat[:, 0:1], 1e-8, ALU.mult, ALU.add) \
                    .then_inc(v, 1)
                dve.wait_ge(v, n + 2)
                vec.reciprocal(stat[:, 2:3], stat[:, 1:2]).then_inc(v, 1)
                dve.wait_ge(v, n + 3)
                vec.tensor_scalar(stat[:, 3:4], stat[:, 2:3], 2.0, None, ALU.mult).then_inc(v, 1)
                dve.wait_ge(v, n + 4)
                vec.scalar_tensor_tensor(c["lapT"][:, :], adjT[:, :], stat[:, 3:4], ident[:, :], ALU.mult,
                                         ALU.subtract)


def attention_layer(nc, c, X, psum, NG, x):
    layer = 0 if x is not None else 1
    ctx = ExitStack()
    with ctx:
        def sb(name, shape, dt=F32):
            return ctx.enter_context(nc.sbuf_tensor(f"{name}_{layer}", shape, dt))

        sem = ctx.enter_context(phase_semaphores(nc, f"layer{layer}"))

        ring = [P, 2, GROUP, P]
        xin, xT, val, prob, probT, res = (sb(n, ring) for n in ("xin", "xT", "val", "prob", "probT", "res"))
        keyT = sb("keyT", ring) if layer == 0 else None
        score = sb("score", ring)
        top, total, inv = (sb(n, [P, 2, GROUP]) for n in ("top", "total", "inv"))
        st6, mv, rstd = sb("st6", [P, 2, GROUP, 6]), sb("mv", [P, 2, GROUP, 2]), sb("rstd", [P, 2, GROUP])
        var, shift = sb("var", [P, 2, 2, GROUP]), sb("shift", [P, 2, GROUP])

        loaded, staged = ([sem(f"{n}{b}") for b in range(2)] for n in ("loaded", "staged"))
        xT_done, xT_copied = sem("xT_done"), sem("xT_copied")
        key_done, key_copied, val_done, val_copied = sem("key_done"), sem("key_copied"), sem("val_done"), sem("val_copied")
        scores_done, scores_ready, top_ready = sem("scores_done"), sem("scores_ready"), sem("top_ready")
        probs_ready, probT_done, probT_copied = sem("probs_ready"), sem("probT_done"), sem("probT_copied")
        mixed, inv_ready, res_ready = sem("mixed"), sem("inv_ready"), sem("res_ready")
        st6_ready, stats_ready, var_ready = sem("st6_ready"), sem("stats_ready"), sem("var_ready")
        scale_ready, rstd_ready, normed_a, normed_v = sem("scale_ready"), sem("rstd_ready"), sem("normed_a"), sem("normed_v")
        b_xT, b_key, b_probT, b_mix = psum[0:4]
        b_val, b_score = psum[4:6], psum[6:8]
        small_slope = sem("small_slope")
        HEAD = 6
        ACT_TILES = 2

        with nc.Block() as block:
            @block.sync
            def _(sync):
                def step(i, u):
                    if live(i, NG):
                        if layer == 0:
                            after_nop(sync, loaded[u], landed(i, u))
                        after_nop(sync, xT_done, i - 1)
                        sync.dma_start(xin[:, u], batches(X, i)).then_inc(staged[u], 16)
                        if layer == 0 and (not isinstance(i, int) or i + 2 < NG):
                            load(i + 2, u)

                def load(g, b):
                    sync.dma_start(batches(X, g), x[bass.ds(g * GROUP, GROUP), :, :].rearrange("b t c -> t b c")) \
                        .then_inc(loaded[b], 16)

                if layer == 0:
                    load(0, 0)
                    load(1, 1)
                run_steps(sync, step, NG, 0, HEAD, NG - 2)

            @block.tensor
            def _(pe):
                def transpose_x(g, b):
                    after(pe, staged[b], landed(g, b))
                    after(pe, xT_copied, g)
                    for k in range(GROUP):
                        t = nc.tensor.transpose(b_xT[:, k, :], xin[:, b, k, :], c["ident"][:, :])
                    t.then_inc(xT_done, 1)

                def mix(g, b):
                    after(pe, probT_copied, g + 1)
                    after(pe, val_copied, g + 1)
                    after(pe, res_ready, g)
                    for k in range(GROUP):
                        t = nc.tensor.matmul(b_mix[:, k, :], probT[:, b, k, :], val[:, b, k, :], start=True, stop=True)
                    t.then_inc(mixed, 1)

                def keys(g, b):
                    after(pe, xT_copied, g + 1)
                    after(pe, key_copied, g)
                    nc.tensor.matmul(b_key[:, :, :], c["Gqk"][:, :], xT[:, b], start=True, stop=True) \
                        .then_inc(key_done, 1)

                def values(g, b):
                    after(pe, xT_copied, g + 1)
                    after(pe, val_copied, g - 1)
                    w = c["Gvo"] if layer == 0 else c["W1g"]
                    for k in range(GROUP):
                        t = nc.tensor.matmul(b_val[b][:, k, :], xT[:, b, k, :], w[:, :], start=True, stop=True)
                    t.then_inc(val_done, 1)

                def transpose_probs(g, b):
                    after(pe, probs_ready, g + 1)
                    after(pe, probT_copied, g)
                    for k in range(GROUP):
                        t = nc.tensor.transpose(b_probT[:, k, :], prob[:, b, k, :], c["ident"][:, :])
                    t.then_inc(probT_done, 1)

                def scores(g, b):
                    after(pe, scores_ready, g - 1)
                    if layer == 0:
                        after(pe, key_copied, g + 1)
                        for k in range(GROUP):
                            t = nc.tensor.matmul(b_score[b][:, k, :], keyT[:, b, k, :], xT[:, b, k, :],
                                                 start=True, stop=True)
                    else:
                        nc.tensor.matmul(b_score[b][:, :, :], c["identb"][:, :], over(c["gat_mask"][:, :]),
                                         start=True, stop=True)
                        nc.tensor.matmul(b_score[b][:, :, :], c["a2rep"][:, :], xT[:, b], start=False, stop=True, skip_group_check=True)
                        for k in range(GROUP):
                            t = nc.tensor.matmul(b_score[b][:, k, :], xT[:, b, k, :], c["a1rep"][:, :],
                                                 start=False, stop=True, skip_group_check=True)
                    t.then_inc(scores_done, 1)

                def step(i, u):
                    w = 1 - u
                    if live(i, NG):
                        transpose_x(i, u)
                    if live(i - 1, NG):
                        scores(i - 1, w)
                    if live(i - 3, NG):
                        mix(i - 3, w)
                    if live(i, NG):
                        if layer == 0:
                            keys(i, u)
                        values(i, u)
                    if live(i - 2, NG):
                        transpose_probs(i - 2, u)
                run_steps(pe, step, NG, 3, HEAD)

            @block.scalar
            def _(act):
                def copy_xT(g, b):
                    after(act, xT_done, g + 1)
                    after(act, scores_done, g - 1)
                    nc.scalar.activation(xT[:, b], b_xT[:, :, :], ACT.Copy).then_inc(xT_copied, 1)

                def exps(g, b):
                    after(act, top_ready, g + 1)
                    after(act, probT_done, g - 1)
                    after(act, inv_ready, g - 1)
                    for k in range(GROUP):
                        t = nc.scalar.activation(prob[:, b, k, :], score[:, b, k, :], ACT.Exp,
                                                 bias=top[:, b, k:k + 1], accum_out=total[:, b, k:k + 1])
                    t.then_inc(probs_ready, 1)

                def copy_values(g, b):
                    after(act, val_done, g + 1)
                    after(act, mixed, g - 1)
                    nc.scalar.activation(val[:, b], b_val[b][:, :, :], ACT.Copy).then_inc(val_copied, 1)

                def copy_probT(g, b):
                    after(act, probT_done, g + 1)
                    after(act, mixed, g - 1)
                    nc.scalar.activation(probT[:, b], b_probT[:, :, :], ACT.Copy).then_inc(probT_copied, 1)

                def small_slopes(g, b):
                    after(act, scores_done, g + 1)
                    after(act, probs_ready, g - 1)
                    nc.scalar.activation(score[:, b], b_score[b][:, :, :], ACT.Copy, scale=ALPHA) \
                        .then_inc(small_slope, 1)

                def copy_keys(g, b):
                    after(act, key_done, g + 1)
                    after(act, scores_done, g - 1)
                    nc.scalar.activation(keyT[:, b], b_key[:, :, :], ACT.Copy).then_inc(key_copied, 1)

                def normalise(g, b):
                    after(act, rstd_ready, g + 1)
                    for k in range(ACT_TILES):
                        t = nc.scalar.activation(
                            X[:, bass.ds(g * GROUP + k, 1), :].rearrange("p a c -> p (a c)"), res[:, b, k, :],
                            ACT.Identity, bias=shift[:, b, k:k + 1], scale=rstd[:, b, k:k + 1])
                    t.then_inc(normed_a, 1)

                def step(i, u):
                    w = 1 - u
                    if live(i - 3, NG):
                        copy_probT(i - 3, w)
                    if live(i, NG):
                        copy_xT(i, u)
                    if live(i - 2, NG):
                        exps(i - 2, u)
                    if live(i - 1, NG):
                        copy_values(i - 1, w)
                        if layer == 1:
                            small_slopes(i - 1, w)
                    if live(i, NG) and layer == 0:
                        copy_keys(i, u)
                    if live(i - 4, NG):
                        normalise(i - 4, u)
                run_steps(act, step, NG, 4, HEAD)

            @block.vector
            def _(dve):
                def biased(g, b):
                    after(dve, scores_done, g + 1)
                    after(dve, probs_ready, g - 1)
                    nc.vector.tensor_tensor(score[:, b], b_score[b][:, :, :], over(c["causal"][:, :]), ALU.add) \
                        .then_inc(scores_ready, 1)

                def row_max(g, b):
                    after(dve, scores_ready, g + 1)
                    after(dve, probs_ready, g - 1)
                    nc.vector.tensor_reduce(top[:, b, :], score[:, b], AX, ALU.max, negate=True).then_inc(top_ready, 1)

                def residual(g, b):
                    after(dve, probs_ready, g + 1)
                    nc.vector.reciprocal(inv[:, b, :], total[:, b, :]).then_inc(inv_ready, 1)
                    after(dve, inv_ready, g + 1)
                    after(dve, mixed, g + 1)
                    after(dve, normed_a, g - 1)
                    after(dve, normed_v, g - 1)
                    for k in range(GROUP):
                        t = nc.vector.scalar_tensor_tensor(
                            res[:, b, k, :], b_mix[:, k, :], inv[:, b, k:k + 1],
                            X[:, bass.ds(g * GROUP + k, 1), :].rearrange("p a c -> p (a c)"), ALU.mult, ALU.add)
                    t.then_inc(res_ready, 1)

                def leaky(g, b):
                    after(dve, small_slope, g + 1)
                    nc.vector.tensor_tensor(score[:, b], b_score[b][:, :, :], score[:, b], ALU.max) \
                        .then_inc(scores_ready, 1)

                def normalise(g, b):
                    after(dve, rstd_ready, g + 1)
                    for k in range(ACT_TILES, GROUP):
                        t = nc.vector.tensor_scalar(
                            X[:, bass.ds(g * GROUP + k, 1), :].rearrange("p a c -> p (a c)"), res[:, b, k, :],
                            rstd[:, b, k:k + 1], shift[:, b, k:k + 1], ALU.mult, ALU.add)
                    t.then_inc(normed_v, 1)

                def step(i, u):
                    w = 1 - u
                    if live(i - 3, NG):
                        residual(i - 3, w)
                        tile_stats(nc, dve, res[:, w], st6, w, i - 3, res_ready, st6_ready)
                    if live(i - 1, NG):
                        if layer == 0:
                            biased(i - 1, w)
                        else:
                            leaky(i - 1, w)
                    if live(i - 3, NG):
                        tile_moments(nc, dve, st6, mv, w, i - 3, st6_ready, var_ready, stats_ready)
                    if live(i - 1, NG):
                        row_max(i - 1, w)
                    if live(i - 4, NG):
                        normalise(i - 4, u)
                run_steps(dve, step, NG, 4, HEAD)

            @block.gpsimd
            def _(pool):
                def step(i, u):
                    layer_rstd(nc, pool, c, mv, var, rstd, shift, u, i, stats_ready, (normed_a, normed_v), var_ready,
                               scale_ready, rstd_ready)
                run_steps(pool, step, NG, 0, HEAD)


def tile_stats(nc, dve, tiles, st6, b, g, res_ready, st6_ready):
    if res_ready is not None:
        after(dve, res_ready, g + 1)
    for k in range(GROUP):
        t = nc.vector.bn_stats(st6[:, b, k, :], tiles[:, k, :])
    t.then_inc(st6_ready, 1)


def tile_moments(nc, dve, st6, mv, b, g, st6_ready, mv_free, stats_ready):
    after_nop(dve, mv_free, g - 1)
    after_nop(dve, st6_ready, g + 1)
    for k in range(GROUP):
        t = nc.vector.bn_aggr(mv[:, b, k, :], st6[:, b, k, :])
    t.then_inc(stats_ready, 1)


def layer_rstd(nc, pool, c, mv, var, rstd, shift, b, g, stats_ready, normed, var_ready, scale_ready, rstd_ready):
    after_nop(pool, stats_ready, g + 1)
    nc.gpsimd.tensor_scalar(var[:, b, 0, :], mv[:, b, :, 1], EPS, None, ALU.add)
    nc.gpsimd.tensor_scalar(var[:, b, 1, :], mv[:, b, :, 0], -1.0, None, ALU.mult).then_inc(var_ready, 1)
    for n in normed:
        after_nop(pool, n, g - 1)
    after_nop(pool, var_ready, g + 1)
    nc.gpsimd.tensor_tensor(rstd[:, b, :], var[:, b, 0, :], c["half"][:, :], ALU.pow).then_inc(scale_ready, 1)
    after(pool, scale_ready, g + 1)
    nc.gpsimd.tensor_tensor(shift[:, b, :], var[:, b, 1, :], rstd[:, b, :], ALU.mult).then_inc(rstd_ready, 1)


def gcn_layer(nc, c, X, H, psum, NG):
    ctx = ExitStack()
    with ctx:
        def sb(name):
            return ctx.enter_context(nc.sbuf_tensor(f"gcn_{name}", [P, 2, GROUP, P], F32))

        sem = ctx.enter_context(phase_semaphores(nc, "gcn"))

        xin, m1, h1, m2 = sb("xin"), sb("m1"), sb("h1"), sb("m2")
        staged = [sem(f"staged{b}") for b in range(2)]
        m1_done, m1_copied, h1_done, h1_ready = sem("m1_done"), sem("m1_copied"), sem("h1_done"), sem("h1_ready")
        m2_done, m2_copied, h2_done, h2_ready = sem("m2_done"), sem("m2_copied"), sem("h2_done"), sem("h2_ready")
        LAG, HEAD = 1, 4

        with nc.Block() as block:
            @block.sync
            def _(sync):
                def step(i, u):
                    after_nop(sync, m1_done, i - 1)
                    sync.dma_start(xin[:, u], batches(X, i)).then_inc(staged[u], 16)
                run_steps(sync, step, NG, 0, HEAD)

            @block.tensor
            def _(pe):
                def spread_x(g, b):
                    after(pe, staged[b], landed(g, b))
                    after(pe, m1_copied, g - 1)
                    for k in range(GROUP):
                        t = nc.tensor.matmul(psum[b][:, k, :], xin[:, b, k, :], c["adjT"][:, :], start=True, stop=True)
                    t.then_inc(m1_done, 1)

                def project_1(g, b):
                    after(pe, h1_ready, g - 1)
                    nc.tensor.matmul(psum[2 + b][:, :, :], c["rowsum"][:, :], over(c["bg"][:, 0, :]),
                                     start=True, stop=True)
                    after(pe, m1_copied, g + 1)
                    for k in range(GROUP):
                        t = nc.tensor.matmul(psum[2 + b][:, k, :], m1[:, b, k, :], c["Wg"][:, 0, :],
                                             start=False, stop=True, skip_group_check=True)
                    t.then_inc(h1_done, 1)

                def spread_h(g, b):
                    after(pe, h1_ready, g + 1)
                    after(pe, m2_copied, g - 1)
                    for k in range(GROUP):
                        t = nc.tensor.matmul(psum[4 + b][:, k, :], h1[:, b, k, :], c["adjT"][:, :],
                                             start=True, stop=True)
                    t.then_inc(m2_done, 1)

                def project_2(g, b):
                    after(pe, h2_ready, g - 1)
                    nc.tensor.matmul(psum[6 + b][:, :, :], c["bg"][:, 1, :], over(c["rowsum"][:, :]),
                                     start=True, stop=False)
                    after(pe, m2_copied, g + 1)
                    nc.tensor.matmul(psum[6 + b][:, :, :], c["Wg"][:, 1, :], m2[:, b], start=False, stop=True) \
                        .then_inc(h2_done, 1)

                def step(i, u):
                    if live(i, NG):
                        spread_x(i, u)
                    if live(i - 1, NG):
                        spread_h(i - 1, 1 - u)
                    if live(i, NG):
                        project_1(i, u)
                    if live(i - 1, NG):
                        project_2(i - 1, 1 - u)
                run_steps(pe, step, NG, LAG, HEAD)

            @block.scalar
            def _(act):
                def step(i, u):
                    if live(i, NG):
                        after(act, m1_done, i + 1)
                        after(act, h1_done, i - 1)
                        nc.scalar.activation(m1[:, u], psum[u][:, :, :], ACT.Copy).then_inc(m1_copied, 1)
                    if live(i - 1, NG):
                        after(act, h2_done, i)
                        nc.scalar.activation(batches(H, i - 1), psum[7 - u][:, :, :], ACT.Relu).then_inc(h2_ready, 1)
                run_steps(act, step, NG, LAG, HEAD)

            @block.vector
            def _(dve):
                def step(i, u):
                    if live(i - 1, NG):
                        after(dve, m2_done, i)
                        after(dve, h2_done, i - 2)
                        nc.vector.tensor_copy(m2[:, 1 - u], psum[5 - u][:, :, :]).then_inc(m2_copied, 1)
                    if live(i, NG):
                        after(dve, h1_done, i + 1)
                        after(dve, m2_done, i - 1)
                        nc.vector.tensor_scalar(h1[:, u], psum[2 + u][:, :, :], 0.0, None, ALU.max) \
                            .then_inc(h1_ready, 1)
                run_steps(dve, step, NG, LAG, HEAD)


def lstm_pass(nc, c, H, psum, B, p):
    nb = {1: 4, 2: 8, 3: 8, 4: 16}[p]
    nw = P // p
    cols = nb * nw
    pairs = B // nb // 2
    I, F, G, O = range(GATES)
    gates = [[I, G, O]] + [[I, G, F, O]] * (p - 1)
    per_chunk = sum(len(g) for g in gates)
    q = p - 1
    ctx = ExitStack()
    with ctx:
        def sb(name):
            return ctx.enter_context(nc.sbuf_tensor(f"lstm{p}_{name}", [P, 2, nb, nw], F32))

        sem = ctx.enter_context(phase_semaphores(nc, f"lstm{p}"))

        def sems(name):
            return [sem(f"{name}{b}") for b in range(2)]

        gate = [sb(f"gate{g}") for g in range(GATES)]
        cell, kept, tanh_c, hidden = sb("cell"), sb("kept"), sb("tanh_c"), sb("hidden")
        gate_done, gate_ready, fresh_ready, kept_ready = sems("gate_done"), sems("gate_ready"), sems("fresh"), sems("kept")
        cell_ready, tanh_ready, hidden_ready = sems("cell"), sems("tanh"), sems("hidden")

        def bank(b, g):
            return flat(psum[4 * b + g])[:, 0:cols].rearrange("p (b w) -> p b w", b=nb)

        def tokens(j, b, t):
            return H[:, bass.ds((j * 2 + b) * nb, nb), t:t + (nw - 1) * p + 1:p]

        def gates_before(j, t):
            return j * per_chunk + sum(len(g) for g in gates[:t])

        cells = [(t, b) for t in range(p) for b in range(2)]

        def run_pairs(eng, head, tail=None):
            def body(j, first):
                for n, (t, b) in enumerate(cells):
                    head(j, t, b)
                    if tail is not None and (n or not first):
                        tail(*((j, *cells[n - 1]) if n else (j - 1, *cells[-1])))
            body(0, True)
            with eng.Fori(1, pairs) as j:
                body(j, False)
            if tail is not None:
                tail(pairs - 1, *cells[-1])

        with nc.Block() as block:
            @block.tensor
            def _(pe):
                def products(j, t, b):
                    after(pe, gate_ready[b], gates_before(j, t))
                    for g in gates[t]:
                        m = nc.tensor.matmul(bank(b, g), c["WT"][:, 0, q, g, :], tokens(j, b, t),
                                             start=True, stop=(t == 0))
                        if t == 0:
                            m.then_inc(gate_done[b], 1)
                    if t:
                        after(pe, hidden_ready[b], j * p + t)
                        for g in gates[t]:
                            nc.tensor.matmul(bank(b, g), c["WT"][:, 1, q, g, :], hidden[:, b],
                                             start=False, stop=True).then_inc(gate_done[b], 1)
                run_pairs(pe, products)

            @block.scalar
            def _(act):
                def gate_functions(j, t, b):
                    after(act, hidden_ready[b], j * p + t)
                    for n, g in enumerate(gates[t]):
                        after(act, gate_done[b], gates_before(j, t) + n + 1)
                        nc.scalar.activation(gate[g][:, b], bank(b, g), ACT.Tanh if g == G else ACT.Sigmoid,
                                             bias=c["cols"][:, q * GATES + g:q * GATES + g + 1]) \
                            .then_inc(gate_ready[b], 1)

                def tanh_cell(j, t, b):
                    after(act, cell_ready[b], j * p + t + 1)
                    nc.scalar.activation(tanh_c[:, b], cell[:, b], ACT.Tanh).then_inc(tanh_ready[b], 1)
                run_pairs(act, gate_functions, tanh_cell)

            @block.vector
            def _(dve):
                def update_cell(j, t, b):
                    if t == 0:
                        after(dve, tanh_ready[b], j * p)
                        after(dve, gate_ready[b], gates_before(j, t) + 2)
                        nc.vector.tensor_tensor(cell[:, b], gate[I][:, b], gate[G][:, b], ALU.mult) \
                            .then_inc(cell_ready[b], 1)
                        return
                    after(dve, gate_ready[b], gates_before(j, t) + 2)
                    nc.vector.tensor_tensor(gate[G][:, b], gate[I][:, b], gate[G][:, b], ALU.mult) \
                        .then_inc(fresh_ready[b], 1)
                    after(dve, gate_ready[b], gates_before(j, t) + 3)
                    after(dve, cell_ready[b], j * p + t)
                    nc.vector.tensor_tensor(kept[:, b], gate[F][:, b], cell[:, b], ALU.mult) \
                        .then_inc(kept_ready[b], 1)
                    after(dve, fresh_ready[b], j * (p - 1) + t)
                    after(dve, kept_ready[b], j * (p - 1) + t)
                    nc.vector.tensor_tensor(cell[:, b], kept[:, b], gate[G][:, b], ALU.add) \
                        .then_inc(cell_ready[b], 1)

                def update_hidden(j, t, b):
                    after(dve, tanh_ready[b], j * p + t + 1)
                    after(dve, gate_ready[b], gates_before(j, t + 1))
                    dst = hidden[:, b] if t < p - 1 else tokens(j, b, t)
                    nc.vector.tensor_tensor(dst, gate[O][:, b], tanh_c[:, b], ALU.mult).then_inc(hidden_ready[b], 1)
                run_pairs(dve, update_cell, update_hidden)


def transformer_attention(nc, c, X, H, psum, NG):
    ctx = ExitStack()
    with ctx:
        def sb(name, shape, dt=F32):
            return ctx.enter_context(nc.sbuf_tensor(f"tr_{name}", shape, dt))

        sem = ctx.enter_context(phase_semaphores(nc, "tr"))

        tile, ring = [P, GROUP, P], [P, 2, GROUP, P]
        hin, x3, val = sb("hin", ring), sb("x3", ring), sb("val", ring)
        res0, m1, hidden, x1, x1T, qT, kT = (sb(n, tile) for n in ("res0", "m1", "hidden", "x1", "x1T", "qT", "kT"))
        prob, probT = sb("prob", [P, HEADS, GROUP, P]), sb("probT", [P, HEADS, GROUP, P])
        mixed, mixedT, res2, x2 = (sb(n, tile) for n in ("mixed", "mixedT", "res2", "x2"))
        top, total, inv = (sb(n, [P, HEADS, GROUP]) for n in ("top", "total", "inv"))
        norms = [(sb(f"st6_{n}", [P, 1, GROUP, 6]), sb(f"mv_{n}", [P, 1, GROUP, 2]), sb(f"var_{n}", [P, GROUP]),
                  sb(f"rstd_{n}", [P, GROUP])) for n in range(3)]
        norm_sems = [tuple(sem(f"{s}_{n}") for s in ("st6_ready", "stats_ready", "var_ready", "rstd_ready", "normed"))
                     for n in range(3)]
        hin_staged, x3_stored, x1_stored, x2_stored = ([sem(f"{n}{b}") for b in range(2)] for n in
                                                       ("hin_staged", "x3_stored", "x1_stored", "x2_stored"))
        h_turned, res0_ready, m1_done, m1_copied, h_done = (
            sem(n) for n in ("h_turned", "res0_ready", "m1_done", "m1_copied", "h_done"))
        affine, x1_ready, x1_turned, x1T_copied = (
            sem(n) for n in ("affine", "x1_ready", "x1_turned", "x1T_copied"))
        q_done, q_copied, k_done, k_copied, v_done, v_copied = (
            sem(n) for n in ("q_done", "q_copied", "k_done", "k_copied", "v_done", "v_copied"))
        scores_done, top_ready, probs_ready, inv_ready = (
            sem(n) for n in ("scores_done", "top_ready", "probs_ready", "inv_ready"))
        p_turned, pT_copied_a, pT_copied_v, mix_done, mix_ready = (
            sem(n) for n in ("p_turned", "pT_copied_a", "pT_copied_v", "mix_done", "mix_ready"))
        mix_turned, mixT_copied, o_done, res2_ready, scaled2, x2_ready = (
            sem(n) for n in ("mix_turned", "mixT_copied", "o_done", "res2_ready", "scaled2", "x2_ready"))
        Wc, Wq, Wk, Wv, Wo = (c["Wx"][:, j, :] for j in range(5))
        g1, be1, g2, be2 = (c["rep"][:, j, :] for j in range(4))
        b_x1T, b_hT, b_o, b_q, b_k, b_m1, b_v, b_h, b_mix, b_mixT = (
            psum[n] for n in (4, 5, 6, 7, 4, 5, 6, 7, 5, 6))
        b_pT = [psum[n] for n in (4, 5, 6, 4)]
        LAG, HEAD = 3, 6

        def up_to(n):
            return min(n, NG) if isinstance(n, int) else n

        with nc.Block() as block:
            @block.sync
            def _(sync):
                def step(i, u):
                    if live(i, NG):
                        after_nop(sync, h_turned, i - 1)
                        sync.dma_start(hin[:, u], batches(H, i)).then_inc(hin_staged[u], 16)
                    if live(i - 1, NG):
                        after_nop(sync, norm_sems[0][4], i)
                        sync.dma_start(batches(X, i - 1), x3[:, 1 - u]).then_inc(x3_stored[1 - u], 16)
                    if live(i - 2, NG):
                        after_nop(sync, x1_ready, i - 1)
                        sync.dma_start(batches(H, i - 2), x1[:, :, :]).then_inc(x1_stored[u], 16)
                    if live(i - 5, NG):
                        after_nop(sync, x2_ready, i - 4)
                        sync.dma_start(batches(H, i - 5), x2[:, :, :]).then_inc(x2_stored[1 - u], 16)
                run_steps(sync, step, NG, 5, HEAD)
                for b in range(2):
                    sync.wait_ge(x3_stored[b], landed(NG - 2 + b, b))
                    sync.wait_ge(x2_stored[b], landed(NG - 2 + b, b))

            @block.tensor
            def _(pe):
                def bias_rows(bank, j):
                    nc.tensor.matmul(bank[:, :, :], c["ones3"][:, :], over(c["bias3"][:, j, :]), start=True, stop=True)

                def turn_x1(g):
                    after(pe, x1_ready, g + 1)
                    after(pe, k_copied, g)
                    after(pe, pT_copied_a, (g - 1) * 2)
                    for k in range(GROUP):
                        t = nc.tensor.transpose(b_x1T[:, k, :], x1[:, k, :], c["ident"][:, :])
                    t.then_inc(x1_turned, 1)

                def turn_h(g, b):
                    after(pe, hin_staged[b], landed(g, b))
                    after(pe, mix_ready, g - 3)
                    after(pe, m1_copied, g - 1)
                    after(pe, res0_ready, g)
                    for k in range(GROUP):
                        t = nc.tensor.transpose(b_hT[:, k, :], hin[:, b, k, :], c["ident"][:, :])
                    t.then_inc(h_turned, 1)

                def project_out(g):
                    after(pe, mixT_copied, g + 1)
                    bias_rows(b_o, 1)
                    for k in range(GROUP):
                        t = nc.tensor.matmul(b_o[:, k, :], mixedT[:, k, :], Wo, start=False, stop=True, skip_group_check=True)
                    t.then_inc(o_done, 1)

                def queries(g):
                    after(pe, x1T_copied, g + 1)
                    after(pe, norm_sems[1][4], g + 1)
                    nc.tensor.matmul(b_q[:, :, :], Wq, x1T[:, :, :], start=True, stop=True).then_inc(q_done, 1)

                def keys(g):
                    nc.tensor.matmul(b_k[:, :, :], Wk, x1T[:, :, :], start=True, stop=True).then_inc(k_done, 1)

                def spread_x(g, b):
                    after(pe, norm_sems[0][4], g + 1)
                    after(pe, res0_ready, up_to(g + 2))
                    after(pe, mix_ready, g - 2)
                    for k in range(GROUP):
                        t = nc.tensor.matmul(b_m1[:, k, :], x3[:, b, k, :], c["lapT"][:, :], start=True, stop=True)
                    t.then_inc(m1_done, 1)

                def values(g):
                    after(pe, res2_ready, g - 1)
                    after(pe, v_copied, g)
                    for k in range(GROUP):
                        t = nc.tensor.matmul(b_v[:, k, :], x1T[:, k, :], Wv, start=True, stop=True)
                    t.then_inc(v_done, 1)

                def project_h(g):
                    after(pe, q_copied, g)
                    bias_rows(b_h, 0)
                    after(pe, m1_copied, g + 1)
                    for k in range(GROUP):
                        t = nc.tensor.matmul(b_h[:, k, :], m1[:, k, :], Wc, start=False, stop=True, skip_group_check=True)
                    t.then_inc(h_done, 1)

                def turn_probs(g, h):
                    after(pe, probs_ready, g * HEADS + h + 1)
                    if h == 0:
                        after(pe, k_copied, up_to(g + 2))
                        after(pe, pT_copied_a, g * 2)
                    if h == 1:
                        after(pe, m1_copied, up_to(g + 3))
                        after(pe, mix_ready, g)
                    if h == 2:
                        after(pe, v_copied, up_to(g + 2))
                        after(pe, res2_ready, g)
                    if h == 3:
                        after(pe, pT_copied_v, g * 2 + 1)
                    for k in range(GROUP):
                        t = nc.tensor.transpose(b_pT[h][:, k, :], prob[:, h, k, :], c["ident"][:, :])
                    t.then_inc(p_turned, 1)

                def mask(g, h):
                    after(pe, probs_ready, (g - 1) * HEADS + h + 1)
                    nc.tensor.matmul(psum[h][:, :, :], c["identb"][:, :], over(c["head_mask"][:, :]),
                                     start=True, stop=True)

                def mix(g, b):
                    after(pe, pT_copied_a, g * 2 + 2)
                    after(pe, pT_copied_v, g * 2 + 2)
                    for k in range(GROUP):
                        for h in range(HEADS):
                            a = k * P + h * HD
                            cols = slice(a, min(a + WIDE, GROUP * P))
                            t = nc.tensor.matmul(flat(b_mix)[:, cols], probT[:, h, k, :], flat(val[:, b])[:, cols],
                                                 start=True, stop=True)
                    t.then_inc(mix_done, 1)

                def scores(g, pair):
                    after(pe, q_copied, g + 1)
                    after(pe, k_copied, g + 1)
                    for k in range(GROUP):
                        for h in (2 * pair, 2 * pair + 1):
                            rows = slice(h * HD, (h + 1) * HD)
                            t = nc.tensor.matmul(psum[h][:, k, :], qT[rows, k, :], kT[rows, k, :],
                                                 start=False, stop=True, skip_group_check=True)
                    t.then_inc(scores_done, 1)

                def turn_mixed(g):
                    after(pe, mix_ready, g + 1)
                    for k in range(GROUP):
                        t = nc.tensor.transpose(b_mixT[:, k, :], mixed[:, k, :], c["ident"][:, :])
                    t.then_inc(mix_turned, 1)

                def step(i, u):
                    if live(i - 2, NG):
                        turn_x1(i - 2)
                    if live(i, NG):
                        turn_h(i, u)
                    if live(i - 4, NG):
                        project_out(i - 4)
                    if live(i - 2, NG):
                        queries(i - 2)
                        keys(i - 2)
                    if live(i - 1, NG):
                        spread_x(i - 1, 1 - u)
                    if live(i - 2, NG):
                        values(i - 2)
                    for h in range(HEADS):
                        if h == 3 and live(i - 2, NG):
                            scores(i - 2, 0)
                        if live(i - 3, NG):
                            turn_probs(i - 3, h)
                        if live(i - 2, NG):
                            mask(i - 2, h)
                    if live(i - 1, NG):
                        project_h(i - 1)
                    if live(i - 3, NG):
                        mix(i - 3, 1 - u)
                    if live(i - 2, NG):
                        scores(i - 2, 1)
                    if live(i - 3, NG):
                        turn_mixed(i - 3)
                run_steps(pe, step, NG, LAG + 1, HEAD)

            @block.scalar
            def _(act):
                def copy(bank, dst, done, n, copied):
                    after(act, done, n)
                    nc.scalar.activation(dst, bank[:, :, :], ACT.Copy).then_inc(copied, 1)

                def exps(g, h):
                    after(act, top_ready, g * HEADS + h + 1)
                    after(act, p_turned, (g - 1) * HEADS + h + 1)
                    if h == 0:
                        after(act, inv_ready, g)
                    for k in range(GROUP):
                        t = nc.scalar.activation(prob[:, h, k, :], psum[h][:, k, :], ACT.Exp,
                                                 bias=top[:, h, k:k + 1], accum_out=total[:, h, k:k + 1])
                    t.then_inc(probs_ready, 1)

                def step(i, u):
                    g2, g3 = i - 2, i - 3
                    if live(g2, NG):
                        after(act, v_done, g2)
                        copy(b_x1T, x1T[:, :, :], x1_turned, g2 + 1, x1T_copied)
                    if live(g3, NG):
                        exps(g3, 2)
                    if live(g2, NG):
                        copy(b_q, qT[:, :, :], q_done, g2 + 1, q_copied)
                        copy(b_k, kT[:, :, :], k_done, g2 + 1, k_copied)
                    if live(i - 1, NG):
                        after(act, h_done, i - 1)
                        copy(b_m1, m1[:, :, :], m1_done, i, m1_copied)
                    if live(g3, NG):
                        exps(g3, 3)
                    if live(g2, NG):
                        after(act, mix_done, g2 - 1)
                        copy(b_v, val[:, u], v_done, g2 + 1, v_copied)
                    if live(g3, NG):
                        after(act, mix_done, g3)
                        copy(b_pT[2], probT[:, 2], p_turned, g3 * HEADS + 3, pT_copied_a)
                        copy(b_pT[3], probT[:, 3], p_turned, g3 * HEADS + 4, pT_copied_a)
                    if live(g2, NG):
                        exps(g2, 0)
                        exps(g2, 1)
                    if live(g3, NG):
                        after(act, o_done, g3)
                        copy(b_mixT, mixedT[:, :, :], mix_turned, g3 + 1, mixT_copied)
                run_steps(act, step, NG, LAG, HEAD)

            @block.vector
            def _(dve):
                def stats(n, tiles, g, ready):
                    tile_stats(nc, dve, tiles, norms[n][0], 0, g, ready, norm_sems[n][0])

                def moments(n, g):
                    tile_moments(nc, dve, norms[n][0], norms[n][1], 0, g, norm_sems[n][0], norm_sems[n][4],
                                 norm_sems[n][1])

                def normalise(n, dst, src, g):
                    after(dve, norm_sems[n][3], g + 1)
                    for k in range(GROUP):
                        t = nc.vector.tensor_scalar(dst[:, k, :], src[:, k, :], norms[n][1][:, 0, k, 0:1],
                                                    norms[n][3][:, k:k + 1], ALU.subtract, ALU.mult)
                    t.then_inc(norm_sems[n][4], 1)

                def row_max(g, h):
                    if h % 2 == 0:
                        after(dve, scores_done, g * 2 + h // 2 + 1)
                    nc.vector.tensor_reduce(top[:, h, :], psum[h][:, :, :], AX, ALU.max, negate=True) \
                        .then_inc(top_ready, 1)

                def residual_0(g):
                    after(dve, h_turned, g + 1)
                    after(dve, norm_sems[0][4], g)
                    nc.vector.tensor_tensor(res0[:, :, :], b_hT[:, :, :], batches(X, g), ALU.add).then_inc(res0_ready, 1)

                def residual_2(g, b):
                    after(dve, o_done, g + 1)
                    after_nop(dve, x1_stored[b], landed(g, b))
                    after(dve, scaled2, g)
                    nc.vector.tensor_tensor(res2[:, :, :], b_o[:, :, :], batches(H, g), ALU.add).then_inc(res2_ready, 1)

                def copy_probT(g, h):
                    if h == 0:
                        after(dve, mix_done, g)
                    after(dve, p_turned, g * HEADS + h + 1)
                    nc.vector.tensor_copy(probT[:, h], b_pT[h][:, :, :]).then_inc(pT_copied_v, 1)

                def invert(g):
                    after(dve, probs_ready, (g + 1) * HEADS)
                    nc.vector.reciprocal(inv[:, :, :], total[:, :, :]).then_inc(inv_ready, 1)

                def weigh_mixed(g):
                    after(dve, inv_ready, g + 1)
                    after(dve, mix_done, g + 1)
                    after(dve, mix_turned, g)
                    nc.vector.tensor_tensor(
                        mixed[:, :, :].rearrange("p k (h d) -> p k h d", h=HEADS),
                        b_mix[:, :, :].rearrange("p k (h d) -> p k h d", h=HEADS),
                        inv[:, :, :].rearrange("p h k -> p k h").unsqueeze(3).broadcast_to([P, GROUP, HEADS, HD]),
                        ALU.mult).then_inc(mix_ready, 1)

                def scale_hidden(g):
                    after(dve, x1_ready, g)
                    after(dve, norm_sems[1][1], g + 1)
                    for k in range(GROUP):
                        t = nc.vector.scalar_tensor_tensor(hidden[:, k, :], b_h[:, k, :], norms[1][1][:, 0, k, 0:1],
                                                           g1, ALU.subtract, ALU.mult)
                    t.then_inc(norm_sems[1][4], 1)

                def shift_hidden(g):
                    after(dve, norm_sems[1][4], g + 1)
                    after(dve, norm_sems[1][3], g + 1)
                    for k in range(GROUP):
                        t = nc.vector.scalar_tensor_tensor(hidden[:, k, :], hidden[:, k, :], norms[1][3][:, k:k + 1],
                                                           be1, ALU.mult, ALU.add)
                    t.then_inc(affine, 1)

                def step(i, u):
                    h, g2, g3, g4 = i - 1, i - 2, i - 3, i - 4
                    if live(g3, NG):
                        row_max(g3, 2)
                    if live(i, NG):
                        residual_0(i)
                    if live(g3, NG):
                        row_max(g3, 3)
                    if live(g4, NG):
                        residual_2(g4, u)
                    if live(i, NG):
                        stats(0, res0, i, res0_ready)
                    if live(g4, NG):
                        stats(2, res2, g4, res2_ready)
                    if live(i, NG):
                        moments(0, i)
                    if live(g4, NG):
                        moments(2, g4)
                    if live(i, NG):
                        after(dve, x1_ready, i - 1)
                        after_nop(dve, x3_stored[u], landed(i - 2, u))
                        after(dve, m1_done, i - 1)
                        normalise(0, x3[:, u], res0, i)
                    if live(g3, NG):
                        copy_probT(g3, 0)
                        copy_probT(g3, 1)
                        invert(g3)
                    if live(g4, NG):
                        normalise(2, res2, res2, g4)
                    if live(g2, NG):
                        row_max(g2, 0)
                        row_max(g2, 1)
                    if live(h, NG):
                        stats(1, b_h, h, h_done)
                        moments(1, h)
                        scale_hidden(h)
                    if live(g3, NG):
                        weigh_mixed(g3)
                    if live(h, NG):
                        shift_hidden(h)
                        after(dve, affine, i)
                        after(dve, x1_turned, h)
                        after_nop(dve, x1_stored[u], landed(i - 2, u))
                        nc.vector.scalar_tensor_tensor(flat(x1), flat(hidden), 0.0, flat(x3[:, 1 - u]), ALU.max, ALU.add) \
                            .then_inc(x1_ready, 1)
                run_steps(dve, step, NG, LAG + 1, HEAD)

            @block.gpsimd
            def _(pool):
                def rstd(n, g):
                    st6_ready, stats_ready, var_ready, rstd_ready, normed = norm_sems[n]
                    mv, var, rs = norms[n][1:]
                    after_nop(pool, stats_ready, g + 1)
                    nc.gpsimd.tensor_scalar(var[:, :], mv[:, 0, :, 1], EPS, None, ALU.add).then_inc(var_ready, 1)
                    after_nop(pool, var_ready, g + 1)
                    nc.gpsimd.tensor_tensor(rs[:, :], var[:, :], c["half"][:, :], ALU.pow).then_inc(rstd_ready, 1)

                def step(i, u):
                    if live(i, NG):
                        rstd(0, i)
                    if live(i - 4, NG):
                        rstd(2, i - 4)
                    if live(i - 1, NG):
                        rstd(1, i - 1)
                    if live(i - 4, NG):
                        after(pool, norm_sems[2][4], i - 3)
                        after(pool, x2_stored[1 - u], landed(i - 5, 1 - u))
                        nc.gpsimd.tensor_tensor(x2[:, :, :], res2[:, :, :], over(g2), ALU.mult).then_inc(scaled2, 1)
                        after(pool, scaled2, i - 3)
                        nc.gpsimd.tensor_tensor(x2[:, :, :], x2[:, :, :], over(be2), ALU.add).then_inc(x2_ready, 1)
                run_steps(pool, step, NG, LAG + 1, HEAD)


def transformer_mlp(nc, c, X, H, psum, NG, out):
    ctx = ExitStack()
    with ctx:
        def sb(name, shape, dt=F32):
            return ctx.enter_context(nc.sbuf_tensor(f"mlp_{name}", shape, dt))

        sem = ctx.enter_context(phase_semaphores(nc, "mlp"))

        ring = [P, 2, GROUP, P]
        x2, x2T, res3, part, skip, res4, done = (sb(n, ring) for n in
                                                ("x2", "x2T", "res3", "part", "skip", "res4", "done"))
        act_h = sb("act_h", [P, 2, 2, GROUP, P])
        norms = [(sb(f"st6_{n}", [P, 2, GROUP, 6]), sb(f"mv_{n}", [P, 2, GROUP, 2]), sb(f"var_{n}", [P, 2, 2, GROUP]),
                  sb(f"rstd_{n}", [P, 2, GROUP]), sb(f"shift_{n}", [P, 2, GROUP])) for n in range(2)]
        norm_sems = [tuple(sem(f"{s}_{n}") for s in ("st6_ready", "stats_ready", "var_ready", "rstd_ready", "normed", "scale_ready"))
                     for n in range(2)]
        staged, stored = ([sem(f"{n}{b}") for b in range(2)] for n in ("staged", "stored"))
        turned, turned_copied, up_done, gelu_ready, down_done = (
            sem(n) for n in ("turned", "turned_copied", "up_done", "gelu_ready", "down_done"))
        res3_ready, scaled, skip_ready, res4_ready = (sem(n) for n in ("res3_ready", "scaled", "skip_ready", "res4_ready"))
        g3, be3 = c["rep"][:, 4, :], c["rep"][:, 5, :]
        HEAD = 8

        with nc.Block() as block:
            @block.sync
            def _(sync):
                def step(i, u):
                    if live(i, NG):
                        after_nop(sync, turned, i - 1)
                        sync.dma_start(x2[:, u], batches(H, i)).then_inc(staged[u], 16)
                    if live(i - 8, NG):
                        after_nop(sync, norm_sems[1][4], i - 7)
                        sync.dma_start(out[bass.ds((i - 8) * GROUP, GROUP), :, :].rearrange("b t c -> t b c"),
                                       done[:, u]).then_inc(stored[u], 16)
                run_steps(sync, step, NG, 8, HEAD)
                for b in range(2):
                    sync.wait_ge(stored[b], landed(NG - 2 + b, b))

            @block.tensor
            def _(pe):
                def turn(g, b):
                    after(pe, staged[b], landed(g, b))
                    after(pe, turned_copied, g)
                    for k in range(GROUP):
                        t = nc.tensor.transpose(psum[0][:, k, :], x2[:, b, k, :], c["ident"][:, :])
                    t.then_inc(turned, 1)

                def up(g, b):
                    after(pe, turned_copied, g + 1)
                    after(pe, gelu_ready, g * 2 - 2)
                    for j in range(2):
                        nc.tensor.matmul(psum[1 + 2 * b + j][:, :, :], c["W1"][:, j * P:(j + 1) * P], x2T[:, b],
                                         start=True, stop=True).then_inc(up_done, 1)

                def down(g, b):
                    after(pe, res3_ready, g - 1)
                    nc.tensor.matmul(psum[5 + b][:, :, :], c["ones3"][:, :], over(c["bias3"][:, 2, :]),
                                     start=True, stop=True)
                    after(pe, gelu_ready, g * 2 + 2)
                    for k in range(GROUP):
                        for j in range(2):
                            t = nc.tensor.matmul(psum[5 + b][:, k, :], act_h[:, b, j, k, :], c["W2"][:, j, :],
                                                 start=False, stop=(j == 1), skip_group_check=True)
                    t.then_inc(down_done, 1)

                def step(i, u):
                    if live(i, NG):
                        turn(i, u)
                    if live(i - 1, NG):
                        up(i - 1, 1 - u)
                    if live(i - 2, NG):
                        down(i - 2, u)
                run_steps(pe, step, NG, 2, HEAD)

            @block.scalar
            def _(act):
                def gelu(g, b):
                    after(act, down_done, g - 1)
                    for j in range(2):
                        after(act, up_done, g * 2 + j + 1)
                        nc.scalar.activation(act_h[:, b, j], psum[1 + 2 * b + j][:, :, :], ACT.Gelu,
                                             bias=c["cols"][:, 16 + j:17 + j]).then_inc(gelu_ready, 1)

                def normalise(n, dst, src, g, b):
                    after(act, norm_sems[n][3], g + 1)
                    for k in range(GROUP):
                        t = nc.scalar.activation(dst[:, k, :], src[:, k, :], ACT.Identity,
                                                 bias=norms[n][4][:, b, k:k + 1], scale=norms[n][3][:, b, k:k + 1])
                    t.then_inc(norm_sems[n][4], 1)

                def step(i, u):
                    if live(i, NG):
                        after(act, turned, i + 1)
                        after(act, up_done, i * 2 - 2)
                        nc.scalar.activation(x2T[:, u], psum[0][:, :, :], ACT.Copy).then_inc(turned_copied, 1)
                    if live(i - 4, NG):
                        after(act, res4_ready, i - 5)
                        normalise(0, part[:, u], res3[:, u], i - 4, u)
                    if live(i - 1, NG):
                        gelu(i - 1, 1 - u)
                    if live(i - 6, NG):
                        after_nop(act, stored[u], landed(i - 8, u))
                        normalise(1, done[:, u], res4[:, u], i - 6, u)
                run_steps(act, step, NG, 6, HEAD)

            @block.vector
            def _(dve):
                def stats(n, tiles, g, b, ready):
                    tile_stats(nc, dve, tiles, norms[n][0], b, g, ready, norm_sems[n][0])

                def moments(n, g, b):
                    tile_moments(nc, dve, norms[n][0], norms[n][1], b, g, norm_sems[n][0], norm_sems[n][2],
                                 norm_sems[n][1])

                def step(i, u):
                    w = 1 - u
                    if live(i - 5, NG):
                        after(dve, norm_sems[0][4], i - 4)
                        nc.vector.tensor_tensor(part[:, w], part[:, w], over(g3), ALU.mult).then_inc(scaled, 1)
                    if live(i - 3, NG):
                        after(dve, down_done, i - 2)
                        after(dve, norm_sems[0][4], i - 4)
                        nc.vector.tensor_tensor(res3[:, w], psum[5 + w][:, :, :], batches(H, i - 3), ALU.add) \
                            .then_inc(res3_ready, 1)
                    if live(i - 5, NG):
                        after(dve, scaled, i - 4)
                        after(dve, skip_ready, i - 4)
                        after(dve, norm_sems[1][4], i - 6)
                        nc.vector.tensor_tensor(res4[:, w], part[:, w], skip[:, w], ALU.add).then_inc(res4_ready, 1)
                    if live(i - 3, NG):
                        stats(0, res3[:, w], i - 3, w, res3_ready)
                    if live(i - 5, NG):
                        stats(1, res4[:, w], i - 5, w, res4_ready)
                    if live(i - 3, NG):
                        moments(0, i - 3, w)
                    if live(i - 5, NG):
                        moments(1, i - 5, w)
                run_steps(dve, step, NG, 5, HEAD)

            @block.gpsimd
            def _(pool):
                def rstd(n, g, b):
                    _, stats_ready, var_ready, rstd_ready, normed, scale_ready = norm_sems[n]
                    layer_rstd(nc, pool, c, *norms[n][1:], b, g, stats_ready, (normed,), var_ready, scale_ready,
                               rstd_ready)

                def step(i, u):
                    if live(i - 4, NG):
                        after(pool, res4_ready, i - 5)
                        nc.gpsimd.tensor_tensor(skip[:, u], batches(X, i - 4), over(be3), ALU.add) \
                            .then_inc(skip_ready, 1)
                    if live(i - 3, NG):
                        rstd(0, i - 3, 1 - u)
                    if live(i - 5, NG):
                        rstd(1, i - 5, 1 - u)
                run_steps(pool, step, NG, 5, HEAD)


_INS = ['x', 'adj', 'L0_gnn_Wqkv', 'L0_gnn_Wo', 'L1_gnn_W', 'L1_gnn_a', 'L2_gnn_Wg0', 'L2_gnn_bg0', 'L2_gnn_Wg1',
        'L2_gnn_bg1', 'L2_gnn_Wih', 'L2_gnn_Whh', 'L2_gnn_bih', 'L2_gnn_bhh', 'L3_gnn_Wc', 'L3_gnn_bc', 'L3_gnn_g1',
        'L3_gnn_be1', 'L3_gnn_Wq', 'L3_gnn_Wk', 'L3_gnn_Wv', 'L3_gnn_Wo', 'L3_gnn_bo', 'L3_gnn_g2', 'L3_gnn_be2',
        'L3_gnn_W1', 'L3_gnn_b1', 'L3_gnn_W2', 'L3_gnn_b2', 'L3_gnn_g3', 'L3_gnn_be3']


def kernel(**inputs):
    import numpy as _np
    import concourse.bacc as _bacc
    from concourse import mybir as _mybir
    from concourse.bass_utils import run_bass_kernel_spmd as _run

    nc = _bacc.Bacc("TRN2", target_bir_lowering=False, num_devices=1)
    arrays, args = {}, {}
    for name in _INS:
        arr = _np.ascontiguousarray(inputs[name])
        arrays[f"in_{name}_dram"] = arr
        args[name] = nc.dram_tensor(f"in_{name}_dram", arr.shape, _mybir.dt.from_np(arr.dtype),
                                    kind="ExternalInput").ap()
    out = nc.dram_tensor("out_0_dram", inputs["x"].shape, _mybir.dt.float32, kind="ExternalOutput").ap()
    program(nc, args, out)
    r = _run(nc, [arrays], core_ids=[0])
    return r.results[0]["out_0_dram"]
```

```python
from contextlib import ExitStack, contextmanager

import concourse.bass as bass
from concourse import mybir

F32 = mybir.dt.float32
BF16 = mybir.dt.bfloat16
F32R = mybir.dt.float32r
ALU = mybir.AluOpType
ACT = mybir.ActivationFunctionType
AX = mybir.AxisListType.X

P = 128
GROUP = 4
EPS = 1e-5
NEG = -1e30
NEG3 = -1e9
ALPHA = 0.2
HEADS = 4
HD = P // HEADS
WIDE = 128
SKIPS = 4
GATES = 4


def after(eng, sem, n):
    if isinstance(n, int) and n <= 0:
        return
    eng.wait_ge(sem, n)


def after_nop(eng, sem, n):
    if isinstance(n, int) and n <= 0:
        return
    eng.wait_ge(sem, n)
    eng.nop(nofuse=True)


def run_steps(eng, step, n, lag, head, tail=None):
    assert head % 2 == 0 and n % 2 == 0 and head >= lag
    for i in range(head):
        step(i, i % 2)
    tail = n if tail is None else tail
    with eng.Fori(head // 2, tail // 2) as pair:
        step(pair * 2, 0)
        step(pair * 2 + 1, 1)
    for i in range(tail, n + lag):
        step(i, i % 2)


def live(g, n):
    return not isinstance(g, int) or 0 <= g < n


def batches(buf, g, count=GROUP):
    return buf[:, bass.ds(g * count, count), :]


def over(ap, count=GROUP):
    return ap.unsqueeze(1).broadcast_to([ap.shape[0], count, ap.shape[-1]])


def landed(g, b):
    return (g - b) * 8 + 16


@contextmanager
def phase_semaphores(nc, prefix):
    held = []

    def sem(name):
        held.append(nc.alloc_semaphore(name=f"{prefix}_{name}"))
        return held[-1]
    yield sem
    nc.clear_and_free_semaphores(held)
    nc.all_engine_barrier()


def flat(ap):
    return ap.rearrange("p k c -> p (k c)")


def program(nc, a, out):
    x = a["x"]
    B = x.shape[0]
    NG = B // GROUP
    ctx = ExitStack()

    def sb(name, shape, dt=F32):
        return ctx.enter_context(nc.sbuf_tensor(name, shape, dt))

    with ctx:
        X = sb("X", [P, B, P])
        H = sb("H", [P, B, P])
        c = dict(
            ident=sb("ident", [P, P]), identb=sb("identb", [P, P], BF16), adjT=sb("adjT", [P, P]),
            causal=sb("causal", [P, P]), gat_mask=sb("gat_mask", [P, P], BF16),
            head_mask=sb("head_mask", [P, P], BF16), lapT=sb("lapT", [P, P]),
            sym=sb("sym", [P, P]), power=sb("power", [P, P]), ones3=sb("ones3", [3, P], BF16),
            half=sb("half", [P, GROUP]), Gqk=sb("Gqk", [P, P]), Gvo=sb("Gvo", [P, P]), W1g=sb("W1g", [P, P]),
            a1rep=sb("a1rep", [P, P]), a2rep=sb("a2rep", [P, P]),
            rowsum9=sb("rowsum9", [9, P], BF16), bg9=sb("bg9", [9, 2, P], BF16), Wg=sb("Wg", [P, 2, P]),
            cols=sb("cols", [P, 20]), bias3=sb("bias3", [3, 3, P], BF16), Wx=sb("Wx", [P, 5, P]),
            W1=sb("W1", [P, 2 * P]), W2=sb("W2", [P, 2, P]), rep=sb("rep", [P, 6, P]),
        )
        lstm_weights = ExitStack()
        c["WT"] = lstm_weights.enter_context(nc.sbuf_tensor("WT", [P, 2, SKIPS, GATES, P], F32))
        psum = [ctx.enter_context(nc.psum_tensor(f"bank{i}", [P, GROUP, P], F32)) for i in range(8)]
        bias_parts = ExitStack()
        bpart = bias_parts.enter_context(nc.sbuf_tensor("bpart", [1, 3, 6, P], BF16))
        setup(nc, a, c, X, H, psum, bpart)
        attention_layer(nc, c, X, psum, NG, x, late_constants(a, c, bpart))
        bias_parts.close()
        attention_layer(nc, c, X, psum, NG, None)
        gcn_layer(nc, c, X, H, psum, NG)
        for p in range(1, SKIPS + 1):
            lstm_pass(nc, c, H, psum, B, p)
        lstm_weights.close()
        transformer_attention(nc, c, X, H, psum, NG)
        transformer_mlp(nc, c, X, H, psum, NG, out)


def late_constants(a, c, bpart):
    late = [(c["Wg"][:, 0, :], a["L2_gnn_Wg0"]), (c["Wg"][:, 1, :], a["L2_gnn_Wg1"]),
            (c["W1"][:, :], a["L3_gnn_W1"]), (c["W2"][:, :, :], a["L3_gnn_W2"].rearrange("(j d) n -> d j n", j=2))]
    late += [(c["Wx"][:, j, :], a["L3_gnn_" + w]) for j, w in enumerate(("Wc", "Wq", "Wk", "Wv", "Wo"))]
    late += [(c["rep"][:, j, :], a["L3_gnn_" + w].rearrange("(a n) -> a n", a=1).broadcast_to([P, P]))
             for j, w in enumerate(("g1", "be1", "g2", "be2", "g3", "be3"))]
    for part in range(3):
        late.append((c["bias3"][part:part + 1, :, :], bpart[0:1, part, 0:3, :]))
        for other in range(3):
            row = 3 * part + other
            late.append((c["bg9"][row:row + 1, :, :], bpart[0:1, part, 3:5, :]))
            late.append((c["rowsum9"][row:row + 1, :], bpart[0:1, other, 5, :]))
    return late


def setup(nc, a, c, X, H, psum, bpart):
    ctx = ExitStack()
    with ctx:
        def sb(name, shape, dt=F32):
            return ctx.enter_context(nc.sbuf_tensor(name, shape, dt))

        sem = ctx.enter_context(phase_semaphores(nc, "setup"))
        ident, adjT, ones = c["ident"], c["adjT"], sb("ones", [P, P])
        raw_ih, raw_hh = H[:, 0:16, :], H[:, 16:32, :]
        adj, Wqkv, Wo, W1g = H[:, 32, :], H[:, 33:36, :], H[:, 36, :], c["W1g"]
        wT = H[:, 40:44, :]
        avec = H[:, 44:46, :]
        rows_a, rows_b = sb("rows_a", [20, P]), sb("rows_b", [20, P])
        brow, bres = sb("brow", [1, 6, P]), sb("bres", [1, 6, P])
        sym, power, scratch = c["sym"], c["power"], sb("scratch", [P, P])
        sums, stat, norm = sb("sums", [P, 1]), sb("stat", [P, 2]), sb("norm", [P, 1])
        powhalf = sb("powhalf", [P, 1])

        small_loaded, lstm_loaded = sem("small_loaded"), sem("lstm_loaded")
        rows_zeroed, zeroed, ident_ready = sem("rows_zeroed"), sem("zeroed"), sem("ident_ready")
        rows_loaded, row_copied = sem("rows_loaded"), sem("row_copied")
        masks_filled, copied, products = sem("masks_filled"), sem("copied"), sem("products")
        v = sem("setup_v")
        root_ready, eig_pe, eig_v = sem("root_ready"), sem("eig_pe"), sem("eig_v")

        SMALL = [
            (adj, a["adj"]), (Wqkv, a["L0_gnn_Wqkv"].rearrange("d (j e) -> d j e", j=3)), (Wo, a["L0_gnn_Wo"]),
            (W1g[:, :], a["L1_gnn_W"]),
        ]
        SMALL += [(brow[0:1, j, :], a[w].rearrange("(a n) -> a n", a=1))
                  for j, w in enumerate(("L3_gnn_bc", "L3_gnn_bo", "L3_gnn_b2", "L2_gnn_bg0", "L2_gnn_bg1"))]
        ROWS = [
            (rows_a[0:16, :], a["L2_gnn_bih"].rearrange("q (g d) -> (q g) d", d=P)),
            (rows_a[16:18, :], a["L3_gnn_b1"].rearrange("(j d) -> j d", j=2)),
            (rows_a[18:20, :], a["L1_gnn_a"].rearrange("(j d) o -> j (d o)", j=2)),
            (rows_b[0:16, :], a["L2_gnn_bhh"].rearrange("q (g d) -> (q g) d", d=P)),
        ]

        with nc.Block() as block:
            @block.sync
            def _(sync):
                for dst, src in SMALL:
                    sync.dma_start(dst, src).then_inc(small_loaded, 16)
                sync.wait_ge(rows_zeroed, 1)
                for dst, src in ROWS:
                    sync.dma_start(dst, src).then_inc(rows_loaded, 16)
                for raw, name in ((raw_ih, "L2_gnn_Wih"), (raw_hh, "L2_gnn_Whh")):
                    sync.dma_start(raw, a[name].rearrange("q (g o) i -> o (q g) i", g=GATES)).then_inc(lstm_loaded, 16)

            @block.gpsimd
            def _(pool):
                nc.gpsimd.memset(ident[:, :], 0.0).then_inc(zeroed, 1)
                nc.gpsimd.memset(powhalf[:, :], 0.5)
                nc.gpsimd.memset(c["half"][:, :], -0.5)
                nc.gpsimd.memset(ones[:, :], 1.0)
                nc.gpsimd.memset(c["ones3"][:, :], 1.0)
                pool.wait_ge(zeroed, 1)
                nc.gpsimd.affine_select(out=ident[:, :], in_=ident[:, :], compare_op=ALU.not_equal, fill=1.0,
                                        base=0, pattern=[[-1, P]], channel_multiplier=1).then_inc(ident_ready, 1)
                pool.wait_ge(small_loaded, 16 * len(SMALL))
                nc.gpsimd.affine_select(out=c["causal"][:, :], in_=adj, compare_op=ALU.is_ge, fill=NEG,
                                        base=0, pattern=[[-1, P]], channel_multiplier=1).then_inc(masks_filled, 1)
                pool.wait_ge(eig_v, 2)
                nc.gpsimd.tensor_tensor(norm[:, :], stat[:, 0:1], powhalf[:, :], ALU.pow).then_inc(root_ready, 1)

            TRANSPOSES = [(adj, adjT[:, :]), (Wqkv[:, 0, :], wT[:, 0, :]), (Wqkv[:, 1, :], wT[:, 1, :]),
                          (Wqkv[:, 2, :], wT[:, 2, :]), (W1g[:, :], wT[:, 3, :])]

            @block.tensor
            def _(pe):
                pe.wait_ge(ident_ready, 1)
                pe.wait_ge(small_loaded, 16 * len(SMALL))
                for n, (src, _) in enumerate(TRANSPOSES):
                    t = nc.tensor.transpose(psum[n // 4][:, n % 4, :], src, ident[:, :])
                t.then_inc(products, 1)
                pe.wait_ge(v, 1)
                nc.tensor.matmul(psum[6][0:1, 0, :], ones[:, 0:1], adjT[:, :], start=True, stop=True) \
                    .then_inc(products, 1)
                pe.wait_ge(v, 2)
                nc.tensor.transpose(psum[2][:, 0, 0:20], rows_a[:, :], ident[0:20, 0:20]).then_inc(products, 1)
                pe.wait_ge(eig_v, 1)
                nc.tensor.matmul(psum[7][:, 0, 0:1], ones[:, :], sums[:, 0:1], start=True, stop=True).then_inc(eig_pe, 1)
                pe.wait_ge(lstm_loaded, 32)
                for n in range(2 * SKIPS):
                    kind, q = n // SKIPS, n % SKIPS
                    raw = (raw_ih, raw_hh)[kind]
                    if n >= 2:
                        pe.wait_ge(copied, n - 1)
                    for g in range(GATES):
                        t = nc.tensor.transpose(psum[3 + n % 2][:, g, :], raw[:, q * GATES + g, :], ident[:, :])
                    t.then_inc(products, 1)
                pe.wait_ge(v, 5)
                nc.tensor.matmul(psum[5][:, 0, :], wT[:, 0, :], wT[:, 1, :], start=True, stop=True)
                nc.tensor.matmul(psum[5][:, 1, :], wT[:, 2, :], Wo, start=True, stop=True)
                for j in range(2):
                    t = nc.tensor.matmul(psum[5][:, 2 + j, :], wT[:, 3, :], avec[:, j, :], start=True, stop=True)
                t.then_inc(products, 1)
            @block.vector
            def _(dve):
                vec = nc.vector
                vec.memset(rows_b[:, :], 0.0).then_inc(rows_zeroed, 1)
                dve.wait_ge(products, 1)
                for n, (_, dst) in enumerate(TRANSPOSES):
                    t = vec.tensor_copy(dst, psum[n // 4][:, n % 4, :])
                t.then_inc(v, 1)
                dve.wait_ge(rows_loaded, 16 * len(ROWS))
                vec.tensor_tensor(rows_a[:, :], rows_a[:, :], rows_b[:, :], ALU.add).then_inc(v, 1)
                dve.wait_ge(v, 1)
                vec.tensor_tensor(sym[:, :], adj, adjT[:, :], ALU.add).then_inc(v, 1)
                dve.wait_ge(products, 3)
                vec.tensor_copy(c["cols"][:, :], psum[2][:, 0, 0:20]).then_inc(v, 1)
                dve.wait_ge(v, 4)
                for j in range(2):
                    t = vec.tensor_scalar(avec[:, j, :], ones[:, :], c["cols"][:, 18 + j:19 + j], None, ALU.mult)
                t.then_inc(v, 1)
                vec.tensor_scalar(sym[:, :], sym[:, :], 0.5, None, ALU.mult).then_inc(v, 1)
                dve.wait_ge(v, 6)
                vec.tensor_tensor_reduce(scratch[:, :], sym[:, :], sym[:, :], 1.0, 0.0, ALU.mult, ALU.add,
                                         sums[:, 0:1]).then_inc(eig_v, 1)
                dve.wait_ge(products, 2)
                vec.tensor_copy(brow[0:1, 5, :], psum[6][0:1, 0, :]).then_inc(row_copied, 1)
                dve.wait_ge(row_copied, 1)
                vec.tensor_copy(bpart[:, 0, :, :], brow[:, :, :]).then_inc(v, 1)
                dve.wait_ge(v, 7)
                vec.tensor_tensor(bres[:, :, :], brow[:, :, :], bpart[:, 0, :, :], ALU.subtract).then_inc(v, 1)
                dve.wait_ge(v, 8)
                vec.tensor_copy(bpart[:, 1, :, :], bres[:, :, :]).then_inc(v, 1)
                dve.wait_ge(v, 9)
                vec.tensor_tensor(bres[:, :, :], bres[:, :, :], bpart[:, 1, :, :], ALU.subtract).then_inc(v, 1)
                dve.wait_ge(v, 10)
                vec.tensor_copy(bpart[:, 2, :, :], bres[:, :, :])
                vec.tensor_copy(c["identb"][:, :], ident[:, :])
                vec.tensor_scalar(c["gat_mask"][:, :], adj, 0.0, NEG, ALU.is_equal, ALU.mult)
                vec.tensor_scalar(c["head_mask"][:, :], adj, 0.0, NEG3, ALU.is_le, ALU.mult)
                for n in range(2 * SKIPS):
                    kind, q = n // SKIPS, n % SKIPS
                    dve.wait_ge(products, 4 + n)
                    vec.tensor_copy(c["WT"][:, kind, q, :, :], psum[3 + n % 2][:, :, :]).then_inc(copied, 1)
                    if n == 0:
                        dve.wait_ge(eig_pe, 1)
                        vec.tensor_scalar(stat[:, 0:1], psum[7][:, 0, 0:1], 1e-30, None, ALU.add).then_inc(eig_v, 1)
                dve.wait_ge(products, 4 + 2 * SKIPS)
                vec.tensor_scalar(c["Gqk"][:, :], psum[5][:, 0, :], float(P) ** -0.5, None, ALU.mult)
                vec.tensor_copy(c["Gvo"][:, :], psum[5][:, 1, :])
                vec.tensor_copy(c["a1rep"][:, :], psum[5][:, 2, :])
                vec.tensor_copy(c["a2rep"][:, :], psum[5][:, 3, :])
                dve.wait_ge(root_ready, 1)
                vec.reciprocal(stat[:, 1:2], norm[:, :]).then_inc(v, 1)
                dve.wait_ge(v, 11)
                vec.scalar_tensor_tensor(power[:, :], sym[:, :], stat[:, 1:2], ident[:, :], ALU.mult, ALU.add)


def attention_layer(nc, c, X, psum, NG, x, late=()):
    layer = 0 if x is not None else 1
    ctx = ExitStack()
    with ctx:
        def sb(name, shape, dt=F32):
            return ctx.enter_context(nc.sbuf_tensor(f"{name}_{layer}", shape, dt))

        sem = ctx.enter_context(phase_semaphores(nc, f"layer{layer}"))

        ring = [P, 2, GROUP, P]
        xin, xT, val, prob, probT, res = (sb(n, ring) for n in ("xin", "xT", "val", "prob", "probT", "res"))
        keyT = sb("keyT", ring) if layer == 0 else None
        score = sb("score", ring)
        top, total, inv = (sb(n, [P, 2, GROUP]) for n in ("top", "total", "inv"))
        st6, mv, rstd = sb("st6", [P, 2, GROUP, 6]), sb("mv", [P, 2, GROUP, 2]), sb("rstd", [P, 2, GROUP])
        var, shift = sb("var", [P, 2, 2, GROUP]), sb("shift", [P, 2, GROUP])

        loaded, staged = ([sem(f"{n}{b}") for b in range(2)] for n in ("loaded", "staged"))
        late_loaded = sem("late_loaded")
        xT_done, xT_copied = sem("xT_done"), sem("xT_copied")
        key_done, key_copied, val_done, val_copied = sem("key_done"), sem("key_copied"), sem("val_done"), sem("val_copied")
        scores_done, scores_ready, top_ready = sem("scores_done"), sem("scores_ready"), sem("top_ready")
        probs_ready, probT_done, probT_copied = sem("probs_ready"), sem("probT_done"), sem("probT_copied")
        mixed, inv_ready, res_ready = sem("mixed"), sem("inv_ready"), sem("res_ready")
        st6_ready, stats_ready, var_ready = sem("st6_ready"), sem("stats_ready"), sem("var_ready")
        scale_ready, rstd_ready, normed_a, normed_v = sem("scale_ready"), sem("rstd_ready"), sem("normed_a"), sem("normed_v")
        b_xT, b_key, b_probT, b_mix = psum[0:4]
        b_val, b_score = psum[4:6], psum[6:8]
        small_slope = sem("small_slope")
        HEAD = 6
        ACT_TILES = 2

        with nc.Block() as block:
            @block.sync
            def _(sync):
                def step(i, u):
                    if live(i, NG):
                        if layer == 0:
                            after_nop(sync, loaded[u], landed(i, u))
                        after_nop(sync, xT_done, i - 1)
                        sync.dma_start(xin[:, u], batches(X, i)).then_inc(staged[u], 16)
                        if layer == 0 and (not isinstance(i, int) or i + 2 < NG):
                            load(i + 2, u)
                        if isinstance(i, int) and 1 <= i < HEAD:
                            for dst, src in late[i - 1::HEAD - 1]:
                                sync.dma_start(dst, src).then_inc(late_loaded, 16)

                def load(g, b):
                    sync.dma_start(batches(X, g), x[bass.ds(g * GROUP, GROUP), :, :].rearrange("b t c -> t b c")) \
                        .then_inc(loaded[b], 16)

                if layer == 0:
                    load(0, 0)
                    load(1, 1)
                run_steps(sync, step, NG, 0, HEAD, NG - 2)
                if late:
                    sync.wait_ge(late_loaded, 16 * len(late))

            @block.tensor
            def _(pe):
                def transpose_x(g, b):
                    after(pe, staged[b], landed(g, b))
                    after(pe, xT_copied, g)
                    for k in range(GROUP):
                        t = nc.tensor.transpose(b_xT[:, k, :], xin[:, b, k, :], c["ident"][:, :])
                    t.then_inc(xT_done, 1)

                def mix(g, b):
                    after(pe, probT_copied, g + 1)
                    after(pe, val_copied, g + 1)
                    after(pe, res_ready, g)
                    for k in range(GROUP):
                        t = nc.tensor.matmul(b_mix[:, k, :], probT[:, b, k, :], val[:, b, k, :], start=True, stop=True)
                    t.then_inc(mixed, 1)

                def keys(g, b):
                    after(pe, xT_copied, g + 1)
                    after(pe, key_copied, g)
                    nc.tensor.matmul(b_key[:, :, :], c["Gqk"][:, :], xT[:, b], start=True, stop=True) \
                        .then_inc(key_done, 1)

                def values(g, b):
                    after(pe, xT_copied, g + 1)
                    after(pe, val_copied, g - 1)
                    w = c["Gvo"] if layer == 0 else c["W1g"]
                    for k in range(GROUP):
                        t = nc.tensor.matmul(b_val[b][:, k, :], xT[:, b, k, :], w[:, :], start=True, stop=True)
                    t.then_inc(val_done, 1)

                def transpose_probs(g, b):
                    after(pe, probs_ready, g + 1)
                    after(pe, probT_copied, g)
                    for k in range(GROUP):
                        t = nc.tensor.transpose(b_probT[:, k, :], prob[:, b, k, :], c["ident"][:, :])
                    t.then_inc(probT_done, 1)

                def scores(g, b):
                    after(pe, scores_ready, g - 1)
                    if layer == 0:
                        after(pe, key_copied, g + 1)
                        for k in range(GROUP):
                            t = nc.tensor.matmul(b_score[b][:, k, :], keyT[:, b, k, :], xT[:, b, k, :],
                                                 start=True, stop=True)
                    else:
                        nc.tensor.matmul(b_score[b][:, :, :], c["identb"][:, :], over(c["gat_mask"][:, :]),
                                         start=True, stop=True)
                        nc.tensor.matmul(b_score[b][:, :, :], c["a2rep"][:, :], xT[:, b], start=False, stop=True, skip_group_check=True)
                        for k in range(GROUP):
                            t = nc.tensor.matmul(b_score[b][:, k, :], xT[:, b, k, :], c["a1rep"][:, :],
                                                 start=False, stop=True, skip_group_check=True)
                    t.then_inc(scores_done, 1)

                def step(i, u):
                    w = 1 - u
                    if live(i, NG):
                        transpose_x(i, u)
                    if live(i - 1, NG):
                        scores(i - 1, w)
                    if live(i - 3, NG):
                        mix(i - 3, w)
                    if live(i, NG):
                        if layer == 0:
                            keys(i, u)
                        values(i, u)
                    if live(i - 2, NG):
                        transpose_probs(i - 2, u)
                run_steps(pe, step, NG, 3, HEAD)

            @block.scalar
            def _(act):
                def copy_xT(g, b):
                    after(act, xT_done, g + 1)
                    after(act, scores_done, g - 1)
                    nc.scalar.activation(xT[:, b], b_xT[:, :, :], ACT.Copy).then_inc(xT_copied, 1)

                def exps(g, b):
                    after(act, top_ready, g + 1)
                    after(act, probT_done, g - 1)
                    after(act, inv_ready, g - 1)
                    for k in range(GROUP):
                        t = nc.scalar.activation(prob[:, b, k, :], score[:, b, k, :], ACT.Exp,
                                                 bias=top[:, b, k:k + 1], accum_out=total[:, b, k:k + 1])
                    t.then_inc(probs_ready, 1)

                def copy_values(g, b):
                    after(act, val_done, g + 1)
                    after(act, mixed, g - 1)
                    nc.scalar.activation(val[:, b], b_val[b][:, :, :], ACT.Copy).then_inc(val_copied, 1)

                def copy_probT(g, b):
                    after(act, probT_done, g + 1)
                    after(act, mixed, g - 1)
                    nc.scalar.activation(probT[:, b], b_probT[:, :, :], ACT.Copy).then_inc(probT_copied, 1)

                def small_slopes(g, b):
                    after(act, scores_done, g + 1)
                    after(act, probs_ready, g - 1)
                    nc.scalar.activation(score[:, b], b_score[b][:, :, :], ACT.Copy, scale=ALPHA) \
                        .then_inc(small_slope, 1)

                def copy_keys(g, b):
                    after(act, key_done, g + 1)
                    after(act, scores_done, g - 1)
                    nc.scalar.activation(keyT[:, b], b_key[:, :, :], ACT.Copy).then_inc(key_copied, 1)

                def normalise(g, b):
                    after(act, rstd_ready, g + 1)
                    for k in range(ACT_TILES):
                        t = nc.scalar.activation(
                            X[:, bass.ds(g * GROUP + k, 1), :].rearrange("p a c -> p (a c)"), res[:, b, k, :],
                            ACT.Identity, bias=shift[:, b, k:k + 1], scale=rstd[:, b, k:k + 1])
                    t.then_inc(normed_a, 1)

                def step(i, u):
                    w = 1 - u
                    if live(i - 3, NG):
                        copy_probT(i - 3, w)
                    if live(i, NG):
                        copy_xT(i, u)
                    if live(i - 2, NG):
                        exps(i - 2, u)
                    if live(i - 1, NG):
                        copy_values(i - 1, w)
                        if layer == 1:
                            small_slopes(i - 1, w)
                    if live(i, NG) and layer == 0:
                        copy_keys(i, u)
                    if live(i - 4, NG):
                        normalise(i - 4, u)
                run_steps(act, step, NG, 4, HEAD)

            @block.vector
            def _(dve):
                def biased(g, b):
                    after(dve, scores_done, g + 1)
                    after(dve, probs_ready, g - 1)
                    nc.vector.tensor_tensor(score[:, b], b_score[b][:, :, :], over(c["causal"][:, :]), ALU.add) \
                        .then_inc(scores_ready, 1)

                def row_max(g, b):
                    after(dve, scores_ready, g + 1)
                    after(dve, probs_ready, g - 1)
                    nc.vector.tensor_reduce(top[:, b, :], score[:, b], AX, ALU.max, negate=True).then_inc(top_ready, 1)

                def residual(g, b):
                    after(dve, probs_ready, g + 1)
                    nc.vector.reciprocal(inv[:, b, :], total[:, b, :]).then_inc(inv_ready, 1)
                    after(dve, inv_ready, g + 1)
                    after(dve, mixed, g + 1)
                    after(dve, normed_a, g - 1)
                    after(dve, normed_v, g - 1)
                    for k in range(GROUP):
                        t = nc.vector.scalar_tensor_tensor(
                            res[:, b, k, :], b_mix[:, k, :], inv[:, b, k:k + 1],
                            X[:, bass.ds(g * GROUP + k, 1), :].rearrange("p a c -> p (a c)"), ALU.mult, ALU.add)
                    t.then_inc(res_ready, 1)

                def leaky(g, b):
                    after(dve, small_slope, g + 1)
                    nc.vector.tensor_tensor(score[:, b], b_score[b][:, :, :], score[:, b], ALU.max) \
                        .then_inc(scores_ready, 1)

                def normalise(g, b):
                    after(dve, rstd_ready, g + 1)
                    for k in range(ACT_TILES, GROUP):
                        t = nc.vector.tensor_scalar(
                            X[:, bass.ds(g * GROUP + k, 1), :].rearrange("p a c -> p (a c)"), res[:, b, k, :],
                            rstd[:, b, k:k + 1], shift[:, b, k:k + 1], ALU.mult, ALU.add)
                    t.then_inc(normed_v, 1)

                def step(i, u):
                    w = 1 - u
                    if live(i - 3, NG):
                        residual(i - 3, w)
                        tile_stats(nc, dve, res[:, w], st6, w, i - 3, res_ready, st6_ready)
                    if live(i - 1, NG):
                        if layer == 0:
                            biased(i - 1, w)
                        else:
                            leaky(i - 1, w)
                    if live(i - 3, NG):
                        tile_moments(nc, dve, st6, mv, w, i - 3, st6_ready, var_ready, stats_ready)
                    if live(i - 1, NG):
                        row_max(i - 1, w)
                    if live(i - 4, NG):
                        normalise(i - 4, u)
                run_steps(dve, step, NG, 4, HEAD)

            @block.gpsimd
            def _(pool):
                def step(i, u):
                    layer_rstd(nc, pool, c, mv, var, rstd, shift, u, i, stats_ready, (normed_a, normed_v), var_ready,
                               scale_ready, rstd_ready)
                run_steps(pool, step, NG, 0, HEAD)


def tile_stats(nc, dve, tiles, st6, b, g, res_ready, st6_ready):
    if res_ready is not None:
        after(dve, res_ready, g + 1)
    for k in range(GROUP):
        t = nc.vector.bn_stats(st6[:, b, k, :], tiles[:, k, :])
    t.then_inc(st6_ready, 1)


def tile_moments(nc, dve, st6, mv, b, g, st6_ready, mv_free, stats_ready):
    after_nop(dve, mv_free, g - 1)
    after_nop(dve, st6_ready, g + 1)
    for k in range(GROUP):
        t = nc.vector.bn_aggr(mv[:, b, k, :], st6[:, b, k, :])
    t.then_inc(stats_ready, 1)


def layer_rstd(nc, pool, c, mv, var, rstd, shift, b, g, stats_ready, normed, var_ready, scale_ready, rstd_ready):
    after_nop(pool, stats_ready, g + 1)
    nc.gpsimd.tensor_scalar(var[:, b, 0, :], mv[:, b, :, 1], EPS, None, ALU.add)
    nc.gpsimd.tensor_scalar(var[:, b, 1, :], mv[:, b, :, 0], -1.0, None, ALU.mult).then_inc(var_ready, 1)
    for n in normed:
        after_nop(pool, n, g - 1)
    after_nop(pool, var_ready, g + 1)
    nc.gpsimd.tensor_tensor(rstd[:, b, :], var[:, b, 0, :], c["half"][:, :], ALU.pow).then_inc(scale_ready, 1)
    after(pool, scale_ready, g + 1)
    nc.gpsimd.tensor_tensor(shift[:, b, :], var[:, b, 1, :], rstd[:, b, :], ALU.mult).then_inc(rstd_ready, 1)


def gcn_layer(nc, c, X, H, psum, NG):
    ctx = ExitStack()
    with ctx:
        def sb(name):
            return ctx.enter_context(nc.sbuf_tensor(f"gcn_{name}", [P, 2, GROUP, P], F32))

        sem = ctx.enter_context(phase_semaphores(nc, "gcn"))

        xin, m1, h1, m2 = sb("xin"), sb("m1"), sb("h1"), sb("m2")
        ones, scratch, sums, stat = (ctx.enter_context(nc.sbuf_tensor(f"eig_{n}", [P, w], F32))
                                     for n, w in (("ones", P), ("scratch", P), ("sums", 2), ("stat", 4)))
        sym, power, square, trace = c["sym"], c["power"], psum[7][:, 0, :], psum[7][:, 1, 0:2]
        squared, diagonal, summed, traced, inverted, scaled, last = (
            sem(f"eig_{n}") for n in ("squared", "diagonal", "summed", "traced", "inverted", "scaled", "last"))
        staged = [sem(f"staged{b}") for b in range(2)]
        m1_done, m1_copied, h1_done, h1_ready = sem("m1_done"), sem("m1_copied"), sem("h1_done"), sem("h1_ready")
        m2_done, m2_copied, h2_done, h2_ready = sem("m2_done"), sem("m2_copied"), sem("h2_done"), sem("h2_ready")
        LAG, HEAD = 1, 4

        with nc.Block() as block:
            @block.sync
            def _(sync):
                def step(i, u):
                    after_nop(sync, m1_done, i - 1)
                    sync.dma_start(xin[:, u], batches(X, i)).then_inc(staged[u], 16)
                run_steps(sync, step, NG, 0, HEAD)

            @block.tensor
            def _(pe):
                def spread_x(g, b):
                    after(pe, staged[b], landed(g, b))
                    after(pe, m1_copied, g - 1)
                    for k in range(GROUP):
                        t = nc.tensor.matmul(psum[b][:, k, :], xin[:, b, k, :], c["adjT"][:, :], start=True, stop=True)
                    t.then_inc(m1_done, 1)

                def project_1(g, b):
                    after(pe, h1_ready, g - 1)
                    nc.tensor.matmul(psum[2 + b][:, :, :], c["rowsum9"][:, :], over(c["bg9"][:, 0, :]),
                                     start=True, stop=True)
                    after(pe, m1_copied, g + 1)
                    for k in range(GROUP):
                        t = nc.tensor.matmul(psum[2 + b][:, k, :], m1[:, b, k, :], c["Wg"][:, 0, :],
                                             start=False, stop=True, skip_group_check=True)
                    t.then_inc(h1_done, 1)

                def spread_h(g, b):
                    after(pe, h1_ready, g + 1)
                    after(pe, m2_copied, g - 1)
                    for k in range(GROUP):
                        t = nc.tensor.matmul(psum[4 + b][:, k, :], h1[:, b, k, :], c["adjT"][:, :],
                                             start=True, stop=True)
                    t.then_inc(m2_done, 1)

                def project_2(g, b):
                    after(pe, h2_ready, g)
                    nc.tensor.matmul(psum[6][:, :, :], c["bg9"][:, 1, :], over(c["rowsum9"][:, :]),
                                     start=True, stop=True)
                    after(pe, m2_copied, g + 1)
                    nc.tensor.matmul(psum[6][:, :, :], c["Wg"][:, 1, :], m2[:, b],
                                     start=False, stop=True, skip_group_check=True).then_inc(h2_done, 1)

                def sum_over_partitions(n):
                    nc.tensor.matmul(trace[:, 0:n], ones[:, :], sums[:, 0:n], start=True, stop=True).then_inc(traced, 1)

                def square_power():
                    nc.tensor.matmul(square, power[:, :], power[:, :], start=True, stop=True).then_inc(squared, 1)

                def step(i, u):
                    if live(i, NG):
                        spread_x(i, u)
                    if live(i - 1, NG):
                        spread_h(i - 1, 1 - u)
                    if live(i, NG):
                        after(pe, summed, i + 1)
                        sum_over_partitions(1)
                        project_1(i, u)
                    if live(i - 1, NG):
                        project_2(i - 1, 1 - u)
                    if live(i, NG):
                        after(pe, scaled, i + 1)
                        square_power()
                square_power()
                run_steps(pe, step, NG, LAG, HEAD)
                pe.wait_ge(summed, NG + 1)
                sum_over_partitions(1)
                pe.wait_ge(scaled, NG + 1)
                nc.tensor.matmul(square, sym[:, :], power[:, :], start=True, stop=True).then_inc(squared, 1)
                pe.wait_ge(summed, NG + 2)
                sum_over_partitions(2)

            @block.scalar
            def _(act):
                def step(i, u):
                    if live(i, NG):
                        after(act, m1_done, i + 1)
                        after(act, h1_done, i - 1)
                        nc.scalar.activation(m1[:, u], psum[u][:, :, :], ACT.Copy).then_inc(m1_copied, 1)
                    if live(i - 1, NG):
                        after(act, h2_done, i)
                        nc.scalar.activation(batches(H, i - 1), psum[6][:, :, :], ACT.Relu).then_inc(h2_ready, 1)
                run_steps(act, step, NG, LAG, HEAD)

            @block.vector
            def _(dve):
                vec = nc.vector

                def sum_diagonal(n):
                    after(dve, squared, n + 1)
                    vec.tensor_tensor(scratch[:, :], square, c["ident"][:, :], ALU.mult).then_inc(diagonal, 1)
                    after(dve, diagonal, n + 1)
                    vec.reduce_sum(sums[:, 0:1], scratch[:, :], AX).then_inc(summed, 1)

                def divide_by_trace(n):
                    after(dve, traced, n + 1)
                    vec.reciprocal(stat[:, 0:1], trace[:, 0:1]).then_inc(inverted, 1)
                    after(dve, inverted, n + 1)
                    vec.tensor_scalar(power[:, :], square, stat[:, 0:1], None, ALU.mult).then_inc(scaled, 1)

                def step(i, u):
                    if live(i, NG):
                        sum_diagonal(i)
                    if live(i - 1, NG):
                        after(dve, m2_done, i)
                        after(dve, h2_done, i - 2)
                        nc.vector.tensor_copy(m2[:, 1 - u], psum[5 - u][:, :, :]).then_inc(m2_copied, 1)
                    if live(i, NG):
                        divide_by_trace(i)
                        after(dve, h1_done, i + 1)
                        after(dve, m2_done, i - 1)
                        nc.vector.tensor_scalar(h1[:, u], psum[2 + u][:, :, :], 0.0, None, ALU.max) \
                            .then_inc(h1_ready, 1)
                vec.memset(ones[:, :], 1.0)
                run_steps(dve, step, NG, LAG, HEAD)
                sum_diagonal(NG)
                divide_by_trace(NG)
                dve.wait_ge(squared, NG + 2)
                dve.wait_ge(scaled, NG + 1)
                vec.tensor_tensor_reduce(scratch[:, :], square, power[:, :], 1.0, 0.0, ALU.mult, ALU.add,
                                         sums[:, 0:1]).then_inc(last, 1)
                dve.wait_ge(last, 1)
                vec.tensor_tensor_reduce(scratch[:, :], power[:, :], power[:, :], 1.0, 0.0, ALU.mult, ALU.add,
                                         sums[:, 1:2]).then_inc(summed, 1)
                dve.wait_ge(traced, NG + 2)
                vec.reciprocal(stat[:, 0:1], trace[:, 1:2]).then_inc(last, 1)
                dve.wait_ge(last, 2)
                vec.tensor_scalar(stat[:, 1:2], trace[:, 0:1], stat[:, 0:1], 1e-8, ALU.mult, ALU.add).then_inc(last, 1)
                dve.wait_ge(last, 3)
                vec.reciprocal(stat[:, 2:3], stat[:, 1:2]).then_inc(last, 1)
                dve.wait_ge(last, 4)
                vec.tensor_scalar(stat[:, 3:4], stat[:, 2:3], 2.0, None, ALU.mult).then_inc(last, 1)
                dve.wait_ge(last, 5)
                vec.scalar_tensor_tensor(c["lapT"][:, :], c["adjT"][:, :], stat[:, 3:4], c["ident"][:, :], ALU.mult,
                                         ALU.subtract)


def lstm_pass(nc, c, H, psum, B, p):
    nb = {1: 4, 2: 8, 3: 8, 4: 16}[p]
    nw = P // p
    cols = nb * nw
    pairs = B // nb // 2
    I, F, G, O = range(GATES)
    gates = [[I, G, O]] + [[I, G, F, O]] * (p - 1)
    per_chunk = sum(len(g) for g in gates)
    q = p - 1
    ctx = ExitStack()
    with ctx:
        def sb(name, dt=F32):
            return ctx.enter_context(nc.sbuf_tensor(f"lstm{p}_{name}", [P, 2, nb, nw], dt))

        sem = ctx.enter_context(phase_semaphores(nc, f"lstm{p}"))

        def sems(name):
            return [sem(f"{name}{b}") for b in range(2)]

        gate = [sb(f"gate{g}") for g in range(GATES)]
        cell = sb("cell")
        tanh_c, state = gate[I], gate[G]
        W_high, W_low = (ctx.enter_context(nc.sbuf_tensor(f"lstm{p}_{n}", [P, 2, GATES, P], F32R))
                         for n in ("W_high", "W_low"))
        token_high, token_low = sb("token_high", F32R), sb("token_low", F32R)
        state_high, state_low = (sb("state_high", F32R), sb("state_low", F32R)) if p > 1 else (None, None)
        W_high_ready, W_low_ready = sem("W_high_ready"), sem("W_low_ready")
        gate_done, gate_ready, fresh_ready, kept_ready = sems("gate_done"), sems("gate_ready"), sems("fresh"), sems("kept")
        cell_ready, tanh_ready, hidden_ready, state_ready = sems("cell"), sems("tanh"), sems("hidden"), sems("state")
        token_high_ready, token_low_ready = sems("token_high_ready"), sems("token_low_ready")
        kinds = 2 if p > 1 else 1

        def bank(b, g):
            return flat(psum[4 * b + g])[:, 0:cols].rearrange("p (b w) -> p b w", b=nb)

        def tokens(j, b, t):
            return H[:, bass.ds((j * 2 + b) * nb, nb), t:t + (nw - 1) * p + 1:p]

        def gates_before(j, t):
            return j * per_chunk + sum(len(g) for g in gates[:t])

        cells = [(t, b) for t in range(p) for b in range(2)]

        def run_pairs(eng, cell_work):
            def body(j, last):
                for n, (t, b) in enumerate(cells):
                    inside = n + 2 < len(cells)
                    following = (j, *cells[n + 2]) if inside else (j + 1, *cells[n + 2 - len(cells)])
                    cell_work(j, t, b, None if last and not inside else following)
            body(0, False)
            with eng.Fori(1, pairs - 1) as j:
                body(j, False)
            body(pairs - 1, True)

        with nc.Block() as block:
            @block.gpsimd
            def _(pool):
                def split_high(j, t, b):
                    nc.gpsimd.tensor_copy(token_high[:, b], tokens(j, b, t)).then_inc(token_high_ready[b], 1)

                def split_following(j, t, b, following):
                    if following:
                        after(pool, gate_done[b], gates_before(j, t) + (1 if t else len(gates[t])))
                        split_high(*following)
                split_high(0, *cells[0])
                split_high(0, *cells[1])
                run_pairs(pool, split_following)

            @block.tensor
            def _(pe):
                def products(b, g, kind, high, low, start, stop):
                    W = [w[:, kind, g, :] for w in (W_high, W_low)]
                    nc.tensor.matmul(bank(b, g), W[0], high[:, b], start=start, stop=False)
                    nc.tensor.matmul(bank(b, g), W[1], high[:, b], start=False, stop=False)
                    return nc.tensor.matmul(bank(b, g), W[0], low[:, b], start=False, stop=stop)

                def cell_products(j, t, b, _):
                    after(pe, gate_ready[b], gates_before(j, t))
                    after(pe, token_high_ready[b], j * p + t + 1)
                    after(pe, token_low_ready[b], j * p + t + 1)
                    for g in gates[t]:
                        m = products(b, g, 0, token_high, token_low, True, t == 0)
                        if t == 0:
                            m.then_inc(gate_done[b], 1)
                    if t:
                        after(pe, hidden_ready[b], j * p + t)
                        for g in gates[t]:
                            products(b, g, 1, state_high, state_low, False, True).then_inc(gate_done[b], 1)
                pe.wait_ge(W_low_ready, 1)
                run_pairs(pe, cell_products)

            @block.scalar
            def _(act):
                def cell_functions(j, t, b, _):
                    after(act, hidden_ready[b], j * p + t)
                    for n, g in enumerate(gates[t]):
                        after(act, gate_done[b], gates_before(j, t) + n + 1)
                        nc.scalar.activation(gate[g][:, b], bank(b, g), ACT.Tanh if g == G else ACT.Sigmoid,
                                             bias=c["cols"][:, q * GATES + g:q * GATES + g + 1]) \
                            .then_inc(gate_ready[b], 1)
                    after(act, cell_ready[b], j * p + t + 1)
                    nc.scalar.activation(tanh_c[:, b], cell[:, b], ACT.Tanh).then_inc(tanh_ready[b], 1)
                nc.scalar.activation(W_high[:, 0:kinds], c["WT"][:, 0:kinds, q], ACT.Copy).then_inc(W_high_ready, 1)
                run_pairs(act, cell_functions)

            @block.vector
            def _(dve):
                def update_cell(j, t, b):
                    if t == 0:
                        after(dve, tanh_ready[b], j * p)
                        after(dve, gate_ready[b], gates_before(j, t) + 2)
                        nc.vector.tensor_tensor(cell[:, b], gate[I][:, b], gate[G][:, b], ALU.mult) \
                            .then_inc(cell_ready[b], 1)
                        return
                    after(dve, gate_ready[b], gates_before(j, t) + 2)
                    nc.vector.tensor_tensor(gate[G][:, b], gate[I][:, b], gate[G][:, b], ALU.mult) \
                        .then_inc(fresh_ready[b], 1)
                    after(dve, gate_ready[b], gates_before(j, t) + 3)
                    after(dve, cell_ready[b], j * p + t)
                    nc.vector.tensor_tensor(gate[F][:, b], gate[F][:, b], cell[:, b], ALU.mult) \
                        .then_inc(kept_ready[b], 1)
                    after(dve, fresh_ready[b], j * (p - 1) + t)
                    after(dve, kept_ready[b], j * (p - 1) + t)
                    nc.vector.tensor_tensor(cell[:, b], gate[F][:, b], gate[G][:, b], ALU.add) \
                        .then_inc(cell_ready[b], 1)

                def update_hidden(j, t, b):
                    after(dve, tanh_ready[b], j * p + t + 1)
                    after(dve, gate_ready[b], gates_before(j, t + 1))
                    if t == p - 1:
                        nc.vector.tensor_tensor(tokens(j, b, t), gate[O][:, b], tanh_c[:, b], ALU.mult) \
                            .then_inc(hidden_ready[b], 1)
                        return
                    nc.vector.tensor_tensor(state_high[:, b], gate[O][:, b], tanh_c[:, b], ALU.mult)
                    nc.vector.tensor_tensor(state[:, b], gate[O][:, b], tanh_c[:, b], ALU.mult) \
                        .then_inc(state_ready[b], 1)
                    after(dve, state_ready[b], j * (p - 1) + t + 1)
                    nc.vector.tensor_tensor(state_low[:, b], state[:, b], state_high[:, b], ALU.subtract) \
                        .then_inc(hidden_ready[b], 1)

                def split_low(j, t, b):
                    after(dve, token_high_ready[b], j * p + t + 1)
                    nc.vector.tensor_tensor(token_low[:, b], tokens(j, b, t), token_high[:, b], ALU.subtract) \
                        .then_inc(token_low_ready[b], 1)

                def cell_updates(j, t, b, following):
                    update_cell(j, t, b)
                    if following:
                        split_low(*following)
                    update_hidden(j, t, b)
                dve.wait_ge(W_high_ready, 1)
                nc.vector.tensor_tensor(W_low[:, 0:kinds], c["WT"][:, 0:kinds, q], W_high[:, 0:kinds], ALU.subtract) \
                    .then_inc(W_low_ready, 1)
                split_low(0, *cells[0])
                split_low(0, *cells[1])
                run_pairs(dve, cell_updates)


def transformer_attention(nc, c, X, H, psum, NG):
    ctx = ExitStack()
    with ctx:
        def sb(name, shape, dt=F32):
            return ctx.enter_context(nc.sbuf_tensor(f"tr_{name}", shape, dt))

        sem = ctx.enter_context(phase_semaphores(nc, "tr"))

        tile, ring = [P, GROUP, P], [P, 2, GROUP, P]
        hin, x3, val = sb("hin", ring), sb("x3", ring), sb("val", ring)
        res0, m1, hidden, x1, x1T, qT, kT = (sb(n, tile) for n in ("res0", "m1", "hidden", "x1", "x1T", "qT", "kT"))
        prob, probT = sb("prob", [P, HEADS, GROUP, P]), sb("probT", [P, HEADS, GROUP, P])
        mixed, mixedT, res2, x2 = (sb(n, tile) for n in ("mixed", "mixedT", "res2", "x2"))
        top, total, inv = (sb(n, [P, HEADS, GROUP]) for n in ("top", "total", "inv"))
        norms = [(sb(f"st6_{n}", [P, 1, GROUP, 6]), sb(f"mv_{n}", [P, 1, GROUP, 2]), sb(f"var_{n}", [P, GROUP]),
                  sb(f"rstd_{n}", [P, GROUP])) for n in range(3)]
        norm_sems = [tuple(sem(f"{s}_{n}") for s in ("st6_ready", "stats_ready", "var_ready", "rstd_ready", "normed"))
                     for n in range(3)]
        hin_staged, x3_stored, x1_stored, x2_stored = ([sem(f"{n}{b}") for b in range(2)] for n in
                                                       ("hin_staged", "x3_stored", "x1_stored", "x2_stored"))
        h_turned, res0_ready, m1_done, m1_copied, h_done = (
            sem(n) for n in ("h_turned", "res0_ready", "m1_done", "m1_copied", "h_done"))
        affine, x1_ready, x1_turned, x1T_copied = (
            sem(n) for n in ("affine", "x1_ready", "x1_turned", "x1T_copied"))
        q_done, q_copied, k_done, k_copied, v_done, v_copied = (
            sem(n) for n in ("q_done", "q_copied", "k_done", "k_copied", "v_done", "v_copied"))
        scores_done, top_ready, probs_ready, inv_ready = (
            sem(n) for n in ("scores_done", "top_ready", "probs_ready", "inv_ready"))
        p_turned, pT_copied_a, pT_copied_v, mix_done, mix_ready = (
            sem(n) for n in ("p_turned", "pT_copied_a", "pT_copied_v", "mix_done", "mix_ready"))
        mix_turned, mixT_copied, o_done, res2_ready, scaled2, x2_ready = (
            sem(n) for n in ("mix_turned", "mixT_copied", "o_done", "res2_ready", "scaled2", "x2_ready"))
        Wc, Wq, Wk, Wv, Wo = (c["Wx"][:, j, :] for j in range(5))
        g1, be1, g2, be2 = (c["rep"][:, j, :] for j in range(4))
        b_x1T, b_hT, b_o, b_q, b_k, b_m1, b_v, b_h, b_mix, b_mixT = (
            psum[n] for n in (4, 5, 6, 7, 4, 5, 6, 7, 5, 6))
        b_pT = [psum[n] for n in (4, 5, 6, 4)]
        Wq_scaled = sem("Wq_scaled")
        LAG, HEAD = 3, 6

        def up_to(n):
            return min(n, NG) if isinstance(n, int) else n

        with nc.Block() as block:
            @block.sync
            def _(sync):
                def step(i, u):
                    if live(i, NG):
                        after_nop(sync, h_turned, i - 1)
                        sync.dma_start(hin[:, u], batches(H, i)).then_inc(hin_staged[u], 16)
                    if live(i - 1, NG):
                        after_nop(sync, norm_sems[0][4], i)
                        sync.dma_start(batches(X, i - 1), x3[:, 1 - u]).then_inc(x3_stored[1 - u], 16)
                    if live(i - 2, NG):
                        after_nop(sync, x1_ready, i - 1)
                        sync.dma_start(batches(H, i - 2), x1[:, :, :]).then_inc(x1_stored[u], 16)
                    if live(i - 5, NG):
                        after_nop(sync, x2_ready, i - 4)
                        sync.dma_start(batches(H, i - 5), x2[:, :, :]).then_inc(x2_stored[1 - u], 16)
                run_steps(sync, step, NG, 5, HEAD)
                for b in range(2):
                    sync.wait_ge(x3_stored[b], landed(NG - 2 + b, b))
                    sync.wait_ge(x2_stored[b], landed(NG - 2 + b, b))

            @block.tensor
            def _(pe):
                def bias_rows(bank, j):
                    nc.tensor.matmul(bank[:, :, :], c["ones3"][:, :], over(c["bias3"][:, j, :]), start=True, stop=True)

                def turn_x1(g):
                    after(pe, x1_ready, g + 1)
                    after(pe, k_copied, g)
                    after(pe, pT_copied_a, (g - 1) * 2)
                    for k in range(GROUP):
                        t = nc.tensor.transpose(b_x1T[:, k, :], x1[:, k, :], c["ident"][:, :])
                    t.then_inc(x1_turned, 1)

                def turn_h(g, b):
                    after(pe, hin_staged[b], landed(g, b))
                    after(pe, mix_ready, g - 3)
                    after(pe, m1_copied, g - 1)
                    after(pe, res0_ready, g)
                    for k in range(GROUP):
                        t = nc.tensor.transpose(b_hT[:, k, :], hin[:, b, k, :], c["ident"][:, :])
                    t.then_inc(h_turned, 1)

                def project_out(g):
                    after(pe, mixT_copied, g + 1)
                    bias_rows(b_o, 1)
                    for k in range(GROUP):
                        t = nc.tensor.matmul(b_o[:, k, :], mixedT[:, k, :], Wo, start=False, stop=True, skip_group_check=True)
                    t.then_inc(o_done, 1)

                def queries(g):
                    after(pe, x1T_copied, g + 1)
                    after(pe, norm_sems[1][4], g + 1)
                    nc.tensor.matmul(b_q[:, :, :], Wq, x1T[:, :, :], start=True, stop=True).then_inc(q_done, 1)

                def keys(g):
                    nc.tensor.matmul(b_k[:, :, :], Wk, x1T[:, :, :], start=True, stop=True).then_inc(k_done, 1)

                def spread_x(g, b):
                    after(pe, norm_sems[0][4], g + 1)
                    after(pe, res0_ready, up_to(g + 2))
                    after(pe, mix_ready, g - 2)
                    for k in range(GROUP):
                        t = nc.tensor.matmul(b_m1[:, k, :], x3[:, b, k, :], c["lapT"][:, :], start=True, stop=True)
                    t.then_inc(m1_done, 1)

                def values(g):
                    after(pe, res2_ready, g - 1)
                    after(pe, v_copied, g)
                    for k in range(GROUP):
                        t = nc.tensor.matmul(b_v[:, k, :], x1T[:, k, :], Wv, start=True, stop=True)
                    t.then_inc(v_done, 1)

                def project_h(g):
                    after(pe, q_copied, g)
                    bias_rows(b_h, 0)
                    after(pe, m1_copied, g + 1)
                    for k in range(GROUP):
                        t = nc.tensor.matmul(b_h[:, k, :], m1[:, k, :], Wc, start=False, stop=True, skip_group_check=True)
                    t.then_inc(h_done, 1)

                def turn_probs(g, h):
                    after(pe, probs_ready, g * HEADS + h + 1)
                    if h == 0:
                        after(pe, k_copied, up_to(g + 2))
                        after(pe, pT_copied_a, g * 2)
                    if h == 1:
                        after(pe, m1_copied, up_to(g + 3))
                        after(pe, mix_ready, g)
                    if h == 2:
                        after(pe, v_copied, up_to(g + 2))
                        after(pe, res2_ready, g)
                    if h == 3:
                        after(pe, pT_copied_v, g * 2 + 1)
                    for k in range(GROUP):
                        t = nc.tensor.transpose(b_pT[h][:, k, :], prob[:, h, k, :], c["ident"][:, :])
                    t.then_inc(p_turned, 1)

                def mask(g, h):
                    after(pe, probs_ready, (g - 1) * HEADS + h + 1)
                    nc.tensor.matmul(psum[h][:, :, :], c["identb"][:, :], over(c["head_mask"][:, :]),
                                     start=True, stop=True)

                def mix(g, b):
                    after(pe, pT_copied_a, g * 2 + 2)
                    after(pe, pT_copied_v, g * 2 + 2)
                    for k in range(GROUP):
                        for h in range(HEADS):
                            a = k * P + h * HD
                            cols = slice(a, min(a + WIDE, GROUP * P))
                            t = nc.tensor.matmul(flat(b_mix)[:, cols], probT[:, h, k, :], flat(val[:, b])[:, cols],
                                                 start=True, stop=True)
                    t.then_inc(mix_done, 1)

                def scores(g, pair):
                    after(pe, q_copied, g + 1)
                    after(pe, k_copied, g + 1)
                    for k in range(GROUP):
                        for h in (2 * pair, 2 * pair + 1):
                            rows = slice(h * HD, (h + 1) * HD)
                            t = nc.tensor.matmul(psum[h][:, k, :], qT[rows, k, :], kT[rows, k, :],
                                                 start=False, stop=True, skip_group_check=True)
                    t.then_inc(scores_done, 1)

                def turn_mixed(g):
                    after(pe, mix_ready, g + 1)
                    for k in range(GROUP):
                        t = nc.tensor.transpose(b_mixT[:, k, :], mixed[:, k, :], c["ident"][:, :])
                    t.then_inc(mix_turned, 1)

                def step(i, u):
                    if live(i - 2, NG):
                        turn_x1(i - 2)
                    if live(i, NG):
                        turn_h(i, u)
                    if live(i - 4, NG):
                        project_out(i - 4)
                    if live(i - 2, NG):
                        queries(i - 2)
                        keys(i - 2)
                    if live(i - 1, NG):
                        spread_x(i - 1, 1 - u)
                    if live(i - 2, NG):
                        values(i - 2)
                    for h in range(HEADS):
                        if h == 3 and live(i - 2, NG):
                            scores(i - 2, 0)
                        if live(i - 3, NG):
                            turn_probs(i - 3, h)
                        if live(i - 2, NG):
                            mask(i - 2, h)
                    if live(i - 1, NG):
                        project_h(i - 1)
                    if live(i - 3, NG):
                        mix(i - 3, 1 - u)
                    if live(i - 2, NG):
                        scores(i - 2, 1)
                    if live(i - 3, NG):
                        turn_mixed(i - 3)
                pe.wait_ge(Wq_scaled, 1)
                run_steps(pe, step, NG, LAG + 1, HEAD)

            @block.scalar
            def _(act):
                def copy(bank, dst, done, n, copied):
                    after(act, done, n)
                    nc.scalar.activation(dst, bank[:, :, :], ACT.Copy).then_inc(copied, 1)

                def exps(g, h):
                    after(act, top_ready, g * HEADS + h + 1)
                    after(act, p_turned, (g - 1) * HEADS + h + 1)
                    if h == 0:
                        after(act, inv_ready, g)
                    for k in range(GROUP):
                        t = nc.scalar.activation(prob[:, h, k, :], psum[h][:, k, :], ACT.Exp,
                                                 bias=top[:, h, k:k + 1], accum_out=total[:, h, k:k + 1])
                    t.then_inc(probs_ready, 1)

                def step(i, u):
                    g2, g3 = i - 2, i - 3
                    if live(g2, NG):
                        after(act, v_done, g2)
                        copy(b_x1T, x1T[:, :, :], x1_turned, g2 + 1, x1T_copied)
                    if live(g3, NG):
                        exps(g3, 2)
                    if live(g2, NG):
                        copy(b_q, qT[:, :, :], q_done, g2 + 1, q_copied)
                    if live(g3, NG):
                        exps(g3, 3)
                    if live(g2, NG):
                        copy(b_k, kT[:, :, :], k_done, g2 + 1, k_copied)
                    if live(i - 1, NG):
                        after(act, h_done, i - 1)
                        copy(b_m1, m1[:, :, :], m1_done, i, m1_copied)
                    if live(g2, NG):
                        after(act, mix_done, g2 - 1)
                        copy(b_v, val[:, u], v_done, g2 + 1, v_copied)
                    if live(g3, NG):
                        after(act, mix_done, g3)
                        copy(b_pT[2], probT[:, 2], p_turned, g3 * HEADS + 3, pT_copied_a)
                        copy(b_pT[3], probT[:, 3], p_turned, g3 * HEADS + 4, pT_copied_a)
                    if live(g2, NG):
                        exps(g2, 0)
                        exps(g2, 1)
                    if live(g3, NG):
                        after(act, o_done, g3)
                        copy(b_mixT, mixedT[:, :, :], mix_turned, g3 + 1, mixT_copied)
                run_steps(act, step, NG, LAG, HEAD)

            @block.vector
            def _(dve):
                def stats(n, tiles, g, ready):
                    tile_stats(nc, dve, tiles, norms[n][0], 0, g, ready, norm_sems[n][0])

                def moments(n, g):
                    tile_moments(nc, dve, norms[n][0], norms[n][1], 0, g, norm_sems[n][0], norm_sems[n][4],
                                 norm_sems[n][1])

                def normalise(n, dst, src, g):
                    after(dve, norm_sems[n][3], g + 1)
                    for k in range(GROUP):
                        t = nc.vector.tensor_scalar(dst[:, k, :], src[:, k, :], norms[n][1][:, 0, k, 0:1],
                                                    norms[n][3][:, k:k + 1], ALU.subtract, ALU.mult)
                    t.then_inc(norm_sems[n][4], 1)

                def row_max(g, h):
                    if h % 2 == 0:
                        after(dve, scores_done, g * 2 + h // 2 + 1)
                    nc.vector.tensor_reduce(top[:, h, :], psum[h][:, :, :], AX, ALU.max, negate=True) \
                        .then_inc(top_ready, 1)

                def residual_0(g):
                    after(dve, h_turned, g + 1)
                    after(dve, norm_sems[0][4], g)
                    nc.vector.tensor_tensor(res0[:, :, :], b_hT[:, :, :], batches(X, g), ALU.add).then_inc(res0_ready, 1)

                def residual_2(g, b):
                    after(dve, o_done, g + 1)
                    after_nop(dve, x1_stored[b], landed(g, b))
                    after(dve, scaled2, g)
                    nc.vector.tensor_tensor(res2[:, :, :], b_o[:, :, :], batches(H, g), ALU.add).then_inc(res2_ready, 1)

                def copy_probT(g, h):
                    if h == 0:
                        after(dve, mix_done, g)
                    after(dve, p_turned, g * HEADS + h + 1)
                    nc.vector.tensor_copy(probT[:, h], b_pT[h][:, :, :]).then_inc(pT_copied_v, 1)

                def invert(g):
                    after(dve, probs_ready, (g + 1) * HEADS)
                    nc.vector.reciprocal(inv[:, :, :], total[:, :, :]).then_inc(inv_ready, 1)

                def weigh_mixed(g):
                    after(dve, inv_ready, g + 1)
                    after(dve, mix_done, g + 1)
                    after(dve, mix_turned, g)
                    nc.vector.tensor_tensor(
                        mixed[:, :, :].rearrange("p k (h d) -> p k h d", h=HEADS),
                        b_mix[:, :, :].rearrange("p k (h d) -> p k h d", h=HEADS),
                        inv[:, :, :].rearrange("p h k -> p k h").unsqueeze(3).broadcast_to([P, GROUP, HEADS, HD]),
                        ALU.mult).then_inc(mix_ready, 1)

                def scale_hidden(g):
                    after(dve, x1_ready, g)
                    after(dve, norm_sems[1][1], g + 1)
                    for k in range(GROUP):
                        t = nc.vector.scalar_tensor_tensor(hidden[:, k, :], b_h[:, k, :], norms[1][1][:, 0, k, 0:1],
                                                           g1, ALU.subtract, ALU.mult)
                    t.then_inc(norm_sems[1][4], 1)

                def shift_hidden(g):
                    after(dve, norm_sems[1][4], g + 1)
                    after(dve, norm_sems[1][3], g + 1)
                    for k in range(GROUP):
                        t = nc.vector.scalar_tensor_tensor(hidden[:, k, :], hidden[:, k, :], norms[1][3][:, k:k + 1],
                                                           be1, ALU.mult, ALU.add)
                    t.then_inc(affine, 1)

                def step(i, u):
                    h, g2, g3, g4 = i - 1, i - 2, i - 3, i - 4
                    if live(g3, NG):
                        row_max(g3, 2)
                    if live(i, NG):
                        residual_0(i)
                    if live(g3, NG):
                        row_max(g3, 3)
                    if live(g4, NG):
                        residual_2(g4, u)
                    if live(i, NG):
                        stats(0, res0, i, res0_ready)
                    if live(g4, NG):
                        stats(2, res2, g4, res2_ready)
                    if live(i, NG):
                        moments(0, i)
                    if live(g4, NG):
                        moments(2, g4)
                    if live(i, NG):
                        after(dve, x1_ready, i - 1)
                        after_nop(dve, x3_stored[u], landed(i - 2, u))
                        after(dve, m1_done, i - 1)
                        normalise(0, x3[:, u], res0, i)
                    if live(g3, NG):
                        copy_probT(g3, 0)
                        copy_probT(g3, 1)
                        invert(g3)
                    if live(g4, NG):
                        normalise(2, res2, res2, g4)
                    if live(g2, NG):
                        row_max(g2, 0)
                        row_max(g2, 1)
                    if live(h, NG):
                        stats(1, b_h, h, h_done)
                        moments(1, h)
                        scale_hidden(h)
                        shift_hidden(h)
                    if live(g3, NG):
                        weigh_mixed(g3)
                    if live(h, NG):
                        after(dve, affine, i)
                        after(dve, x1_turned, h)
                        after_nop(dve, x1_stored[u], landed(i - 2, u))
                        nc.vector.scalar_tensor_tensor(flat(x1), flat(hidden), 0.0, flat(x3[:, 1 - u]), ALU.max, ALU.add) \
                            .then_inc(x1_ready, 1)
                nc.vector.tensor_scalar(Wq, Wq, float(HD) ** -0.5, None, ALU.mult).then_inc(Wq_scaled, 1)
                run_steps(dve, step, NG, LAG + 1, HEAD)

            @block.gpsimd
            def _(pool):
                def rstd(n, g):
                    st6_ready, stats_ready, var_ready, rstd_ready, normed = norm_sems[n]
                    mv, var, rs = norms[n][1:]
                    after_nop(pool, stats_ready, g + 1)
                    nc.gpsimd.tensor_scalar(var[:, :], mv[:, 0, :, 1], EPS, None, ALU.add).then_inc(var_ready, 1)
                    after_nop(pool, var_ready, g + 1)
                    nc.gpsimd.tensor_tensor(rs[:, :], var[:, :], c["half"][:, :], ALU.pow).then_inc(rstd_ready, 1)

                def step(i, u):
                    if live(i, NG):
                        rstd(0, i)
                    if live(i - 4, NG):
                        rstd(2, i - 4)
                    if live(i - 1, NG):
                        rstd(1, i - 1)
                    if live(i - 4, NG):
                        after(pool, norm_sems[2][4], i - 3)
                        after(pool, x2_stored[1 - u], landed(i - 5, 1 - u))
                        nc.gpsimd.tensor_tensor(x2[:, :, :], res2[:, :, :], over(g2), ALU.mult).then_inc(scaled2, 1)
                        after(pool, scaled2, i - 3)
                        nc.gpsimd.tensor_tensor(x2[:, :, :], x2[:, :, :], over(be2), ALU.add).then_inc(x2_ready, 1)
                run_steps(pool, step, NG, LAG + 1, HEAD)


def transformer_mlp(nc, c, X, H, psum, NG, out):
    ctx = ExitStack()
    with ctx:
        def sb(name, shape, dt=F32):
            return ctx.enter_context(nc.sbuf_tensor(f"mlp_{name}", shape, dt))

        sem = ctx.enter_context(phase_semaphores(nc, "mlp"))

        ring = [P, 2, GROUP, P]
        x2, x2T, res3, part, skip, res4, done = (sb(n, ring) for n in
                                                ("x2", "x2T", "res3", "part", "skip", "res4", "done"))
        act_h = sb("act_h", [P, 2, 2, GROUP, P])
        norms = [(sb(f"st6_{n}", [P, 2, GROUP, 6]), sb(f"mv_{n}", [P, 2, GROUP, 2]), sb(f"var_{n}", [P, 2, 2, GROUP]),
                  sb(f"rstd_{n}", [P, 2, GROUP]), sb(f"shift_{n}", [P, 2, GROUP])) for n in range(2)]
        norm_sems = [tuple(sem(f"{s}_{n}") for s in ("st6_ready", "stats_ready", "var_ready", "rstd_ready", "normed", "scale_ready"))
                     for n in range(2)]
        staged, stored = ([sem(f"{n}{b}") for b in range(2)] for n in ("staged", "stored"))
        turned, turned_copied, up_done, gelu_ready, down_done = (
            sem(n) for n in ("turned", "turned_copied", "up_done", "gelu_ready", "down_done"))
        res3_ready, scaled, skip_ready, res4_ready = (sem(n) for n in ("res3_ready", "scaled", "skip_ready", "res4_ready"))
        g3, be3 = c["rep"][:, 4, :], c["rep"][:, 5, :]
        HEAD = 8

        with nc.Block() as block:
            @block.sync
            def _(sync):
                def step(i, u):
                    if live(i, NG):
                        after_nop(sync, turned, i - 1)
                        sync.dma_start(x2[:, u], batches(H, i)).then_inc(staged[u], 16)
                    if live(i - 8, NG):
                        after_nop(sync, norm_sems[1][4], i - 7)
                        sync.dma_start(out[bass.ds((i - 8) * GROUP, GROUP), :, :].rearrange("b t c -> t b c"),
                                       done[:, u]).then_inc(stored[u], 16)
                run_steps(sync, step, NG, 8, HEAD)
                for b in range(2):
                    sync.wait_ge(stored[b], landed(NG - 2 + b, b))

            @block.tensor
            def _(pe):
                def turn(g, b):
                    after(pe, staged[b], landed(g, b))
                    after(pe, turned_copied, g)
                    for k in range(GROUP):
                        t = nc.tensor.transpose(psum[0][:, k, :], x2[:, b, k, :], c["ident"][:, :])
                    t.then_inc(turned, 1)

                def up(g, b):
                    after(pe, turned_copied, g + 1)
                    after(pe, gelu_ready, g * 2 - 2)
                    for j in range(2):
                        nc.tensor.matmul(psum[1 + 2 * b + j][:, :, :], c["W1"][:, j * P:(j + 1) * P], x2T[:, b],
                                         start=True, stop=True).then_inc(up_done, 1)

                def down(g, b):
                    after(pe, res3_ready, g - 1)
                    nc.tensor.matmul(psum[5 + b][:, :, :], c["ones3"][:, :], over(c["bias3"][:, 2, :]),
                                     start=True, stop=True)
                    after(pe, gelu_ready, g * 2 + 2)
                    for k in range(GROUP):
                        for j in range(2):
                            t = nc.tensor.matmul(psum[5 + b][:, k, :], act_h[:, b, j, k, :], c["W2"][:, j, :],
                                                 start=False, stop=(j == 1), skip_group_check=True)
                    t.then_inc(down_done, 1)

                def step(i, u):
                    if live(i, NG):
                        turn(i, u)
                    if live(i - 1, NG):
                        up(i - 1, 1 - u)
                    if live(i - 2, NG):
                        down(i - 2, u)
                run_steps(pe, step, NG, 2, HEAD)

            @block.scalar
            def _(act):
                def gelu(g, b):
                    after(act, down_done, g - 1)
                    for j in range(2):
                        after(act, up_done, g * 2 + j + 1)
                        nc.scalar.activation(act_h[:, b, j], psum[1 + 2 * b + j][:, :, :], ACT.Gelu,
                                             bias=c["cols"][:, 16 + j:17 + j]).then_inc(gelu_ready, 1)

                def normalise(n, dst, src, g, b):
                    after(act, norm_sems[n][3], g + 1)
                    for k in range(GROUP):
                        t = nc.scalar.activation(dst[:, k, :], src[:, k, :], ACT.Identity,
                                                 bias=norms[n][4][:, b, k:k + 1], scale=norms[n][3][:, b, k:k + 1])
                    t.then_inc(norm_sems[n][4], 1)

                def step(i, u):
                    if live(i, NG):
                        after(act, turned, i + 1)
                        after(act, up_done, i * 2 - 2)
                        nc.scalar.activation(x2T[:, u], psum[0][:, :, :], ACT.Copy).then_inc(turned_copied, 1)
                    if live(i - 4, NG):
                        after(act, res4_ready, i - 5)
                        normalise(0, part[:, u], res3[:, u], i - 4, u)
                    if live(i - 1, NG):
                        gelu(i - 1, 1 - u)
                    if live(i - 6, NG):
                        after_nop(act, stored[u], landed(i - 8, u))
                        normalise(1, done[:, u], res4[:, u], i - 6, u)
                run_steps(act, step, NG, 6, HEAD)

            @block.vector
            def _(dve):
                def stats(n, tiles, g, b, ready):
                    tile_stats(nc, dve, tiles, norms[n][0], b, g, ready, norm_sems[n][0])

                def moments(n, g, b):
                    tile_moments(nc, dve, norms[n][0], norms[n][1], b, g, norm_sems[n][0], norm_sems[n][2],
                                 norm_sems[n][1])

                def step(i, u):
                    w = 1 - u
                    if live(i - 5, NG):
                        after(dve, norm_sems[0][4], i - 4)
                        nc.vector.tensor_tensor(part[:, w], part[:, w], over(g3), ALU.mult).then_inc(scaled, 1)
                    if live(i - 3, NG):
                        after(dve, down_done, i - 2)
                        after(dve, norm_sems[0][4], i - 4)
                        nc.vector.tensor_tensor(res3[:, w], psum[5 + w][:, :, :], batches(H, i - 3), ALU.add) \
                            .then_inc(res3_ready, 1)
                    if live(i - 5, NG):
                        after(dve, scaled, i - 4)
                        after(dve, skip_ready, i - 4)
                        after(dve, norm_sems[1][4], i - 6)
                        nc.vector.tensor_tensor(res4[:, w], part[:, w], skip[:, w], ALU.add).then_inc(res4_ready, 1)
                    if live(i - 3, NG):
                        stats(0, res3[:, w], i - 3, w, res3_ready)
                    if live(i - 5, NG):
                        stats(1, res4[:, w], i - 5, w, res4_ready)
                    if live(i - 3, NG):
                        moments(0, i - 3, w)
                    if live(i - 5, NG):
                        moments(1, i - 5, w)
                run_steps(dve, step, NG, 5, HEAD)

            @block.gpsimd
            def _(pool):
                def rstd(n, g, b):
                    _, stats_ready, var_ready, rstd_ready, normed, scale_ready = norm_sems[n]
                    layer_rstd(nc, pool, c, *norms[n][1:], b, g, stats_ready, (normed,), var_ready, scale_ready,
                               rstd_ready)

                def step(i, u):
                    if live(i - 4, NG):
                        after(pool, res4_ready, i - 5)
                        nc.gpsimd.tensor_tensor(skip[:, u], batches(X, i - 4), over(be3), ALU.add) \
                            .then_inc(skip_ready, 1)
                    if live(i - 3, NG):
                        rstd(0, i - 3, 1 - u)
                    if live(i - 5, NG):
                        rstd(1, i - 5, 1 - u)
                run_steps(pool, step, NG, 5, HEAD)


_INS = ['x', 'adj', 'L0_gnn_Wqkv', 'L0_gnn_Wo', 'L1_gnn_W', 'L1_gnn_a', 'L2_gnn_Wg0', 'L2_gnn_bg0', 'L2_gnn_Wg1',
        'L2_gnn_bg1', 'L2_gnn_Wih', 'L2_gnn_Whh', 'L2_gnn_bih', 'L2_gnn_bhh', 'L3_gnn_Wc', 'L3_gnn_bc', 'L3_gnn_g1',
        'L3_gnn_be1', 'L3_gnn_Wq', 'L3_gnn_Wk', 'L3_gnn_Wv', 'L3_gnn_Wo', 'L3_gnn_bo', 'L3_gnn_g2', 'L3_gnn_be2',
        'L3_gnn_W1', 'L3_gnn_b1', 'L3_gnn_W2', 'L3_gnn_b2', 'L3_gnn_g3', 'L3_gnn_be3']


def kernel(**inputs):
    import numpy as _np
    import concourse.bacc as _bacc
    from concourse import mybir as _mybir
    from concourse.bass_utils import run_bass_kernel_spmd as _run

    nc = _bacc.Bacc("TRN2", target_bir_lowering=False, num_devices=1)
    arrays, args = {}, {}
    for name in _INS:
        arr = _np.ascontiguousarray(inputs[name])
        arrays[f"in_{name}_dram"] = arr
        args[name] = nc.dram_tensor(f"in_{name}_dram", arr.shape, _mybir.dt.from_np(arr.dtype),
                                    kind="ExternalInput").ap()
    out = nc.dram_tensor("out_0_dram", inputs["x"].shape, _mybir.dt.float32, kind="ExternalOutput").ap()
    program(nc, args, out)
    r = _run(nc, [arrays], core_ids=[0])
    return r.results[0]["out_0_dram"]
```
